# Optimizing a Trainium2 kernel written in Bass

```python
import numpy as np
import jax
import jax.numpy as jnp

def _softmax(x, axis=-1):
    return jax.nn.softmax(x, axis=axis)

def _gelu(x):
    return jax.nn.gelu(x, approximate=True)

def _silu(x):
    return jax.nn.silu(x)

def _sigmoid(x):
    return jax.nn.sigmoid(x)

def _layernorm(x, axis=-1, eps=1e-05):
    m = jnp.mean(x, axis=axis, keepdims=True)
    v = jnp.var(x, axis=axis, keepdims=True)
    return (x - m) / jnp.sqrt(v + eps)

def _scatter_add(tgt, idx, src, axis=0):
    return tgt.at[idx].add(src)

def _segment_sum(src, seg, n):
    return jax.ops.segment_sum(src, seg, n)
kernel_name = 'mk_gnn_ffn_d1_gnn_r32_990c88'

def setup_inputs(seed: int=0):
    np.random.seed(seed)
    _w = jnp.asarray

    def _rec_inputs():
        import jax
        import jax.numpy as jnp
        _gk = jax.random.key(seed)
        x = -0.0003713 + 1 * jax.random.normal(jax.random.fold_in(_gk, 1), (3125, 256), jnp.float32)
        src = jax.random.randint(jax.random.fold_in(_gk, 2), (50000,), 0, 3125, jnp.int32)
        dst = jax.random.randint(jax.random.fold_in(_gk, 3), (50000,), 0, 3125, jnp.int32)
        _o = jnp.argsort(dst, stable=True)
        src = src[_o]
        dst = dst[_o]
        return (x, src, dst)
    x, src, dst = _rec_inputs()

    def _L0_gnn_setup():
        import jax, jax.numpy as jnp
        import numpy as np
        N_NODES = 50000
        N_EDGES = 25000
        D_MODEL = 256
        NUM_HEADS = 8
        HEAD_DIM = D_MODEL // NUM_HEADS
        D_FF = 2 * D_MODEL
        NEG_SLOPE = 0.2
        BN_EPS = 1e-05

        def _batch_norm(h, g, b):
            mean = jnp.mean(h, axis=0)
            var = jnp.mean((h - mean) ** 2, axis=0)
            return (h - mean) * jax.lax.rsqrt(var + BN_EPS) * g + b
        key = jax.random.key(seed)
        ks = jax.random.split(key, 16)
        x = jax.random.normal(ks[0], (N_NODES, D_MODEL), dtype=jnp.float32)
        src = jax.random.randint(ks[1], (N_EDGES,), 0, N_NODES)
        off = jax.random.randint(ks[2], (N_EDGES,), 1, N_NODES)
        dst = (src + off) % N_NODES
        edge_index = jnp.stack([src, dst]).astype(jnp.int64)

        def lin(k, fi, fo):
            s = 1.0 / np.sqrt(fi)
            return jax.random.uniform(k, (fi, fo), jnp.float32, -s, s)
        inp = {'x': x, 'edge_index': edge_index, 'Wq': lin(ks[3], D_MODEL, D_MODEL), 'bq': jnp.zeros((D_MODEL,), jnp.float32), 'Wk': lin(ks[4], D_MODEL, D_MODEL), 'bk': jnp.zeros((D_MODEL,), jnp.float32), 'Wv': lin(ks[5], D_MODEL, D_MODEL), 'bv': jnp.zeros((D_MODEL,), jnp.float32), 'Wo': lin(ks[6], D_MODEL, D_MODEL), 'bo': jnp.zeros((D_MODEL,), jnp.float32), 'W1': lin(ks[7], D_MODEL, D_FF), 'b1': jnp.zeros((D_FF,), jnp.float32), 'W2': lin(ks[8], D_FF, D_MODEL), 'b2': jnp.zeros((D_MODEL,), jnp.float32), 'bn1_g': jnp.ones((D_MODEL,), jnp.float32), 'bn1_b': jnp.zeros((D_MODEL,), jnp.float32), 'bn2_g': jnp.ones((D_MODEL,), jnp.float32), 'bn2_b': jnp.zeros((D_MODEL,), jnp.float32)}
        return inp
    _L0_gnn_all = _L0_gnn_setup()
    _L0_gnn_in = {k: v for k, v in _L0_gnn_all.items() if k in ('Wq', 'bq', 'Wk', 'bk', 'Wv', 'bv', 'Wo', 'bo', 'W1', 'b1', 'W2', 'b2', 'bn1_g', 'bn1_b', 'bn2_g', 'bn2_b')}
    del _L0_gnn_all

    def _L0_ffn_setup():
        import jax, jax.numpy as jnp
        import numpy as np
        E, D, H, TOP_K = (6, 256, 256, 2)
        ROUTER_H = D // 2
        key = jax.random.key(seed)
        ks = jax.random.split(key, 12)
        s = 1.0 / np.sqrt(D)
        sh = 1.0 / np.sqrt(H)
        sr = 1.0 / np.sqrt(ROUTER_H)
        return {'features': jax.random.normal(ks[0], (8, 128, D), dtype=jnp.float32), 'router_w1': jax.random.uniform(ks[1], (D, ROUTER_H), jnp.float32, -s, s), 'router_b1': jnp.zeros((ROUTER_H,), jnp.float32), 'router_w2': jax.random.uniform(ks[2], (ROUTER_H, E), jnp.float32, -sr, sr), 'router_b2': jnp.zeros((E,), jnp.float32), 'expert_w1': jax.random.uniform(ks[3], (E, D, H), jnp.float32, -s, s), 'expert_b1': jnp.zeros((E, H), jnp.float32), 'expert_w2': jax.random.uniform(ks[4], (E, H, H), jnp.float32, -sh, sh), 'expert_b2': jnp.zeros((E, H), jnp.float32), 'expert_w3': jax.random.uniform(ks[5], (E, H, D), jnp.float32, -sh, sh), 'expert_b3': jnp.zeros((E, D), jnp.float32)}
    _L0_ffn_all = _L0_ffn_setup()
    _L0_ffn_in = {k: v for k, v in _L0_ffn_all.items() if k in ('router_w1', 'router_b1', 'router_w2', 'router_b2', 'expert_w1', 'expert_b1', 'expert_w2', 'expert_b2', 'expert_w3', 'expert_b3')}
    del _L0_ffn_all
    return {'x': x, 'src': src, 'dst': dst, 'L0_gnn_Wq': _L0_gnn_in['Wq'], 'L0_gnn_bq': _L0_gnn_in['bq'], 'L0_gnn_Wk': _L0_gnn_in['Wk'], 'L0_gnn_bk': _L0_gnn_in['bk'], 'L0_gnn_Wv': _L0_gnn_in['Wv'], 'L0_gnn_bv': _L0_gnn_in['bv'], 'L0_gnn_Wo': _L0_gnn_in['Wo'], 'L0_gnn_bo': _L0_gnn_in['bo'], 'L0_gnn_W1': _L0_gnn_in['W1'], 'L0_gnn_b1': _L0_gnn_in['b1'], 'L0_gnn_W2': _L0_gnn_in['W2'], 'L0_gnn_b2': _L0_gnn_in['b2'], 'L0_gnn_bn1_g': _L0_gnn_in['bn1_g'], 'L0_gnn_bn1_b': _L0_gnn_in['bn1_b'], 'L0_gnn_bn2_g': _L0_gnn_in['bn2_g'], 'L0_gnn_bn2_b': _L0_gnn_in['bn2_b'], 'L0_ffn_router_w1': _L0_ffn_in['router_w1'], 'L0_ffn_router_b1': _L0_ffn_in['router_b1'], 'L0_ffn_router_w2': _L0_ffn_in['router_w2'], 'L0_ffn_router_b2': _L0_ffn_in['router_b2'], 'L0_ffn_expert_w1': _L0_ffn_in['expert_w1'], 'L0_ffn_expert_b1': _L0_ffn_in['expert_b1'], 'L0_ffn_expert_w2': _L0_ffn_in['expert_w2'], 'L0_ffn_expert_b2': _L0_ffn_in['expert_b2'], 'L0_ffn_expert_w3': _L0_ffn_in['expert_w3'], 'L0_ffn_expert_b3': _L0_ffn_in['expert_b3']}

def reference(x, src, dst, L0_gnn_Wq, L0_gnn_bq, L0_gnn_Wk, L0_gnn_bk, L0_gnn_Wv, L0_gnn_bv, L0_gnn_Wo, L0_gnn_bo, L0_gnn_W1, L0_gnn_b1, L0_gnn_W2, L0_gnn_b2, L0_gnn_bn1_g, L0_gnn_bn1_b, L0_gnn_bn2_g, L0_gnn_bn2_b, L0_ffn_router_w1, L0_ffn_router_b1, L0_ffn_router_w2, L0_ffn_router_b2, L0_ffn_expert_w1, L0_ffn_expert_b1, L0_ffn_expert_w2, L0_ffn_expert_b2, L0_ffn_expert_w3, L0_ffn_expert_b3):
    import jax
    import jax.numpy as jnp

    def _L0_gnn_ref(x, edge_index, Wq, bq, Wk, bk, Wv, bv, Wo, bo, W1, b1, W2, b2, bn1_g, bn1_b, bn2_g, bn2_b):
        import jax, jax.numpy as jnp
        import numpy as np
        N_NODES = 50000
        N_EDGES = 25000
        D_MODEL = 256
        NUM_HEADS = 8
        HEAD_DIM = D_MODEL // NUM_HEADS
        D_FF = 2 * D_MODEL
        NEG_SLOPE = 0.2
        BN_EPS = 1e-05

        def _batch_norm(h, g, b):
            mean = jnp.mean(h, axis=0)
            var = jnp.mean((h - mean) ** 2, axis=0)
            return (h - mean) * jax.lax.rsqrt(var + BN_EPS) * g + b
        N = x.shape[0]
        Qh = (x @ Wq + bq).reshape(N, NUM_HEADS, HEAD_DIM)
        Kh = (x @ Wk + bk).reshape(N, NUM_HEADS, HEAD_DIM)
        Vh = (x @ Wv + bv).reshape(N, NUM_HEADS, HEAD_DIM)
        s = jnp.einsum('nhc,nhc->nh', Qh, Kh) / jnp.sqrt(jnp.float32(HEAD_DIM))
        loops = jnp.arange(N, dtype=edge_index.dtype)
        src = jnp.concatenate([edge_index[0], loops])
        dst = jnp.concatenate([edge_index[1], loops])
        alpha = jax.nn.leaky_relu(s[src] + s[dst], NEG_SLOPE)
        m = jax.ops.segment_max(alpha, dst, num_segments=N)
        e = jnp.exp(alpha - m[dst])
        denom = jax.ops.segment_sum(e, dst, num_segments=N)
        a = e / denom[dst]
        msg = Vh[src] * a[:, :, None]
        attn = jax.ops.segment_sum(msg, dst, num_segments=N).reshape(N, D_MODEL)
        h = attn @ Wo + bo
        h = x + h
        h = _batch_norm(h, bn1_g, bn1_b)
        h2 = jax.nn.relu(h @ W1 + b1) @ W2 + b2
        h = _batch_norm(h + h2, bn2_g, bn2_b)
        return h

    def _L0_ffn_ref(features, router_w1, router_b1, router_w2, router_b2, expert_w1, expert_b1, expert_w2, expert_b2, expert_w3, expert_b3):
        import jax, jax.numpy as jnp
        import numpy as np
        E, D, H, TOP_K = (6, 256, 256, 2)
        ROUTER_H = D // 2
        rh = jax.nn.relu(features @ router_w1 + router_b1)
        expert_logits = jax.nn.softmax(rh @ router_w2 + router_b2, axis=-1)
        top_w, top_i = jax.lax.top_k(expert_logits, TOP_K)
        routing_weights = jax.nn.softmax(top_w, axis=-1)
        h1 = jax.nn.relu(jnp.einsum('bsd,edh->bseh', features, expert_w1) + expert_b1)
        h2 = jax.nn.relu(jnp.einsum('bseh,ehf->bsef', h1, expert_w2) + expert_b2)
        expert_out = jnp.einsum('bsef,efo->bseo', h2, expert_w3) + expert_b3
        sel = jnp.take_along_axis(expert_out, top_i[:, :, :, None], axis=2)
        combined = jnp.sum(sel * routing_weights[..., None], axis=2)
        return combined
    edge_index = jnp.stack([src, dst])
    x = x + _L0_gnn_ref(_layernorm(x, axis=-1), edge_index, L0_gnn_Wq, L0_gnn_bq, L0_gnn_Wk, L0_gnn_bk, L0_gnn_Wv, L0_gnn_bv, L0_gnn_Wo, L0_gnn_bo, L0_gnn_W1, L0_gnn_b1, L0_gnn_W2, L0_gnn_b2, L0_gnn_bn1_g, L0_gnn_bn1_b, L0_gnn_bn2_g, L0_gnn_bn2_b)
    x = x + _L0_ffn_ref(_layernorm(x, axis=-1)[None], L0_ffn_router_w1, L0_ffn_router_b1, L0_ffn_router_w2, L0_ffn_router_b2, L0_ffn_expert_w1, L0_ffn_expert_b1, L0_ffn_expert_w2, L0_ffn_expert_b2, L0_ffn_expert_w3, L0_ffn_expert_b3)[0]
    return x

_drawn_inputs = setup_inputs


def setup_inputs(seed=0):
    import zlib

    import numpy as np

    out = dict(_drawn_inputs(seed))
    spreads = {'L0_gnn_bq': (0.0, 0.8),
     'L0_gnn_bk': (0.0, 0.8),
     'L0_gnn_bv': (0.0, 0.8),
     'L0_gnn_bo': (0.0, 0.8),
     'L0_gnn_b1': (0.0, 0.496),
     'L0_gnn_b2': (0.0, 0.8),
     'L0_gnn_bn1_g': (1.0, 0.2),
     'L0_gnn_bn1_b': (0.0, 0.792),
     'L0_gnn_bn2_g': (1.0, 0.2),
     'L0_gnn_bn2_b': (0.0, 0.1),
     'L0_ffn_router_b1': (0.0, 0.424),
     'L0_ffn_router_b2': (0.0, 0.283),
     'L0_ffn_expert_b1': (0.0, 0.8),
     'L0_ffn_expert_b2': (0.0, 0.575),
     'L0_ffn_expert_b3': (0.0, 0.1)}
    factors = {'L0_gnn_Wq': 4.904, 'L0_gnn_Wk': 4.946}
    for name, (base, spread) in spreads.items():
        noise = np.random.default_rng([zlib.crc32(name.encode()), seed]).standard_normal(out[name].shape)
        drawn = base * np.exp(spread * noise) if base else spread * noise
        out[name] = jnp.asarray(drawn.astype(out[name].dtype))
    for name, factor in factors.items():
        out[name] = (out[name] * factor).astype(out[name].dtype)
    return out
```

```python
from contextlib import ExitStack

import concourse.bass as bass
from concourse import mybir

F32 = mybir.dt.float32
BF16 = mybir.dt.bfloat16
I32 = mybir.dt.int32
ALU = mybir.AluOpType
ACT = mybir.ActivationFunctionType
X = mybir.AxisListType.X

P = 128
N = 3125
D = 256
DC = D // P
HEADS = 8
HD = D // HEADS
E = 50000
NT = -(-N // P)
NTAIL = N - (NT - 1) * P
ET = -(-E // P)
ETAIL = E - (ET - 1) * P
SB = 16
BATCHES = -(-(ET + NT - 1) // SB)
STEPS = BATCHES * SB
TC = 98
TCH = -(-ET // TC)
CP = STEPS // 4
CCH = STEPS // CP
ROW = D + HEADS
AGG = ROW + 2 * HEADS
HOME = ROW + HEADS
G = 4
NG = SB // G
BIG = 1e30
FAR = 65536.0
EPS = 1e-5
NEG_SLOPE = 0.2
NC = 448
NCH = -(-N // NC)
NCT = N - (NCH - 1) * NC
FF = 512
FC = FF // P
NEXP = 6
RH = 128


def bcast(ap, shape):
    return ap.to_broadcast(shape)


def in_pairs(eng, n, body, peel=1):
    for j in range(min(2 * peel, n)):
        body(j, j % 2)
    if n // 2 > peel:
        with eng.Fori(peel, n // 2) as i:
            body(i * 2, 0)
            body(i * 2 + 1, 1)
    if n % 2 and n > 2 * peel:
        body(n - 1, 0)


class Alloc:

    def __init__(self, nc, ctx, phase):
        self.nc, self.ctx, self.phase = nc, ctx, phase

    def sb(self, name, shape, dt=F32):
        return self.ctx.enter_context(self.nc.sbuf_tensor(f"{self.phase}_{name}", shape, dt))

    def ps(self, name, shape, dt=F32):
        return self.ctx.enter_context(self.nc.psum_tensor(f"{self.phase}_{name}", shape, dt))

    def sem(self, name):
        return self.ctx.enter_context(self.nc.semaphore(f"{self.phase}_{name}"))


def apart(eng, passed):
    eng.sem_inc(passed, 1)


class Chain:

    def __init__(self, eng, sem):
        self.eng, self.sem, self.n = eng, sem, 0

    def link(self, ins):
        self.mark(ins)
        self.join()

    def mark(self, ins):
        ins.then_inc(self.sem, 1)
        self.n = self.n + 1

    def join(self):
        self.eng.wait_ge(self.sem, self.n)


def project_nodes(nc, a, io, keep):
    xnT, sTab, ident = keep["xnT"], keep["sTab"], keep["ident"]
    xN = a.sb("x_rows", [P, NT, D])
    wqkv = a.sb("wqkv", [P, DC, 3 * D])
    bias = a.sb("qkv_bias", [P, 3 * D])
    stats = a.sb("stats", [P, NT, 6])
    meanvar = a.sb("meanvar", [P, NT, 2])
    rstd = a.sb("rstd", [P, NT])
    rstd_in = a.sb("rstd_in", [P, NT])
    xn = a.sb("xn", [P, 2, D])
    xnT_ring = a.sb("xnT_ring", [P, 2, D])
    qkv = a.sb("qkv", [P, 2, 3 * D + HEADS])
    qk = a.sb("qk", [P, 2, D])
    psT = [a.ps(f"psT{i}", [P, 512]) for i in range(2)]
    psQKV = [a.ps(f"psQKV{i}", [P, 1024]) for i in range(2)]

    x_pad = a.sem("x_pad")
    x_in = [a.sem(f"x_in{i}") for i in range(5)]
    w_in = a.sem("w_in")
    id0 = a.sem("id0")
    id_ready = a.sem("id_ready")
    chain = a.sem("dve_chain")
    var_ready = a.sem("var_ready")
    std_ready = a.sem("std_ready")
    xn_ready = a.sem("xn_ready")
    xnT_done = a.sem("xnT_transposed")
    xnT_ready = a.sem("xnT_ready")
    xnT_kept = a.sem("xnT_kept")
    go = a.sem("pool_passed")
    qkv_done = a.sem("qkv_product")
    row_ready = a.sem("row_ready")
    row_out = [a.sem(f"row_out{i}") for i in range(2)]

    block = a.ctx.enter_context(nc.Block())

    @block.sync
    def _(sp):
        xv = io["x"][0:(NT - 1) * P, :].rearrange("(j p) d -> p j d", p=P)
        for g in range(5):
            last = min(5 * g + 5, NT - 1)
            sp.dma_start(xN[:, 5 * g:last, :], xv[:, 5 * g:last, :]).then_inc(x_in[g], 16)
        sp.wait_ge(x_pad, 1)
        sp.dma_start(xN[0:NTAIL, NT - 1, :], io["x"][(NT - 1) * P:N, :]).then_inc(x_in[4], 16)

        def store_row(j, k):
            sp.wait_ge(row_ready, j + 1)
            sp.dma_start(io["table"][bass.ds(j * P, P), :], qkv[:, k, 2 * D:]).then_inc(row_out[k], 16)

        in_pairs(sp, NT, store_row)
        sp.wait_ge(row_out[0], 16 * ((NT + 1) // 2))
        sp.wait_ge(row_out[1], 16 * (NT // 2))

    @block.gpsimd
    def _(pool):
        nc.gpsimd.memset(ident[:], 0.0).then_inc(id0, 1)
        pool.wait_ge(id0, 1)
        nc.gpsimd.affine_select(out=ident[:], in_=ident[:], compare_op=ALU.not_equal, fill=1.0, base=0,
                                pattern=[[-1, P]], channel_multiplier=1).then_inc(id_ready, 1)

        def keep_xnT(j, k):
            pool.wait_ge(xnT_ready, j + 1)
            apart(pool, go)
            nc.gpsimd.tensor_copy(xnT[:, :, bass.ds(j * P, P)],
                                  xnT_ring[:, k, :].rearrange("p (c n) -> p c n", c=DC)).then_inc(xnT_kept, 1)

        in_pairs(pool, NT, keep_xnT)

    @block.scalar
    def _(act):
        for n, w in enumerate(("Wq", "Wk", "Wv")):
            act.dma_start(wqkv[:, :, n * D:(n + 1) * D], io[w].rearrange("(c p) n -> p c n", p=P)).then_inc(w_in, 16)
        for n, b in enumerate(("bq", "bk", "bv")):
            act.dma_start(bias[:, n * D:(n + 1) * D], io[b].partition_broadcast(P)).then_inc(w_in, 16)
        act.wait_ge(var_ready, 1)
        nc.scalar.activation(rstd_in[:], rstd[:], ACT.Sqrt).then_inc(std_ready, 1)

        def evacuate(j, k):
            act.wait_ge(xnT_done, j + 1)
            if not isinstance(j, int) or j >= 2:
                act.wait_ge(xnT_kept, j - 1)
                act.wait_ge(qkv_done, j - 1)
            nc.scalar.copy(xnT_ring[:, k, :], psT[k][:, 0:D]).then_inc(xnT_ready, 1)

        in_pairs(act, NT, evacuate)

    @block.vector
    def _(dve):
        c = Chain(dve, chain)
        nc.vector.memset(xN[:, NT - 1, :], 0.0).then_inc(x_pad, 1)
        c.mark(nc.vector.memset(sTab[:, NT, :], 0.0))
        for g in range(5):
            dve.wait_ge(x_in[g], 16 if g < 4 else 32)
            for j in range(5 * g, 5 * g + 5):
                c.mark(nc.vector.bn_stats(stats[:, j, :], xN[:, j, :]))
        c.join()
        for j in range(NT):
            c.mark(nc.vector.bn_aggr(meanvar[:, j, :], stats[:, j, :]))
        c.join()
        nc.vector.tensor_scalar(rstd[:], meanvar[:, :, 1], EPS, None, ALU.add).then_inc(var_ready, 1)
        dve.wait_ge(std_ready, 1)
        c.link(nc.vector.reciprocal(rstd[:], rstd_in[:]))
        dve.wait_ge(w_in, 96)
        base = c.n

        def normalize(j, k):
            if not isinstance(j, int) or j >= 2:
                dve.wait_ge(xnT_done, j - 1)
            nc.vector.tensor_scalar(xn[:, k, :], xN[:, bass.ds(j, 1), :].rearrange("p a d -> p (a d)"), meanvar[:, bass.ds(j, 1), 0],
                                    rstd[:, bass.ds(j, 1)], ALU.subtract, ALU.mult).then_inc(xn_ready, 1)

        def heads(j, k):
            c.n = base + 4 * j
            dve.wait_ge(qkv_done, j + 1)
            if not isinstance(j, int) or j >= 2:
                dve.wait_ge(row_out[k], (j - k) * 8)
            c.link(nc.vector.tensor_tensor(qkv[:, k, 0:3 * D], psQKV[k][:, 0:3 * D], bias[:], ALU.add))
            c.link(nc.vector.tensor_tensor(qk[:, k, :], qkv[:, k, 0:D], qkv[:, k, D:2 * D], ALU.mult))
            s = qkv[:, k, 3 * D:]
            c.link(nc.vector.tensor_reduce(s, qk[:, k, :].rearrange("p (h c) -> p h c", h=HEADS), X, ALU.add))
            c.link(nc.vector.tensor_scalar(s, s, float(HD) ** -0.5, None, ALU.mult))
            nc.vector.tensor_tensor(sTab[:, bass.ds(j, 1), :].rearrange("p a h -> p (a h)"), s, s, ALU.max).then_inc(row_ready, 1)

        normalize(0, 0)
        def step(j, k):
            if not isinstance(j, int) or j + 1 < NT:
                normalize(j + 1, 1 - k)
            heads(j, k)
        in_pairs(dve, NT, step)

    @block.tensor
    def _(pe):
        pe.wait_ge(id_ready, 1)
        pe.wait_ge(w_in, 96)

        def transpose(j, k):
            pe.wait_ge(xn_ready, j + 1)
            if not isinstance(j, int) or j >= 2:
                pe.wait_ge(xnT_ready, j - 1)
            for c in range(DC):
                last = nc.tensor.transpose(psT[k][:, c * P:(c + 1) * P], xn[:, k, c * P:(c + 1) * P], ident[:])
            last.then_inc(xnT_done, 1)

        def product(j, k):
            pe.wait_ge(xnT_ready, j + 1)
            if not isinstance(j, int) or j >= 2:
                pe.wait_ge(row_ready, j - 1)
            for lo, hi in ((0, 512), (512, 768)):
                for c in range(DC):
                    last = nc.tensor.matmul(psQKV[k][:, lo:hi], xnT_ring[:, k, c * P:(c + 1) * P],
                                            wqkv[:, c, lo:hi], start=(c == 0), stop=(c == DC - 1))
            last.then_inc(qkv_done, 1)

        transpose(0, 0)
        def step(j, k):
            if not isinstance(j, int) or j + 1 < NT:
                transpose(j + 1, 1 - k)
            product(j, k)
        in_pairs(pe, NT, step)


def plan_steps(nc, a, io, keep, plan):
    ident = keep["ident"]
    srcI = a.sb("srcI", [TC, TCH, P], I32)
    dstI = a.sb("dstI", [TC, TCH, P], I32)
    srcF = a.sb("srcF", [TC, TCH, P])
    dstF = a.sb("dstF", [TC, TCH, P + 1])
    prevI = a.sb("prevI", [TC, TCH], I32)
    prevF = a.sb("prevF", [TC, TCH])
    prevB = a.sb("prevB", [TC, TCH, P])
    firstB = a.sb("firstB", [TC, TCH, P])
    tileI = a.sb("tileI", [TC, TCH], I32)
    tileF = a.sb("tileF", [TC, TCH])
    firstKey = a.sb("firstKey", [TC, TCH])
    stepI = a.sb("stepI", [P, STEPS], I32)
    stepF = a.sb("stepF", [P, STEPS])
    bound = a.sb("bound", [P, STEPS])
    started = a.sb("started", [TC, TCH, STEPS])
    ones = a.sb("ones", [TC, P])
    tp = a.sb("tile_of_step", [P, STEPS])
    wp = a.sb("window_of_step", [P, STEPS])
    wp128 = a.sb("window_start", [P, STEPS])
    sel = a.sb("sel", [TC, TCH, STEPS])
    dst = a.sb("dst_of_step", [P, STEPS])
    dstB = a.sb("dst_over_heads", [P, 2, SB, HEADS])
    dstTs = a.sb("dst_T", [P, 2, P])
    prev = a.sb("prev_of_step", [P, STEPS])
    rel = a.sb("rel", [P, STEPS])
    t1 = a.sb("t1", [P, STEPS])
    t2 = a.sb("t2", [P, STEPS])
    iotaI = a.sb("iotaI", [P, P], I32)
    eyeT = a.sb("eyeT", [P, SB, SB])
    psCount = a.ps("psCount", [P, 512])
    psSel = [a.ps(f"psSel{i}", [P, 512]) for i in range(5)]
    psDT = [a.ps(f"psDT{i}", [P, 512]) for i in range(2)]

    pads = a.sem("pads")
    idx_in = a.sem("idx_in")
    iotas = a.sem("iotas")
    chain = a.sem("chain")
    key_ready = a.sem("key_ready")
    counted = a.sem("counted")
    sel_ready = a.sem("sel_ready")
    selected = a.sem("selected")
    dst_ready = a.sem("dst_ready")
    dstB_ready = a.sem("dstB_ready")
    dT_done = a.sem("dT_done")
    dT_copied = a.sem("dT_copied")
    edge_ready = a.sem("edge_ready")

    block = a.ctx.enter_context(nc.Block())
    LASTP = ET - 1 - (TCH - 1) * TC

    @block.sync
    def _(sp):
        sp.wait_ge(pads, 3)
        for name, t in (("src", srcI), ("dst", dstI)):
            full = (TCH - 1) * TC * P
            sp.dma_start(t[:, 0:TCH - 1, :], io[name][0:full].rearrange("(c t e) -> t c e", c=TCH - 1, e=P)).then_inc(idx_in, 16)
            sp.dma_start(t[0:LASTP, TCH - 1, :], io[name][full:full + LASTP * P].rearrange("(t e) -> t e", e=P)).then_inc(idx_in, 16)
            sp.dma_start(t[LASTP:LASTP + 1, TCH - 1, 0:ETAIL], io[name][full + LASTP * P:E].rearrange("(t e) -> t e", t=1)).then_inc(idx_in, 16)
        ends = io["dst"][0:(ET - 1) * P].rearrange("(t e) -> t e", e=P)[:, P - 1:P]
        with nc.allow_non_contiguous_dma(reason="one element of each tile"):
            for c in range(TCH):
                lo, hi = max(1, c * TC), min(ET, (c + 1) * TC)
                sp.dma_start(prevI[lo - c * TC:hi - c * TC, c:c + 1], ends[lo - 1:hi - 1, :]).then_inc(idx_in, 16)

    @block.gpsimd
    def _(pool):
        nc.gpsimd.iota(tileI[:], pattern=[[TC, TCH]], base=0, channel_multiplier=1).then_inc(iotas, 1)
        nc.gpsimd.iota(stepI[:], pattern=[[1, STEPS]], base=0, channel_multiplier=0).then_inc(iotas, 1)
        nc.gpsimd.iota(iotaI[:], pattern=[[1, P]], base=0, channel_multiplier=0).then_inc(iotas, 1)
        nc.gpsimd.memset(eyeT[:], 0.0).then_inc(iotas, 1)
        pool.wait_ge(iotas, 4)
        nc.gpsimd.affine_select(out=eyeT[:], in_=eyeT[:], compare_op=ALU.not_equal, fill=1.0, base=0,
                                pattern=[[1, SB], [-1, SB]], channel_multiplier=0).then_inc(iotas, 1)

    def copy_back(act, b):
        act.wait_ge(dT_done, b + 1)
        if b >= 2:
            act.wait_ge(edge_ready, b - 1)
        nc.scalar.copy(dstTs[:, b % 2, :], psDT[b % 2][:, 0:P]).then_inc(dT_copied, 1)

    @block.scalar
    def _(act):
        act.wait_ge(dst_ready, 1)
        for b in range(BATCHES):
            k = b % 2
            if b >= 2:
                act.wait_ge(dT_done, b - 1)
            nc.scalar.copy(dstB[:, k, :, :], bcast(dst[:, b * SB:(b + 1) * SB].unsqueeze(2), [P, SB, HEADS])).then_inc(dstB_ready, 1)
            if b:
                copy_back(act, b - 1)
        copy_back(act, BATCHES - 1)

    @block.vector
    def _(dve):
        c = Chain(dve, chain)
        nc.vector.memset(srcI[:], 0).then_inc(pads, 1)
        nc.vector.memset(dstI[:], int(FAR)).then_inc(pads, 1)
        nc.vector.memset(prevI[:], -1).then_inc(pads, 1)
        c.mark(nc.vector.memset(ones[:], 1.0))
        c.mark(nc.vector.memset(dstF[:, :, P:P + 1], -5.0))
        c.mark(nc.vector.memset(plan["edge"][:, :, 0:1], -BIG))
        c.mark(nc.vector.memset(plan["edgeBack"][:, :, 0:1], -BIG))
        dve.wait_ge(iotas, 5)
        c.mark(nc.vector.tensor_copy(tileF[:], tileI[:]))
        c.mark(nc.vector.tensor_copy(stepF[:], stepI[:]))
        c.mark(nc.vector.tensor_copy(plan["iota"][:], iotaI[:]))
        c.mark(nc.vector.tensor_copy(plan["iota16"][:], iotaI[:]))
        c.join()
        c.mark(nc.vector.tensor_scalar(bound[:], stepF[:], float(P), float(P), ALU.mult, ALU.add))
        dve.wait_ge(idx_in, 160)
        c.mark(nc.vector.tensor_copy(srcF[:], srcI[:]))
        c.mark(nc.vector.tensor_copy(prevF[:], prevI[:]))
        c.link(nc.vector.tensor_copy(dstF[:, :, 0:P], dstI[:]))
        c.mark(nc.vector.tensor_copy(prevB[:], bcast(prevF[:].unsqueeze(2), [TC, TCH, P])))
        c.mark(nc.vector.tensor_copy(firstB[:], bcast(dstF[:, :, 0:1], [TC, TCH, P])))
        c.link(nc.vector.scalar_tensor_tensor(firstKey[:], tileF[:], float(P), dstF[:, :, 0], ALU.mult, ALU.add))
        for k in range(TCH):
            nc.vector.tensor_scalar(started[:, k, :], bound[0:TC, :], firstKey[:, k:k + 1], None, ALU.is_gt).then_inc(key_ready, 1)
        dve.wait_ge(counted, 1)
        c.link(nc.vector.tensor_scalar(tp[:], psCount[:, 0:STEPS], -1.0, 0.0, ALU.add, ALU.max))
        for k in range(TCH):
            c.mark(nc.vector.tensor_scalar(sel[:, k, :], tp[0:TC, :], tileF[:, k:k + 1], None, ALU.is_equal))
        c.join()
        nc.vector.tensor_tensor(wp[:], stepF[:], tp[:], ALU.subtract).then_inc(sel_ready, 1)
        dve.wait_ge(sel_ready, 1)
        c.mark(nc.vector.tensor_copy(plan["windowI"][:], wp[0:1, :]))
        c.mark(nc.vector.tensor_scalar(wp128[:], wp[:], float(P), None, ALU.mult))
        dve.wait_ge(selected, 5)
        c.link(nc.vector.tensor_copy(dst[:], psSel[1][:, 0:STEPS]))
        c.mark(nc.vector.tensor_copy(plan["srcI"][:], psSel[0][:, 0:STEPS]))
        nc.vector.tensor_copy(prev[:], psSel[3][:, 0:STEPS]).then_inc(dst_ready, 1)
        dve.wait_ge(dst_ready, 1)
        c.mark(nc.vector.tensor_tensor(plan["isLast"][:], dst[:], psSel[2][:, 0:STEPS], ALU.not_equal))
        c.link(nc.vector.tensor_tensor(rel[:], dst[:], wp128[:], ALU.subtract))
        c.mark(nc.vector.tensor_copy(plan["rel16"][:], rel[:]))
        c.link(nc.vector.tensor_tensor(t1[:], dst[:], prev[:], ALU.is_equal))
        c.mark(nc.vector.scalar_tensor_tensor(plan["relHome"][:], t1[:], -1e6, rel[:], ALU.mult, ALU.add))
        c.link(nc.vector.scalar_tensor_tensor(t2[:], rel[:], 0.0, t1[:], ALU.is_ge, ALU.mult))
        c.link(nc.vector.scalar_tensor_tensor(plan["isCarry"][:], rel[:], float(P), t2[:], ALU.is_lt, ALU.mult))
        c.link(nc.vector.tensor_tensor(t1[:], prev[:], psSel[4][:, 0:STEPS], ALU.is_equal))
        c.link(nc.vector.tensor_tensor(rel[:], prev[:], wp128[:], ALU.subtract))
        c.link(nc.vector.scalar_tensor_tensor(t2[:], rel[:], 0.0, t1[:], ALU.is_ge, ALU.mult))
        c.link(nc.vector.scalar_tensor_tensor(t1[:], rel[:], float(P), t2[:], ALU.is_lt, ALU.mult))
        c.link(nc.vector.scalar_tensor_tensor(t2[:], prev[:], 1.0, t1[:], ALU.add, ALU.mult))
        c.mark(nc.vector.tensor_scalar(plan["target"][:], t2[:], -1.0, None, ALU.add))
        c.join()
        c.mark(nc.vector.tensor_copy(plan["eye"][:], eyeT[:]))
        for b in range(BATCHES):
            k = b % 2
            dve.wait_ge(dT_copied, b + 1)
            c.link(nc.vector.tensor_tensor(t1[:, 0:P - 1], dstTs[:, k, 1:P], dstTs[:, k, 0:P - 1], ALU.not_equal))
            c.mark(nc.vector.tensor_scalar(plan["edgeBack"][:, b, P - 1:0:-1], t1[:, 0:P - 1], -BIG, None, ALU.mult))
            nc.vector.tensor_scalar(plan["edge"][:, b, 1:P], t1[:, 0:P - 1], -BIG, None, ALU.mult).then_inc(edge_ready, 1)
            dve.wait_ge(edge_ready, b + 1)

    @block.tensor
    def _(pe):
        pe.wait_ge(key_ready, TCH)
        for k in range(TCH):
            last = nc.tensor.matmul(psCount[:, 0:STEPS], ones[:], started[:, k, :], start=(k == 0), stop=(k == TCH - 1))
        last.then_inc(counted, 1)
        pe.wait_ge(sel_ready, 1)
        for n, rows in enumerate((srcF[:], dstF[:, :, 0:P], dstF[:, :, 1:P + 1], prevB[:], firstB[:])):
            for k in range(TCH):
                last = nc.tensor.matmul(psSel[n][:, 0:STEPS], rows[:, k, :], sel[:, k, :], start=(k == 0), stop=(k == TCH - 1))
            last.then_inc(selected, 1)
        for b in range(BATCHES):
            pe.wait_ge(dstB_ready, b + 1)
            if b >= 2:
                pe.wait_ge(dT_copied, b - 1)
            nc.tensor.transpose(psDT[b % 2][:, 0:P], dstB[:, b % 2, :, :].rearrange("p s h -> p (s h)"), ident[:]).then_inc(dT_done, 1)


def load_dense_weights(nc, sp, sem, io, wts):
    for name, key in (("Wo", "wo"), ("W1", "w1"), ("W2", "w2"), ("router_w1", "rw1")):
        sp.dma_start(wts[key][:], io[name].rearrange("(c p) n -> p c n", p=P)).then_inc(sem, 16)
    sp.dma_start(wts["rw2"][:], io["router_w2"]).then_inc(sem, 16)
    sp.dma_start(wts["rb2"][:], io["router_b2"].partition_broadcast(P)).then_inc(sem, 16)
    sp.dma_start(wts["eb3"][:], io["expert_b3"]).then_inc(sem, 16)
    with nc.allow_non_contiguous_dma(reason="columns of biases"):
        for name, key in (("bo", "bo"), ("b1", "b1"), ("b2", "b2"), ("bn1_g", "g1"), ("bn1_b", "c1"), ("bn2_g", "g2"), ("bn2_b", "c2")):
            sp.dma_start(wts[key][:], io[name].rearrange("(c p) -> p c", p=P)).then_inc(sem, 16)
        sp.dma_start(wts["rb1"][:], io["router_b1"].rearrange("(p c) -> p c", c=1)).then_inc(sem, 16)
        for name, key in (("expert_b1", "eb1"), ("expert_b2", "eb2")):
            for e in range(NEXP):
                sp.dma_start(wts[key][:, e, :], io[name][e, :].rearrange("(c p) -> p c", p=P)).then_inc(sem, 16)


def run_steps(nc, a, io, keep, plan, home, wts):
    ident, sTab = keep["ident"], keep["sTab"]
    rows = [a.sb(f"rows{i}", [P, SB, AGG]) for i in range(2)]
    srcS = a.sb("src_slots", [P, 2, SB], I32)
    hot16 = a.sb("hot16", [P, 2, G, P], BF16)
    hotT = a.sb("hotT", [P, 2, G, P])
    hotHome = a.sb("hotHome", [P, 2, G, P])
    carryEye = a.sb("carryEye", [P, 2, SB, SB])
    ss = a.sb("ss", [P, SB, HEADS])
    ssT = a.sb("ssT", [P, P])
    sd = a.sb("sd", [P, SB, HEADS])
    fwd = a.sb("fwd", [P, P])
    bwd = a.sb("bwd", [P, P])
    runT = a.sb("runT", [P, P])
    al = a.sb("al", [P, SB, HEADS])
    am = a.sb("am", [P, SB, HEADS])
    at = a.sb("at", [P, SB, HEADS])
    ar = a.sb("ar", [P, SB, HEADS])
    carrySb = a.sb("carrySb", [SB, 2, AGG])
    ident16 = a.sb("ident16", [P, P], BF16)

    psHot = [a.ps(f"psHot{i}", [P, G, P], BF16) for i in range(2)]
    psS = a.ps("psS", [P, 512])
    psM = a.ps("psM", [P, SB, HEADS])
    psD = a.ps("psD", [P, SB, HEADS])
    psHome = [a.ps(f"psHome{i}", [P, 512]) for i in range(2)]
    psCarry = a.ps("psCarry", [P, 512])

    gathered = [[a.sem(f"gathered{i}_{g}") for g in range(NG)] for i in range(2)]
    weights_in = a.sem("weights_in")
    slots_ready = a.sem("slots_ready")
    go = a.sem("pool_passed")
    start = a.sem("start")
    hot_ready = a.sem("hot_ready")
    hotT_done = a.sem("hotT_done")
    hotT_ready = a.sem("hotT_ready")
    sd_done = a.sem("sd_done")
    sd_ready = a.sem("sd_ready")
    ss_ready = a.sem("ss_ready")
    ssT_done = a.sem("ssT_done")
    ssT_ready = a.sem("ssT_ready")
    runT_ready = a.sem("runT_ready")
    run_done = a.sem("run_done")
    arg_ready = a.sem("arg_ready")
    exp_ready = a.sem("exp_ready")
    eye_ready = a.sem("eye_ready")
    msg_ready = a.sem("msg_ready")
    home_done = a.sem("home_done")
    agg_done = a.sem("agg_done")
    home_added = a.sem("home_added")
    carry_copied = a.sem("carry_copied")
    carry_out = [a.sem(f"carry_out{i}") for i in range(2)]
    chain = a.sem("dve_chain")

    block = a.ctx.enter_context(nc.Block())

    def past(b, first=1):
        return not isinstance(b, int) or b >= first

    @block.gpsimd
    def _(pool):
        def batch(b, k):
            if past(b, 2):
                pool.wait_ge(agg_done, b * SB - 2 * SB + SB)
                apart(pool, go)
            nc.gpsimd.tensor_copy(srcS[:, k, :], plan["srcI"][:, bass.ds(b * SB, SB)]).then_inc(slots_ready, 1)
            pool.wait_ge(slots_ready, b + 1)
            apart(pool, go)
            for s in range(SB):
                pool.indirect_dma_start(rows[k][:, s, 0:ROW], None, io["table"],
                                        bass.IndirectOffsetOnAxis(srcS[:, k, s:s + 1], 0)).then_inc(gathered[k][s // G], 16)
        in_pairs(pool, BATCHES, batch)

    @block.sync
    def _(sp):
        load_dense_weights(nc, sp, weights_in, io, wts)

        def store_carry(b, k):
            sp.wait_ge(carry_copied, b + 1)
            sp.dma_start(io["carries"][bass.ds(b * SB, SB), :], carrySb[:, k, :]).then_inc(carry_out[k], 16)
        in_pairs(sp, BATCHES, store_carry)
        for k in range(2):
            sp.wait_ge(carry_out[k], 16 * (BATCHES // 2))
        sp.wait_ge(weights_in, 16 * (15 + 2 * NEXP))

    @block.scalar
    def _(act):
        def batch(b, k):
            for g in range(NG):
                act.wait_ge(hotT_done, b * NG + g + 1)
                if past(b) or g >= 2:
                    act.wait_ge(sd_done, b * NG + g - 1)
                nc.scalar.copy(hotT[:, g % 2, :, :], psHot[g % 2][:]).then_inc(hotT_ready, 1)
            act.wait_ge(sd_done, b * NG + NG)
            if past(b):
                act.wait_ge(exp_ready, b)
            nc.scalar.copy(sd[:], psD[:]).then_inc(sd_ready, 1)
            for g in range(NG):
                act.wait_ge(gathered[k][g], (b - k) // 2 * 16 * G + 16 * G if isinstance(b, int) else (b - k) * (8 * G) + 16 * G)
            nc.scalar.copy(ss[:], rows[k][:, :, D:ROW]).then_inc(ss_ready, 1)
            act.wait_ge(ssT_done, b + 1)
            nc.scalar.copy(ssT[:], psS[:, 0:P]).then_inc(ssT_ready, 1)
            act.wait_ge(arg_ready, b + 1)
            nc.scalar.activation(rows[k][:, :, D:ROW], ar[:], ACT.Exp).then_inc(exp_ready, 1)
            act.wait_ge(agg_done, b * SB + SB)
            if past(b, 2):
                act.wait_ge(carry_out[k], (b - k) * 8)
            nc.scalar.copy(carrySb[:, k, :], psCarry[0:SB, 0:AGG]).then_inc(carry_copied, 1)
        in_pairs(act, BATCHES, batch)

    LINKS = 8

    @block.vector
    def _(dve):
        c = Chain(dve, chain)
        nc.vector.tensor_copy(ident16[:], ident[:]).then_inc(start, 1)
        c.link(nc.vector.memset(home[:], 0.0))
        base = c.n

        def add_home(b, s):
            n = b * SB + s
            w = dve.value_load(plan["windowI"][0:1, bass.ds(n, 1)], min_val=0, max_val=NT)
            dve.wait_ge(home_done, n + 1)
            if past(b) or s:
                dve.wait_ge(home_added, n)
            h = home[:, bass.ds(w, 1), :].rearrange("p a d -> p (a d)")
            nc.vector.tensor_tensor(h, h, psHome[s % 2][:, 0:HOME], ALU.add).then_inc(home_added, 1)

        def batch(b, k):
            c.n = base + b * LINKS
            for g in range(NG):
                if past(b) or g >= 2:
                    dve.wait_ge(hotT_done, b * NG + g - 1)
                nc.vector.tensor_tensor(hot16[:, g % 2, :, :], bcast(plan["iota16"][:].unsqueeze(1), [P, G, P]),
                                        bcast(plan["rel16"][:, bass.ds(b * SB + g * G, G)].unsqueeze(2), [P, G, P]),
                                        ALU.is_equal).then_inc(hot_ready, 1)
            nc.vector.tensor_tensor(carryEye[:, k, :, :], plan["eye"][:],
                                    bcast(plan["isCarry"][:, bass.ds(b * SB, SB)].unsqueeze(2), [P, SB, SB]),
                                    ALU.mult).then_inc(eye_ready, 1)
            dve.wait_ge(ssT_ready, b + 1)
            edge = plan["edge"][:, bass.ds(b, 1), :].rearrange("p a e -> p (a e)")
            back = plan["edgeBack"][:, bass.ds(b, 1), :].rearrange("p a e -> p (a e)")
            c.mark(nc.vector.tensor_tensor_scan(fwd[:], edge, ssT[:], -BIG, ALU.add, ALU.max))
            c.link(nc.vector.tensor_tensor_scan(bwd[:, ::-1], back, ssT[:, ::-1], -BIG, ALU.add, ALU.max))
            if past(b):
                dve.wait_ge(run_done, b)
            nc.vector.tensor_tensor(runT[:], fwd[:], bwd[:], ALU.max).then_inc(runT_ready, 1)
            dve.wait_ge(sd_ready, b + 1)
            dve.wait_ge(ss_ready, b + 1)
            c.link(nc.vector.tensor_tensor(at[:], ss[:], sd[:], ALU.add))
            c.mark(nc.vector.scalar_tensor_tensor(al[:], at[:], NEG_SLOPE, at[:], ALU.mult, ALU.max))
            dve.wait_ge(run_done, b + 1)
            c.join()
            c.link(nc.vector.tensor_tensor(at[:], psM[:], sd[:], ALU.add))
            c.link(nc.vector.scalar_tensor_tensor(am[:], at[:], NEG_SLOPE, at[:], ALU.mult, ALU.max))
            nc.vector.tensor_tensor(ar[:], al[:], am[:], ALU.subtract).then_inc(arg_ready, 1)
            last = bcast(plan["isLast"][:, bass.ds(b * SB, SB)].unsqueeze(2), [P, SB, HEADS])
            c.mark(nc.vector.tensor_tensor(rows[k][:, :, ROW:ROW + HEADS], psM[:], last, ALU.mult))
            c.mark(nc.vector.tensor_tensor(rows[k][:, :, ROW + HEADS:], sd[:], last, ALU.mult))
            c.join()
            dve.wait_ge(exp_ready, b + 1)
            for g in range(NG):
                if past(b) or g >= 2:
                    dve.wait_ge(agg_done, b * SB + g * G - G)
                nc.vector.tensor_tensor(hotHome[:, g % 2, :, :], bcast(plan["iota"][:].unsqueeze(1), [P, G, P]),
                                        bcast(plan["relHome"][:, bass.ds(b * SB + g * G, G)].unsqueeze(2), [P, G, P]),
                                        ALU.is_equal).then_inc(msg_ready, 1)
                v = rows[k][:, g * G:g * G + G, 0:D].rearrange("p s (h c) -> p s h c", h=HEADS)
                ex = bcast(rows[k][:, g * G:g * G + G, D:ROW].unsqueeze(3), [P, G, HEADS, HD])
                nc.vector.tensor_tensor(v, v, ex, ALU.mult).then_inc(msg_ready, 1)
                if g:
                    for s in range(g * G - G, g * G):
                        add_home(b, s)
            for s in range(SB - G, SB):
                add_home(b, s)
            if isinstance(b, int):
                assert c.n == base + b * LINKS + LINKS, c.n - base - b * LINKS
        in_pairs(dve, BATCHES, batch)

    @block.tensor
    def _(pe):
        pe.wait_ge(start, 1)
        def batch(b, k):
            def look_up(g):
                pe.wait_ge(hotT_ready, b * NG + g + 1)
                if g == 0 and past(b):
                    pe.wait_ge(sd_ready, b)
                for s in range(g * G, g * G + G):
                    w = pe.value_load(plan["windowI"][0:1, bass.ds(b * SB + s, 1)], min_val=0, max_val=NT)
                    last = nc.tensor.matmul(psD[:, s, :], hotT[:, g % 2, s % G, :],
                                            sTab[:, bass.ds(w, 1), :].rearrange("p a h -> p (a h)"), start=True, stop=True)
                last.then_inc(sd_done, 1)

            for g in range(NG):
                pe.wait_ge(hot_ready, b * NG + g + 1)
                if past(b) or g >= 2:
                    pe.wait_ge(hotT_ready, b * NG + g - 1)
                for s in range(G):
                    last = nc.tensor.transpose(psHot[g % 2][:, s, :], hot16[:, g % 2, s, :], ident16[:])
                last.then_inc(hotT_done, 1)
                if g:
                    look_up(g - 1)
            look_up(NG - 1)
            pe.wait_ge(ss_ready, b + 1)
            if past(b):
                pe.wait_ge(ssT_ready, b)
            nc.tensor.transpose(psS[:, 0:P], ss[:].rearrange("p s h -> p (s h)"), ident[:]).then_inc(ssT_done, 1)
            pe.wait_ge(runT_ready, b + 1)
            if past(b):
                pe.wait_ge(exp_ready, b)
            nc.tensor.transpose(psM[:].rearrange("p s h -> p (s h)"), runT[:], ident[:]).then_inc(run_done, 1)
            pe.wait_ge(eye_ready, b + 1)
            if past(b):
                pe.wait_ge(carry_copied, b)
            for s in range(SB):
                n = b * SB + s
                if s % G == 0:
                    pe.wait_ge(msg_ready, (b * NG + s // G) * 2 + 2)
                if past(b) or s >= 2:
                    pe.wait_ge(home_added, n - 1)
                nc.tensor.matmul(psHome[s % 2][:, 0:AGG], hotHome[:, s // G % 2, s % G, :], rows[k][:, s, :],
                                 start=True, stop=True).then_inc(home_done, 1)
                nc.tensor.matmul(psCarry[0:SB, 0:AGG], carryEye[:, k, s, :], rows[k][:, s, :],
                                 start=(s == 0), stop=(s == SB - 1)).then_inc(agg_done, 1)
        in_pairs(pe, BATCHES, batch)


MC = 4
W = MC * P
CHUNKS = -(-NT // MC)
LASTT = NT - (CHUNKS - 1) * MC
LASTN = N - (CHUNKS - 1) * W


def in_chunks(eng, body):
    full = CHUNKS - 1
    for m in range(2):
        body(m, m % 2, MC, W)
    with eng.Fori(1, full // 2) as i:
        body(i * 2, 0, MC, W)
        body(i * 2 + 1, 1, MC, W)
    body(full, full % 2, LASTT, LASTN)


def later(m, first):
    return not isinstance(m, int) or m >= first


def merge_attention(nc, a, io, keep, home, target, wts):
    ident, sTab, xnT = keep["ident"], keep["sTab"], keep["xnT"]
    cr = a.sb("carry_rows", [CP, CCH, AGG])
    vself = a.sb("vself", [P, NT, D])
    merged = a.sb("carry_sums", [P, NT, HOME])
    edge = a.sb("carry_edge", [HEADS, STEPS])
    back = a.sb("carry_edge_back", [HEADS, STEPS])
    mT = a.sb("carry_maxT", [HEADS, STEPS])
    fwd = a.sb("carry_fwd", [HEADS, STEPS])
    bwd = a.sb("carry_bwd", [HEADS, STEPS])
    run = a.sb("carry_run", [HEADS, STEPS])
    lastRow = a.sb("lastRow", [1, STEPS])
    one = a.sb("one", [1, 1])
    targetP = a.sb("targetP", [CP, CCH])
    lastP = a.sb("lastP", [CP, CCH])
    startI = a.sb("startI", [CP, NT], I32)
    startF = a.sb("startF", [CP, NT])
    iotaI = a.sb("iotaI", [P, P], I32)
    iota = a.sb("iotaM", [P, P])
    relC = a.sb("relC", [CP, NT, CCH])
    c1 = a.sb("c1", [CP, CCH, HEADS])
    c2 = a.sb("c2", [CP, CCH, HEADS])
    c3 = a.sb("c3", [CP, CCH, HEADS])
    c4 = a.sb("c4", [CP, CCH, HEADS])
    hotC = a.sb("hotC", [CP, 2, CCH, P])
    al = [a.sb(f"alpha{n}", [P, NT, HEADS]) for n in range(3)]
    ex = [a.sb(f"expo{n}", [P, NT, HEADS]) for n in range(3)]
    tmp = a.sb("tmp", [P, NT, HEADS])
    mx = a.sb("mx", [P, NT, HEADS])
    den = a.sb("den", [P, NT, HEADS])
    attn = a.sb("attn", [P, 2, MC, D])
    part = a.sb("part", [P, 2, MC, D])
    selfp = a.sb("selfp", [P, 2, MC, D])
    attnT = a.sb("attnT", [P, 2, DC, W])
    stats = wts["stats1"]

    psA = a.ps("psA", [P, 512])
    psB = a.ps("psB", [P, 512])
    psC = [a.ps(f"psC{i}", [P, 512]) for i in range(2)]
    psT = [a.ps(f"psAT{i}", [P, 512]) for i in range(2)]
    psO = [a.ps(f"psO{i}", [P, 512]) for i in range(2)]

    loads = a.sem("loads")
    v_in = a.sem("v_in")
    iotas = a.sem("iotas")
    chain = a.sem("chain")
    cT_done = a.sem("cT_done")
    cT_ready = a.sem("cT_ready")
    run_ready = a.sem("run_ready")
    back_done = a.sem("back_done")
    carg_ready = a.sem("carg_ready")
    cexp_ready = a.sem("cexp_ready")
    rows_ready = a.sem("rows_ready")
    hot_ready = a.sem("hot_ready")
    sum_done = a.sem("sum_done")
    sum_kept = a.sem("sum_kept")
    arg_ready = a.sem("arg_ready")
    exp_ready = a.sem("exp_ready")
    scales_ready = a.sem("scales_ready")
    self_ready = a.sem("self_ready")
    attn_ready = a.sem("attn_ready")
    aT_done = a.sem("aT_done")
    aT_ready = a.sem("aT_ready")
    proj_done = a.sem("proj_done")
    resid_done = a.sem("resid_done")
    go = a.sem("passed")
    passed = a.sem("dve_passed")

    block = a.ctx.enter_context(nc.Block())

    @block.sync
    def _(sp):
        sp.dma_start(cr[:], io["carries"].rearrange("(c p) n -> p c n", p=CP)).then_inc(loads, 16)
        sp.dma_start(vself[:], io["table"].rearrange("(j p) n -> p j n", p=P)[:, :, 0:D]).then_inc(v_in, 16)

    @block.gpsimd
    def _(pool):
        nc.gpsimd.iota(startI[:], pattern=[[P, NT]], base=0, channel_multiplier=0).then_inc(iotas, 1)
        nc.gpsimd.iota(iotaI[:], pattern=[[1, P]], base=0, channel_multiplier=0).then_inc(iotas, 1)
        pool.wait_ge(v_in, 16)
        pool.wait_ge(scales_ready, 3)

        def self_part(m, k, tiles, nodes):
            if later(m, 2):
                pool.wait_ge(attn_ready, m - 1)
            apart(pool, go)
            nc.gpsimd.tensor_tensor(selfp[:, k, 0:tiles, :].rearrange("p j (h c) -> p j h c", h=HEADS),
                                    vself[:, bass.ds(m * MC, tiles), :].rearrange("p j (h c) -> p j h c", h=HEADS),
                                    bcast(ex[2][:, bass.ds(m * MC, tiles), :].unsqueeze(3), [P, tiles, HEADS, HD]),
                                    ALU.mult).then_inc(self_ready, 1)
        in_chunks(pool, self_part)

    @block.scalar
    def _(act):
        act.wait_ge(cT_done, 1)
        nc.scalar.copy(mT[:], psA[0:HEADS, 0:STEPS]).then_inc(cT_ready, 1)
        act.wait_ge(carg_ready, 1)
        nc.scalar.activation(c3[:], c4[:], ACT.Exp).then_inc(cexp_ready, 1)

        def keep_sum(j, k):
            act.wait_ge(sum_done, j + 1)
            apart(act, go)
            nc.scalar.copy(merged[:, bass.ds(j, 1), :].rearrange("p a d -> p (a d)"), psC[k][:, 0:HOME]).then_inc(sum_kept, 1)
        in_pairs(act, NT, keep_sum)
        act.wait_ge(arg_ready, 3)
        for n in range(3):
            nc.scalar.activation(ex[n][:], al[n][:], ACT.Exp).then_inc(exp_ready, 1)

        def evacuate(m, k, tiles, nodes):
            for c in range(DC):
                act.wait_ge(aT_done, m * DC + c + 1)
                if later(m, 2) and c == 0:
                    act.wait_ge(proj_done, m * DC - DC)
                nc.scalar.copy(attnT[:, k, c, 0:tiles * P], psT[c][:, 0:tiles * P]).then_inc(aT_ready, 1)
        in_chunks(act, evacuate)

    @block.tensor
    def _(pe):
        pe.wait_ge(loads, 16)
        for c in range(CCH):
            last = nc.tensor.transpose(psA[0:HEADS, c * CP:(c + 1) * CP], cr[:, c, ROW:ROW + HEADS], ident[0:CP, 0:CP])
        last.then_inc(cT_done, 1)
        pe.wait_ge(run_ready, 1)
        for c in range(CCH):
            nc.tensor.transpose(psB[0:CP, c * HEADS:(c + 1) * HEADS], run[:, c * CP:(c + 1) * CP], ident[0:HEADS, 0:HEADS])
        for c in range(CCH):
            nc.tensor.matmul(psB[0:CP, 64 + c:65 + c], target[0:1, c * CP:(c + 1) * CP], one[:], start=True, stop=True)
            last = nc.tensor.matmul(psB[0:CP, 80 + c:81 + c], lastRow[:, c * CP:(c + 1) * CP], one[:], start=True, stop=True)
        last.then_inc(back_done, 1)
        pe.wait_ge(rows_ready, 2)

        def sum_carries(j, k):
            pe.wait_ge(hot_ready, j + 1)
            if not isinstance(j, int) or j >= 2:
                pe.wait_ge(sum_kept, j - 1)
            for c in range(CCH):
                last = nc.tensor.matmul(psC[k][:, 0:HOME], hotC[:, k, c, :], cr[:, c, 0:HOME], start=(c == 0), stop=(c == CCH - 1))
            last.then_inc(sum_done, 1)
        in_pairs(pe, NT, sum_carries)

        def project(m, k, tiles, nodes):
            pe.wait_ge(attn_ready, m + 1)
            for c in range(DC):
                if later(m, 1):
                    pe.wait_ge(aT_ready, m * DC + c + 1 - DC)
                for j in range(tiles):
                    last = nc.tensor.transpose(psT[c][:, j * P:(j + 1) * P], attn[:, k, j, c * P:(c + 1) * P], ident[:])
                last.then_inc(aT_done, 1)
            pe.wait_ge(aT_ready, m * DC + DC)
            for o in range(DC):
                if later(m, 1):
                    pe.wait_ge(resid_done, m * DC + o + 1 - DC)
                for c in range(DC):
                    last = nc.tensor.matmul(psO[o][:, 0:tiles * P], wts["wo"][:, c, o * P:(o + 1) * P],
                                            attnT[:, k, c, 0:tiles * P], start=(c == 0), stop=(c == DC - 1))
                last.then_inc(proj_done, 1)
        in_chunks(pe, project)

    @block.vector
    def _(dve):
        c = Chain(dve, chain)
        c.mark(nc.vector.memset(one[:], 1.0))
        c.mark(nc.vector.memset(edge[:, 0:1], -BIG))
        c.mark(nc.vector.memset(back[:, 0:1], -BIG))
        c.mark(nc.vector.memset(lastRow[:, STEPS - 1:STEPS], 1.0))
        c.mark(nc.vector.tensor_tensor(lastRow[:, 0:STEPS - 1], target[0:1, 1:STEPS], target[0:1, 0:STEPS - 1], ALU.not_equal))
        c.link(nc.vector.tensor_tensor(fwd[:, 1:STEPS], target[0:HEADS, 1:STEPS], target[0:HEADS, 0:STEPS - 1], ALU.not_equal))
        c.mark(nc.vector.tensor_scalar(edge[:, 1:STEPS], fwd[:, 1:STEPS], -BIG, None, ALU.mult))
        c.link(nc.vector.tensor_scalar(back[:, STEPS - 1:0:-1], fwd[:, 1:STEPS], -BIG, None, ALU.mult))
        dve.wait_ge(iotas, 2)
        c.mark(nc.vector.tensor_copy(startF[:], startI[:]))
        c.mark(nc.vector.tensor_copy(iota[:], iotaI[:]))
        dve.wait_ge(cT_ready, 1)
        c.mark(nc.vector.tensor_tensor_scan(fwd[:], edge[:], mT[:], -BIG, ALU.add, ALU.max))
        c.link(nc.vector.tensor_tensor_scan(bwd[:, ::-1], back[:], mT[:, ::-1], -BIG, ALU.add, ALU.max))
        nc.vector.tensor_tensor(run[:], fwd[:], bwd[:], ALU.max).then_inc(run_ready, 1)
        dve.wait_ge(back_done, 1)
        dve.wait_ge(loads, 16)
        c.mark(nc.vector.tensor_copy(targetP[:], psB[0:CP, 64:64 + CCH]))
        c.link(nc.vector.tensor_copy(lastP[:], psB[0:CP, 80:80 + CCH]))
        c.mark(nc.vector.tensor_tensor(relC[:], bcast(targetP[:].unsqueeze(1), [CP, NT, CCH]),
                                       bcast(startF[:].unsqueeze(2), [CP, NT, CCH]), ALU.subtract))
        crun = psB[0:CP, 0:CCH * HEADS].rearrange("p (c h) -> p c h", h=HEADS)
        cmax, csd = cr[:, :, ROW:ROW + HEADS], cr[:, :, ROW + HEADS:AGG]
        c.mark(nc.vector.tensor_tensor(c1[:], cmax, csd, ALU.add))
        c.link(nc.vector.tensor_tensor(c2[:], crun, csd, ALU.add))
        c.mark(nc.vector.scalar_tensor_tensor(c3[:], c1[:], NEG_SLOPE, c1[:], ALU.mult, ALU.max))
        c.link(nc.vector.scalar_tensor_tensor(c4[:], c2[:], NEG_SLOPE, c2[:], ALU.mult, ALU.max))
        c.link(nc.vector.tensor_tensor(cmax, crun, bcast(lastP[:].unsqueeze(2), [CP, CCH, HEADS]), ALU.mult))
        nc.vector.tensor_tensor(c4[:], c3[:], c4[:], ALU.subtract).then_inc(carg_ready, 1)
        dve.wait_ge(cexp_ready, 1)
        v = cr[:, :, 0:D].rearrange("p s (h c) -> p s h c", h=HEADS)
        nc.vector.tensor_tensor(v, v, bcast(c3[:].unsqueeze(3), [CP, CCH, HEADS, HD]), ALU.mult).then_inc(rows_ready, 1)
        nc.vector.tensor_tensor(cr[:, :, D:ROW], cr[:, :, D:ROW], c3[:], ALU.mult).then_inc(rows_ready, 1)

        def one_hot(j, k):
            if not isinstance(j, int) or j >= 2:
                dve.wait_ge(sum_done, j - 1)
            nc.vector.tensor_tensor(hotC[:, k, :, :], bcast(iota[0:CP, :].unsqueeze(1), [CP, CCH, P]),
                                    bcast(relC[:, bass.ds(j, 1), :].rearrange("p a c -> p (a c)").unsqueeze(2), [CP, CCH, P]),
                                    ALU.is_equal).then_inc(hot_ready, 1)
        in_pairs(dve, NT, one_hot)

        sd = sTab[:, 0:NT, :]
        dve.wait_ge(sum_kept, NT)
        for n, t in enumerate((home[:, 0:NT, :], merged[:])):
            c.link(nc.vector.tensor_scalar(tmp[:], t[:, :, D:ROW], 0.5, -BIG, ALU.is_lt, ALU.mult))
            c.link(nc.vector.tensor_tensor(tmp[:], tmp[:], t[:, :, ROW:HOME], ALU.add))
            c.link(nc.vector.tensor_tensor(tmp[:], tmp[:], sd, ALU.add))
            c.link(nc.vector.scalar_tensor_tensor(al[n][:], tmp[:], NEG_SLOPE, tmp[:], ALU.mult, ALU.max))
        c.link(nc.vector.tensor_scalar(tmp[:], sd, 2.0, None, ALU.mult))
        c.link(nc.vector.scalar_tensor_tensor(al[2][:], tmp[:], NEG_SLOPE, tmp[:], ALU.mult, ALU.max))
        c.link(nc.vector.tensor_tensor(mx[:], al[0][:], al[1][:], ALU.max))
        c.link(nc.vector.tensor_tensor(mx[:], mx[:], al[2][:], ALU.max))
        for n in range(3):
            nc.vector.tensor_tensor(al[n][:], al[n][:], mx[:], ALU.subtract).then_inc(arg_ready, 1)
        dve.wait_ge(exp_ready, 3)
        c.mark(nc.vector.tensor_tensor(den[:], home[:, 0:NT, D:ROW], ex[0][:], ALU.mult))
        c.link(nc.vector.tensor_tensor(mx[:], merged[:, :, D:ROW], ex[1][:], ALU.mult))
        c.link(nc.vector.tensor_tensor(den[:], den[:], mx[:], ALU.add))
        c.link(nc.vector.tensor_tensor(den[:], den[:], ex[2][:], ALU.add))
        c.link(nc.vector.reciprocal(mx[:], den[:]))
        for n in range(3):
            nc.vector.tensor_tensor(ex[n][:], ex[n][:], mx[:], ALU.mult).then_inc(scales_ready, 1)
        dve.wait_ge(scales_ready, 3)
        base = c.n
        LINKS = 3 + DC

        def combine(m, k, tiles, nodes):
            c.n = base + m * LINKS
            t = bass.ds(m * MC, tiles)
            heads = lambda v: v.rearrange("p j (h c) -> p j h c", h=HEADS)
            out, other = attn[:, k, 0:tiles, :], part[:, k, 0:tiles, :]
            if later(m, 2):
                dve.wait_ge(aT_done, m * DC - DC)
            c.mark(nc.vector.tensor_tensor(heads(out), heads(home[:, t, 0:D]), bcast(ex[0][:, t, :].unsqueeze(3), [P, tiles, HEADS, HD]), ALU.mult))
            c.link(nc.vector.tensor_tensor(heads(other), heads(merged[:, t, 0:D]), bcast(ex[1][:, t, :].unsqueeze(3), [P, tiles, HEADS, HD]), ALU.mult))
            c.link(nc.vector.tensor_tensor(out, out, other, ALU.add))
            dve.wait_ge(self_ready, m + 1)
            nc.vector.tensor_tensor(out, out, selfp[:, k, 0:tiles, :], ALU.add).then_inc(attn_ready, 1)

        def residual(m, k, tiles, nodes):
            c.n = base + m * LINKS + 3
            for o in range(DC):
                dve.wait_ge(proj_done, m * DC + o + 1)
                h = xnT[:, o, bass.ds(m * W, tiles * P)]
                nc.vector.scalar_tensor_tensor(h, psO[o][:, 0:tiles * P], wts["bo"][:, o:o + 1], h, ALU.add, ALU.add).then_inc(resid_done, 1)
                dve.wait_ge(resid_done, m * DC + o + 1)
                apart(dve, passed)
                c.link(nc.vector.bn_stats(stats[:, o, bass.ds(m, 1), :].rearrange("p a s -> p (a s)"), xnT[:, o, bass.ds(m * W, nodes)]))

        def both(m, k, tiles, nodes):
            combine(m, k, tiles, nodes)
            residual(m, k, tiles, nodes)
        in_chunks(dve, both)


def batch_norm_scale(nc, c, dve, act_sems, stats, norm, gain, shift):
    var_ready, std_ready = act_sems
    for o in range(DC):
        c.mark(nc.vector.bn_aggr(norm["mv"][:, o, :], stats[:, o, :, :]))
    c.join()
    nc.vector.tensor_scalar(norm["var"][:], norm["mv"][:, :, 1], EPS, None, ALU.add).then_inc(var_ready, 1)
    dve.wait_ge(std_ready, 1)
    c.link(nc.vector.reciprocal(norm["var"][:], norm["std"][:]))
    c.link(nc.vector.tensor_tensor(norm["scale"][:], norm["var"][:], gain, ALU.mult))
    c.link(nc.vector.tensor_tensor(norm["var"][:], norm["mv"][:, :, 0], norm["scale"][:], ALU.mult))
    c.link(nc.vector.tensor_tensor(norm["shift"][:], shift, norm["var"][:], ALU.subtract))


def feed_forward(nc, a, io, keep, wts):
    xnT = keep["xnT"]
    hidden = a.sb("hidden", [P, 2, FC, W])
    norm = {n: a.sb(f"norm_{n}", [P, DC]) for n in ("var", "std", "scale", "shift")}
    norm["mv"] = a.sb("norm_mv", [P, DC, 2])
    scratch = a.sb("scratch", [P, 1])
    psF = [a.ps(f"psF{i}", [P, 512]) for i in range(4)]
    psY = [a.ps(f"psY{i}", [P, 512]) for i in range(4)]
    chain = a.sem("chain")
    var_ready = a.sem("var_ready")
    std_ready = a.sem("std_ready")
    h_ready = a.sem("h_ready")
    ff_done = a.sem("ff_done")
    relu_done = a.sem("relu_done")
    y_done = a.sem("y_done")
    y_added = a.sem("y_added")
    passed = a.sem("passed")
    loads = a.sem("expert_loads")
    tail_zero = a.sem("tail_zero")
    block = a.ctx.enter_context(nc.Block())

    @block.sync
    def _(sp):
        sp.dma_start(wts["xN"][:, 0:NT - 1, :], io["x"][0:(NT - 1) * P, :].rearrange("(j p) d -> p j d", p=P)).then_inc(loads, 16)
        for name, key in (("expert_w1", "ew1"), ("expert_w2", "ew2"), ("expert_w3", "ew3")):
            sp.dma_start(wts[key][:], io[name].rearrange("e (c p) n -> p e c n", p=P)).then_inc(loads, 16)
        sp.wait_ge(tail_zero, 1)
        sp.dma_start(wts["xN"][0:NTAIL, NT - 1, :], io["x"][(NT - 1) * P:N, :]).then_inc(loads, 16)
        sp.wait_ge(loads, 80)

    @block.gpsimd
    def _(pool):
        nc.gpsimd.memset(wts["xN"][:, NT - 1, :], 0.0).then_inc(tail_zero, 1)

    @block.scalar
    def _(act):
        act.wait_ge(var_ready, 1)
        nc.scalar.activation(norm["std"][:], norm["var"][:], ACT.Sqrt).then_inc(std_ready, 1)

        def relu(m, k, tiles, nodes):
            for f in range(FC):
                act.wait_ge(ff_done, m * FC + f + 1)
                if later(m, 2) and f == 0:
                    act.wait_ge(y_done, m * DC - DC)
                nc.scalar.activation(hidden[:, k, f, 0:nodes], psF[f][:, 0:nodes], ACT.Relu,
                                     bias=wts["b1"][:, f:f + 1]).then_inc(relu_done, 1)
        in_chunks(act, relu)

    @block.tensor
    def _(pe):
        def up(m, k, tiles, nodes):
            pe.wait_ge(h_ready, m + 1)
            for f in range(FC):
                if later(m, 1):
                    pe.wait_ge(relu_done, m * FC + f + 1 - FC)
                for c in range(DC):
                    last = nc.tensor.matmul(psF[f][:, 0:nodes], wts["w1"][:, c, f * P:(f + 1) * P],
                                            xnT[:, c, bass.ds(m * W, nodes)], start=(c == 0), stop=(c == DC - 1))
                last.then_inc(ff_done, 1)

        def down(m, k, tiles, nodes):
            for o in range(DC):
                if later(m, 2):
                    pe.wait_ge(y_added, m * DC + o + 1 - 2 * DC)
                for f in range(FC):
                    if o == 0:
                        pe.wait_ge(relu_done, m * FC + f + 1)
                    last = nc.tensor.matmul(psY[2 * k + o][:, 0:nodes], wts["w2"][:, f, o * P:(o + 1) * P],
                                            hidden[:, k, f, 0:nodes], start=(f == 0), stop=(f == FC - 1))
                last.then_inc(y_done, 1)

        def chunk(m, k, tiles, nodes):
            up(m, k, tiles, nodes)
            down(m, k, tiles, nodes)
        in_chunks(pe, chunk)

    @block.vector
    def _(dve):
        c = Chain(dve, chain)
        batch_norm_scale(nc, c, dve, (var_ready, std_ready), wts["stats1"], norm, wts["g1"][:], wts["c1"][:])
        base = c.n

        def normalize(m, k, tiles, nodes):
            for o in range(DC):
                h = xnT[:, o, bass.ds(m * W, nodes)]
                last = nc.vector.tensor_scalar(h, h, norm["scale"][:, o:o + 1], norm["shift"][:, o:o + 1], ALU.mult, ALU.add)
            last.then_inc(h_ready, 1)
        in_chunks(dve, normalize)

        def add(m, k, tiles, nodes):
            for o in range(DC):
                dve.wait_ge(y_done, m * DC + o + 1)
                h = xnT[:, o, bass.ds(m * W, nodes)]
                nc.vector.scalar_tensor_tensor(h, psY[2 * k + o][:, 0:nodes], wts["b2"][:, o:o + 1], h, ALU.add, ALU.add).then_inc(y_added, 1)
                dve.wait_ge(y_added, m * DC + o + 1)
                apart(dve, passed)
                last = nc.vector.bn_stats(wts["stats2"][:, o, bass.ds(m, 1), :].rearrange("p a s -> p (a s)"), h)
        in_chunks(dve, add)


def route_and_mix(nc, a, io, keep, wts):
    xN, xnT, ident = wts["xN"], keep["xnT"], keep["ident"]
    norm = {n: a.sb(f"norm2_{n}", [P, DC]) for n in ("var", "std", "scale", "shift")}
    norm["mv"] = a.sb("norm2_mv", [P, DC, 2])
    y = a.sb("y", [P, 2, DC, W])
    st = a.sb("ln_stats", [P, 2, MC, 6])
    mv = a.sb("ln_mv", [P, 2, MC, 2])
    va = a.sb("ln_var", [P, 2, MC])
    sdv = a.sb("ln_std", [P, 2, MC])
    rs = a.sb("ln_rstd", [P, 2, MC])
    x2 = a.sb("x2", [P, 2, MC, D])
    x2T = a.sb("x2T", [P, 2, DC, W])
    rh = a.sb("rh", [P, 2, W])
    lg = a.sb("lg", [P, MC, 8])
    le = a.sb("le", [P, MC, 8])
    pr = a.sb("pr", [P, MC, 8])
    red = a.sb("red", [P, MC])
    top = a.sb("top", [P, MC, 8])
    topi = a.sb("topi", [P, MC, 8], mybir.dt.uint32)
    topf = a.sb("topf", [P, MC, 8])
    dw = a.sb("dw", [P, MC])
    ew = a.sb("ew", [P, MC])
    w0 = a.sb("w0", [P, MC])
    w1 = a.sb("w1_", [P, MC])
    hit = a.sb("hit", [P, MC, NEXP])
    gate = a.sb("gate", [P, 2, MC, NEXP])
    gateT = a.sb("gateT", [NEXP, 2, W])
    iotaI = a.sb("iotaE", [P, NEXP], I32)
    iotaF = a.sb("iotaEf", [P, NEXP])
    h1 = a.sb("h1", [P, 2, DC, W])
    h2 = a.sb("h2", [P, 2, DC, W])

    psT = [a.ps(f"psX{i}", [P, 512]) for i in range(2)]
    psR = a.ps("psR", [P, 512])
    psL = a.ps("psL", [P, 512])
    psH = [a.ps(f"psH{i}", [P, 512]) for i in range(2)]
    psE = [a.ps(f"psE{i}", [P, 512]) for i in range(2)]

    chain = a.sem("chain")
    var_ready = a.sem("var_ready")
    std_ready = a.sem("std_ready")
    iotas = a.sem("iotas")
    y_ready = a.sem("y_ready")
    yT_done = a.sem("yT_done")
    yT_added = a.sem("yT_added")
    lnvar_ready = a.sem("lnvar_ready")
    lnstd_ready = a.sem("lnstd_ready")
    x2_ready = a.sem("x2_ready")
    x2T_done = a.sem("x2T_done")
    x2T_ready = a.sem("x2T_ready")
    r_done = a.sem("router_done")
    r_relu = a.sem("router_relu")
    l_done = a.sem("logits_done")
    larg_ready = a.sem("larg_ready")
    lexp_ready = a.sem("lexp_ready")
    warg_ready = a.sem("warg_ready")
    wexp_ready = a.sem("wexp_ready")
    gate_ready = a.sem("gate_ready")
    gT_done = a.sem("gT_done")
    gT_ready = a.sem("gT_ready")
    hid_done = a.sem("hid_done")
    hid_relu = a.sem("hid_relu")
    e_done = a.sem("e_done")
    e_added = a.sem("e_added")
    out_done = a.sem("out_done")
    passed = a.sem("passed")
    block = a.ctx.enter_context(nc.Block())
    HALVES = MC // 2
    STORES = NEXP + 1

    def halves(tiles):
        return -(-tiles // 2)

    @block.sync
    def _(sp):
        def store(m, k, tiles, nodes):
            if tiles == MC:
                sp.wait_ge(e_added, (m + 1) * STORES * HALVES)
                sp.dma_start(io["out"][bass.ds(m * W, W), :].rearrange("(j p) d -> p j d", p=P), xN[:, bass.ds(m * MC, MC), :]).then_inc(out_done, 16)
            else:
                sp.wait_ge(e_added, (CHUNKS - 1) * STORES * HALVES + STORES * halves(tiles))
                sp.dma_start(io["out"][m * W:N, :], xN[0:nodes, m * MC, :]).then_inc(out_done, 16)
        in_chunks(sp, store)
        sp.wait_ge(out_done, 16 * CHUNKS)

    @block.gpsimd
    def _(pool):
        nc.gpsimd.iota(iotaI[:], pattern=[[1, NEXP]], base=0, channel_multiplier=0).then_inc(iotas, 1)

    @block.scalar
    def _(act):
        act.wait_ge(var_ready, 1)
        nc.scalar.activation(norm["std"][:], norm["var"][:], ACT.Sqrt).then_inc(std_ready, 1)

        def chunk(m, k, tiles, nodes):
            n = tiles * P
            act.wait_ge(lnvar_ready, m + 1)
            nc.scalar.activation(sdv[:, k, 0:tiles], va[:, k, 0:tiles], ACT.Sqrt).then_inc(lnstd_ready, 1)
            for c in range(DC):
                act.wait_ge(x2T_done, m * DC + c + 1)
                if later(m, 2) and c == 0:
                    act.wait_ge(hid_done, (m - 1) * (NEXP * 2 * DC))
                nc.scalar.copy(x2T[:, k, c, 0:n], psT[c][:, 0:n]).then_inc(x2T_ready, 1)
            act.wait_ge(r_done, m + 1)
            nc.scalar.activation(rh[:, k, 0:n], psR[:, 0:n], ACT.Relu, bias=wts["rb1"][:, 0:1]).then_inc(r_relu, 1)
            act.wait_ge(larg_ready, m + 1)
            nc.scalar.activation(le[:, 0:tiles, 0:NEXP], lg[:, 0:tiles, 0:NEXP], ACT.Exp).then_inc(lexp_ready, 1)
            act.wait_ge(warg_ready, m + 1)
            nc.scalar.activation(ew[:, 0:tiles], dw[:, 0:tiles], ACT.Exp).then_inc(wexp_ready, 1)
            act.wait_ge(gT_done, m + 1)
            nc.scalar.copy(gateT[:, k, 0:n], psR[0:NEXP, 0:n]).then_inc(gT_ready, 1)
            for e in range(NEXP):
                for layer, (h, b) in enumerate(((h1, "eb1"), (h2, "eb2"))):
                    for o in range(DC):
                        act.wait_ge(hid_done, ((m * NEXP + e) * 2 + layer) * DC + o + 1)
                        if layer == 1 and o == 0 and (later(m, 1) or e >= 2):
                            act.wait_ge(e_done, m * STORES * HALVES + (e - 2 + 1 + 1) * halves(tiles) if e >= 2 else m * STORES * HALVES - (2 - e - 1) * HALVES)
                        nc.scalar.activation(h[:, e % 2, o, 0:n], psH[o][:, 0:n], ACT.Relu,
                                             bias=wts[b][:, e, o:o + 1]).then_inc(hid_relu, 1)
        in_chunks(act, chunk)

    @block.tensor
    def _(pe):
        def chunk(m, k, tiles, nodes):
            n = tiles * P
            pe.wait_ge(y_ready, m + 1)
            for b in range(halves(tiles)):
                if later(m, 1):
                    pe.wait_ge(x2T_ready, m * DC)
                for j in range(2 * b, min(2 * b + 2, tiles)):
                    for c in range(DC):
                        last = nc.tensor.transpose(psT[b][:, (j % 2) * D + c * P:(j % 2) * D + (c + 1) * P], y[:, k, c, j * P:(j + 1) * P], ident[:])
            last.then_inc(yT_done, 1)
            pe.wait_ge(x2_ready, m + 1)
            for c in range(DC):
                for j in range(tiles):
                    last = nc.tensor.transpose(psT[c][:, j * P:(j + 1) * P], x2[:, k, j, c * P:(c + 1) * P], ident[:])
                last.then_inc(x2T_done, 1)
            pe.wait_ge(x2T_ready, m * DC + DC)
            if later(m, 1):
                pe.wait_ge(gT_ready, m)
            for c in range(DC):
                last = nc.tensor.matmul(psR[:, 0:n], wts["rw1"][:, c, :], x2T[:, k, c, 0:n], start=(c == 0), stop=(c == DC - 1))
            last.then_inc(r_done, 1)
            pe.wait_ge(r_relu, m + 1)
            if later(m, 1):
                pe.wait_ge(larg_ready, m)
            for j in range(tiles):
                last = nc.tensor.matmul(psL[:, j * 8:j * 8 + NEXP], rh[:, k, j * P:(j + 1) * P], wts["rw2"][:], start=True, stop=True)
            last.then_inc(l_done, 1)
            pe.wait_ge(gate_ready, m + 1)
            for j in range(tiles):
                last = nc.tensor.transpose(psR[0:NEXP, j * P:(j + 1) * P], gate[:, k, j, :], ident[:])
            last.then_inc(gT_done, 1)
            pe.wait_ge(gT_ready, m + 1)

            def node_rows(group, lhs, rhs_list, extra_wait):
                for b in range(halves(tiles)):
                    prior = m * STORES * HALVES + group * halves(tiles) + b
                    if later(m, 1) or group * halves(tiles) + b >= 2:
                        pe.wait_ge(e_added, prior - 1 if halves(tiles) == HALVES else prior)
                    for j in range(2 * b, min(2 * b + 2, tiles)):
                        for i, r in enumerate(rhs_list):
                            last = nc.tensor.matmul(psE[b][:, (j % 2) * D:(j % 2 + 1) * D], lhs(i, j), r, start=(i == 0), stop=(i == len(rhs_list) - 1))
                    last.then_inc(e_done, 1)

            node_rows(0, lambda i, j: gateT[:, k, j * P:(j + 1) * P], [wts["eb3"][:]], None)
            for e in range(NEXP):
                for layer, (src, w) in enumerate(((x2T[:, k], "ew1"), (h1[:, e % 2], "ew2"))):
                    for o in range(DC):
                        idx = ((m * NEXP + e) * 2 + layer) * DC + o
                        if later(m, 1) or idx >= DC:
                            pe.wait_ge(hid_relu, idx + 1 - DC if not (layer == 1 and o == 0) else idx)
                        for c in range(DC):
                            last = nc.tensor.matmul(psH[o][:, 0:n], wts[w][:, e, c, o * P:(o + 1) * P], src[:, c, 0:n], start=(c == 0), stop=(c == DC - 1))
                        last.then_inc(hid_done, 1)
                pe.wait_ge(hid_relu, ((m * NEXP + e) * 2 + 2) * DC)
                node_rows(1 + e, lambda i, j: h2[:, e % 2, i, j * P:(j + 1) * P], [wts["ew3"][:, e, c, :] for c in range(DC)], None)
        in_chunks(pe, chunk)

    @block.vector
    def _(dve):
        c = Chain(dve, chain)
        batch_norm_scale(nc, c, dve, (var_ready, std_ready), wts["stats2"], norm, wts["g2"][:], wts["c2"][:])
        c.mark(nc.vector.memset(pr[:], -1.0))
        dve.wait_ge(iotas, 1)
        c.link(nc.vector.tensor_copy(iotaF[:], iotaI[:]))
        base = c.n

        def chunk(m, k, tiles, nodes):
            LINKS = CHUNK_LINKS
            c.n = base + m * LINKS
            n = tiles * P
            if later(m, 2):
                dve.wait_ge(yT_done, m - 1)
            for o in range(DC):
                last = nc.vector.tensor_scalar(y[:, k, o, 0:n], xnT[:, o, bass.ds(m * W, n)], norm["scale"][:, o:o + 1], norm["shift"][:, o:o + 1], ALU.mult, ALU.add)
            last.then_inc(y_ready, 1)
            dve.wait_ge(yT_done, m + 1)
            for b in range(halves(tiles)):
                w = min(2, tiles - 2 * b)
                x = xN[:, bass.ds(m * MC + 2 * b, w), :].rearrange("p j d -> p (j d)")
                c.mark(nc.vector.tensor_tensor(x, x, psT[b][:, 0:w * D], ALU.add))
            c.join()
            apart(dve, passed)
            for j in range(tiles):
                c.mark(nc.vector.bn_stats(st[:, k, j, :], xN[:, bass.ds(m * MC + j, 1), :].rearrange("p a d -> p (a d)")))
            c.join()
            apart(dve, passed)
            for j in range(tiles):
                c.mark(nc.vector.bn_aggr(mv[:, k, j, :], st[:, k, j, :]))
            c.join()
            nc.vector.tensor_scalar(va[:, k, 0:tiles], mv[:, k, 0:tiles, 1], EPS, None, ALU.add).then_inc(lnvar_ready, 1)
            dve.wait_ge(lnstd_ready, m + 1)
            c.link(nc.vector.reciprocal(rs[:, k, 0:tiles], sdv[:, k, 0:tiles]))
            for j in range(tiles):
                last = nc.vector.tensor_scalar(x2[:, k, j, :], xN[:, bass.ds(m * MC + j, 1), :].rearrange("p a d -> p (a d)"), mv[:, k, j, 0:1],
                                               rs[:, k, j:j + 1], ALU.subtract, ALU.mult)
            last.then_inc(x2_ready, 1)
            dve.wait_ge(l_done, m + 1)
            L = lg[:, 0:tiles, 0:NEXP]
            r3 = bcast(red[:, 0:tiles].unsqueeze(2), [P, tiles, NEXP])
            c.link(nc.vector.tensor_tensor(L, psL[:, 0:tiles * 8].rearrange("p (j e) -> p j e", e=8)[:, :, 0:NEXP], bcast(wts["rb2"][:].unsqueeze(1), [P, tiles, NEXP]), ALU.add))
            c.link(nc.vector.tensor_reduce(red[:, 0:tiles], L, X, ALU.max))
            nc.vector.tensor_tensor(L, L, r3, ALU.subtract).then_inc(larg_ready, 1)
            dve.wait_ge(lexp_ready, m + 1)
            c.link(nc.vector.tensor_reduce(red[:, 0:tiles], le[:, 0:tiles, 0:NEXP], X, ALU.add))
            c.link(nc.vector.reciprocal(red[:, 0:tiles], red[:, 0:tiles]))
            c.link(nc.vector.tensor_tensor(pr[:, 0:tiles, 0:NEXP], le[:, 0:tiles, 0:NEXP], r3, ALU.mult))
            apart(dve, passed)
            for j in range(tiles):
                c.mark(nc.vector.max(top[:, j, :], pr[:, j, :]))
            c.join()
            apart(dve, passed)
            for j in range(tiles):
                c.mark(nc.vector.max_index(topi[:, j, :], top[:, j, :], pr[:, j, :]))
            c.join()
            nc.vector.tensor_tensor(dw[:, 0:tiles], top[:, 0:tiles, 1], top[:, 0:tiles, 0], ALU.subtract).then_inc(warg_ready, 1)
            c.mark(nc.vector.tensor_copy(topf[:, 0:tiles, 0:2], topi[:, 0:tiles, 0:2]))
            dve.wait_ge(wexp_ready, m + 1)
            c.link(nc.vector.tensor_scalar(w1[:, 0:tiles], ew[:, 0:tiles], 1.0, None, ALU.add))
            c.link(nc.vector.reciprocal(w0[:, 0:tiles], w1[:, 0:tiles]))
            if later(m, 2):
                dve.wait_ge(gT_done, m - 1)
            for j in range(tiles):
                c.mark(nc.vector.tensor_scalar(gate[:, k, j, :], iotaF[:], topf[:, j, 0:1], w0[:, j:j + 1], ALU.is_equal, ALU.mult))
            c.join()
            c.link(nc.vector.tensor_tensor(w1[:, 0:tiles], ew[:, 0:tiles], w0[:, 0:tiles], ALU.mult))
            for j in range(tiles):
                c.mark(nc.vector.tensor_scalar(hit[:, j, :], iotaF[:], topf[:, j, 1:2], w1[:, j:j + 1], ALU.is_equal, ALU.mult))
            c.join()
            nc.vector.tensor_tensor(gate[:, k, 0:tiles, :], gate[:, k, 0:tiles, :], hit[:, 0:tiles, :], ALU.add).then_inc(gate_ready, 1)
            for group in range(STORES):
                for b in range(halves(tiles)):
                    seq = m * STORES * HALVES + group * halves(tiles) + b
                    dve.wait_ge(e_done, seq + 1)
                    if group == 0:
                        if b == 0:
                            dve.wait_ge(gate_ready, m + 1)
                        w = min(2, tiles - 2 * b)
                        x = xN[:, bass.ds(m * MC + 2 * b, w), :].rearrange("p j d -> p (j d)")
                        nc.vector.tensor_tensor(x, x, psE[b][:, 0:w * D], ALU.add).then_inc(e_added, 1)
                        continue
                    dve.wait_ge(e_added, seq + 1 - halves(tiles))
                    for j in range(2 * b, min(2 * b + 2, tiles)):
                        x = xN[:, bass.ds(m * MC + j, 1), :].rearrange("p a d -> p (a d)")
                        last = nc.vector.scalar_tensor_tensor(x, psE[b][:, (j % 2) * D:(j % 2 + 1) * D], gate[:, k, j, group - 1:group], x, ALU.mult, ALU.add)
                    last.then_inc(e_added, 1)
            if tiles == MC and isinstance(m, int):
                assert c.n - (base + m * LINKS) == LINKS, c.n - (base + m * LINKS)
        CHUNK_LINKS = 36
        in_chunks(dve, chunk)


def build(nc, io):
    with ExitStack() as ctx:
        a = Alloc(nc, ctx, "all")
        io["table"] = nc.dram_tensor("node_table", [NT * P, ROW], F32, kind="Internal").ap()
        io["carries"] = nc.dram_tensor("carries", [STEPS, AGG], F32, kind="Internal").ap()
        keep = dict(xnT=a.sb("xnT", [P, DC, NT * P]), sTab=a.sb("sTab", [P, NT + 1, HEADS]), ident=a.sb("ident", [P, P]))
        wts = dict(wo=a.sb("wo", [P, DC, D]), w1=a.sb("w1", [P, DC, FF]), w2=a.sb("w2", [P, FC, D]),
                   rw1=a.sb("rw1", [P, DC, RH]), rw2=a.sb("rw2", [RH, NEXP]), rb1=a.sb("rb1", [RH, 1]),
                   rb2=a.sb("rb2", [P, NEXP]), eb1=a.sb("eb1", [P, NEXP, DC]), eb2=a.sb("eb2", [P, NEXP, DC]),
                   eb3=a.sb("eb3", [NEXP, D]), b1=a.sb("b1", [P, FC]),
                   stats1=a.sb("stats1", [P, DC, CHUNKS, 6]), stats2=a.sb("stats2", [P, DC, CHUNKS, 6]),
                   **{n: a.sb(n, [P, DC]) for n in ("bo", "b2", "g1", "c1", "g2", "c2")})
        with ExitStack() as phase:
            project_nodes(nc, Alloc(nc, phase, "project"), io, keep)
        with ExitStack() as edges:
            b = Alloc(nc, edges, "edges")
            home = b.sb("home", [P, NT + 1, HOME])
            target = b.sb("target", [P, STEPS])
            with ExitStack() as steps:
                b = Alloc(nc, steps, "plan")
                plan = dict(srcI=b.sb("step_srcI", [P, STEPS], I32), windowI=b.sb("windowI", [1, STEPS], I32),
                            rel16=b.sb("rel16", [P, STEPS], BF16), relHome=b.sb("relHome", [P, STEPS]),
                            isLast=b.sb("isLast", [P, STEPS]), isCarry=b.sb("isCarry", [P, STEPS]), target=target,
                            edge=b.sb("edge", [P, BATCHES, P]), edgeBack=b.sb("edgeBack", [P, BATCHES, P]),
                            iota=b.sb("iota", [P, P]), iota16=b.sb("iota16", [P, P], BF16), eye=b.sb("eye", [P, SB, SB]))
                with ExitStack() as phase:
                    plan_steps(nc, Alloc(nc, phase, "planning"), io, keep, plan)
                with ExitStack() as phase:
                    run_steps(nc, Alloc(nc, phase, "steps"), io, keep, plan, home, wts)
            with ExitStack() as phase:
                merge_attention(nc, Alloc(nc, phase, "merge"), io, keep, home, target, wts)
        with ExitStack() as dense:
            b = Alloc(nc, dense, "dense")
            wts |= {n: b.sb(n, [P, NEXP, DC, D]) for n in ("ew1", "ew2", "ew3")} | {"xN": b.sb("xN", [P, NT, D])}
            with ExitStack() as phase:
                feed_forward(nc, Alloc(nc, phase, "ffn"), io, keep, wts)
            with ExitStack() as phase:
                route_and_mix(nc, Alloc(nc, phase, "experts"), io, keep, wts)


_GNN = ["Wq", "bq", "Wk", "bk", "Wv", "bv", "Wo", "bo", "W1", "b1", "W2", "b2", "bn1_g", "bn1_b", "bn2_g", "bn2_b"]
_FFN = ["router_w1", "router_b1", "router_w2", "router_b2", "expert_w1", "expert_b1", "expert_w2", "expert_b2",
        "expert_w3", "expert_b3"]
_INS = {"x": "x", "src": "src", "dst": "dst"} | {f"L0_gnn_{n}": n for n in _GNN} | {f"L0_ffn_{n}": n for n in _FFN}


def kernel(**inputs):
    import numpy as _np
    import concourse.bacc as _bacc
    from concourse import mybir as _mybir
    from concourse.bass_utils import run_bass_kernel_spmd as _run

    nc = _bacc.Bacc("TRN2", target_bir_lowering=False, num_devices=1)
    arrays, io = {}, {}
    for name, short in _INS.items():
        a = _np.ascontiguousarray(inputs[name])
        arrays[f"in_{name}_dram"] = a
        io[short] = nc.dram_tensor(f"in_{name}_dram", a.shape, _mybir.dt.from_np(a.dtype), kind="ExternalInput").ap()
    io["out"] = nc.dram_tensor("out_0_dram", (N, D), _mybir.dt.float32, kind="ExternalOutput").ap()
    build(nc, io)
    r = _run(nc, [arrays], core_ids=[0])
    return r.results[0]["out_0_dram"]
```

```python
from contextlib import ExitStack

import concourse.bass as bass
from concourse import mybir

F32 = mybir.dt.float32
BF16 = mybir.dt.bfloat16
I32 = mybir.dt.int32
ALU = mybir.AluOpType
ACT = mybir.ActivationFunctionType
X = mybir.AxisListType.X

P = 128
N = 3125
D = 256
DC = D // P
HEADS = 8
HD = D // HEADS
E = 50000
NT = -(-N // P)
NTAIL = N - (NT - 1) * P
ET = -(-E // P)
ETAIL = E - (ET - 1) * P
SB = 16
BATCHES = -(-(ET + NT - 1) // SB)
STEPS = BATCHES * SB
TC = 98
TCH = -(-ET // TC)
TB = 4
CP = STEPS // 4
CCH = STEPS // CP
ROW = D + HEADS
AGG = ROW + 2 * HEADS
HOME = ROW + HEADS
G = 4
NG = SB // G
PARTS = 3
RING = 3
BANKS = 3
BIG = 1e30
FAR = 65536.0
EPS = 1e-5
NEG_SLOPE = 0.2
NC = 448
NCH = -(-N // NC)
NCT = N - (NCH - 1) * NC
FF = 512
FC = FF // P
NEXP = 6
RH = 128


def bcast(ap, shape):
    return ap.to_broadcast(shape)


def in_pairs(eng, n, body, peel=1):
    for j in range(min(2 * peel, n)):
        body(j, j % 2)
    if n // 2 > peel:
        with eng.Fori(peel, n // 2) as i:
            body(i * 2, 0)
            body(i * 2 + 1, 1)
    if n % 2 and n > 2 * peel:
        body(n - 1, 0)


class Alloc:

    def __init__(self, nc, ctx, phase):
        self.nc, self.ctx, self.phase = nc, ctx, phase

    def sb(self, name, shape, dt=F32):
        return self.ctx.enter_context(self.nc.sbuf_tensor(f"{self.phase}_{name}", shape, dt))

    def ps(self, name, shape, dt=F32):
        return self.ctx.enter_context(self.nc.psum_tensor(f"{self.phase}_{name}", shape, dt))

    def sem(self, name):
        return self.ctx.enter_context(self.nc.semaphore(f"{self.phase}_{name}"))


def apart(eng, passed):
    eng.sem_inc(passed, 1)


class Chain:

    def __init__(self, eng, sem):
        self.eng, self.sem, self.n = eng, sem, 0

    def link(self, ins):
        self.mark(ins)
        self.join()

    def mark(self, ins):
        ins.then_inc(self.sem, 1)
        self.n = self.n + 1

    def join(self):
        self.eng.wait_ge(self.sem, self.n)


def project_nodes(nc, a, io, keep, nodes):
    xnT, sTab, ident = keep["xnT"], keep["sTab"], keep["ident"]
    xN, wqkv, bias, meanvar, rstd = (nodes[n] for n in ("xN", "wqkv", "bias", "meanvar", "rstd"))
    xn = a.sb("xn", [P, 2, D])
    xnT_ring = a.sb("xnT_ring", [P, 2, D])
    qkv = a.sb("qkv", [P, 2, 3 * D + HEADS])
    qk = a.sb("qk", [P, 2, D])
    psT = [a.ps(f"psT{i}", [P, 512]) for i in range(2)]
    psQKV = [a.ps(f"psQKV{i}", [P, 1024]) for i in range(2)]

    chain = a.sem("dve_chain")
    xn_ready = a.sem("xn_ready")
    xnT_done = a.sem("xnT_transposed")
    xnT_ready = a.sem("xnT_ready")
    xnT_kept = a.sem("xnT_kept")
    go = a.sem("pool_passed")
    qkv_done = a.sem("qkv_product")
    row_ready = a.sem("row_ready")
    row_out = [a.sem(f"row_out{i}") for i in range(2)]

    block = a.ctx.enter_context(nc.Block())

    @block.sync
    def _(sp):
        def store_row(j, k):
            sp.wait_ge(row_ready, j + 1)
            sp.dma_start(io["table"][bass.ds(j * P, P), :], qkv[:, k, 2 * D:]).then_inc(row_out[k], 16)

        in_pairs(sp, NT, store_row)
        sp.wait_ge(row_out[0], 16 * ((NT + 1) // 2))
        sp.wait_ge(row_out[1], 16 * (NT // 2))

    @block.gpsimd
    def _(pool):
        def keep_xnT(j, k):
            pool.wait_ge(xnT_ready, j + 1)
            apart(pool, go)
            nc.gpsimd.tensor_copy(xnT[:, :, bass.ds(j * P, P)],
                                  xnT_ring[:, k, :].rearrange("p (c n) -> p c n", c=DC)).then_inc(xnT_kept, 1)

        in_pairs(pool, NT, keep_xnT)

    @block.scalar
    def _(act):
        def evacuate(j, k):
            act.wait_ge(xnT_done, j + 1)
            if not isinstance(j, int) or j >= 2:
                act.wait_ge(xnT_kept, j - 1)
                act.wait_ge(qkv_done, j - 1)
            nc.scalar.copy(xnT_ring[:, k, :], psT[k][:, 0:D]).then_inc(xnT_ready, 1)

        in_pairs(act, NT, evacuate)

    @block.vector
    def _(dve):
        c = Chain(dve, chain)
        c.mark(nc.vector.memset(sTab[:, NT, :], 0.0))
        base = c.n

        def normalize(j, k):
            if not isinstance(j, int) or j >= 2:
                dve.wait_ge(xnT_done, j - 1)
            nc.vector.tensor_scalar(xn[:, k, :], xN[:, bass.ds(j, 1), :].rearrange("p a d -> p (a d)"), meanvar[:, bass.ds(j, 1), 0],
                                    rstd[:, bass.ds(j, 1)], ALU.subtract, ALU.mult).then_inc(xn_ready, 1)

        def heads(j, k):
            c.n = base + 3 * j
            dve.wait_ge(qkv_done, j + 1)
            if not isinstance(j, int) or j >= 2:
                dve.wait_ge(row_out[k], (j - k) * 8)
            c.link(nc.vector.tensor_tensor(qkv[:, k, 0:3 * D], psQKV[k][:, 0:3 * D], bias[:], ALU.add))
            c.link(nc.vector.scalar_tensor_tensor(qk[:, k, :], qkv[:, k, 0:D], float(HD) ** -0.5, qkv[:, k, D:2 * D], ALU.mult, ALU.mult))
            s = qkv[:, k, 3 * D:]
            c.link(nc.vector.tensor_reduce(s, qk[:, k, :].rearrange("p (h c) -> p h c", h=HEADS), X, ALU.add))
            nc.vector.tensor_tensor(sTab[:, bass.ds(j, 1), :].rearrange("p a h -> p (a h)"), s, s, ALU.max).then_inc(row_ready, 1)

        normalize(0, 0)
        normalize(1, 1)

        def step(j, k):
            normalize(j + 2, k)
            heads(j, k)
        in_pairs(dve, NT - 3, step)
        step(NT - 3, (NT - 3) % 2)
        for j in (NT - 2, NT - 1):
            heads(j, j % 2)

    @block.tensor
    def _(pe):
        def transpose(j, k):
            pe.wait_ge(xn_ready, j + 1)
            if not isinstance(j, int) or j >= 2:
                pe.wait_ge(xnT_ready, j - 1)
            for c in range(DC):
                last = nc.tensor.transpose(psT[k][:, c * P:(c + 1) * P], xn[:, k, c * P:(c + 1) * P], ident[:])
            last.then_inc(xnT_done, 1)

        def product(j, k):
            pe.wait_ge(xnT_ready, j + 1)
            if not isinstance(j, int) or j >= 2:
                pe.wait_ge(row_ready, j - 1)
            for lo, hi in ((0, 512), (512, 768)):
                for c in range(DC):
                    last = nc.tensor.matmul(psQKV[k][:, lo:hi], xnT_ring[:, k, c * P:(c + 1) * P],
                                            wqkv[:, c, lo:hi], start=(c == 0), stop=(c == DC - 1))
            last.then_inc(qkv_done, 1)

        transpose(0, 0)
        def step(j, k):
            if not isinstance(j, int) or j + 1 < NT:
                transpose(j + 1, 1 - k)
            product(j, k)
        in_pairs(pe, NT, step)


def plan_steps(nc, a, io, keep, plan, nodes):
    ident = keep["ident"]
    xN, wqkv, bias, meanvar, rstd = (nodes[n] for n in ("xN", "wqkv", "bias", "meanvar", "rstd"))
    xstats = a.sb("x_stats", [P, NT, 6])
    xvar = a.sb("x_var", [P, NT])
    xstd = a.sb("x_std", [P, NT])
    srcI = a.sb("srcI", [TC, TCH, P], I32)
    dstI = a.sb("dstI", [TC, TCH, P], I32)
    srcF = a.sb("srcF", [TC, TCH, P])
    dstF = a.sb("dstF", [TC, TCH, P + 1])
    prevI = a.sb("prevI", [TC, TCH], I32)
    prevF = a.sb("prevF", [TC, TCH])
    prevB = a.sb("prevB", [TC, TCH, P])
    firstB = a.sb("firstB", [TC, TCH, P])
    tileI = a.sb("tileI", [TC, TCH], I32)
    tileF = a.sb("tileF", [TC, TCH])
    firstKey = a.sb("firstKey", [TC, TCH])
    stepI = a.sb("stepI", [P, STEPS], I32)
    stepF = a.sb("stepF", [P, STEPS])
    bound = a.sb("bound", [P, STEPS])
    started = a.sb("started", [TC, TCH, STEPS], BF16)
    ones = a.sb("ones", [TC, P], BF16)
    tp = a.sb("tile_of_step", [P, STEPS])
    wp = a.sb("window_of_step", [P, STEPS])
    wp128 = a.sb("window_start", [P, STEPS])
    sel = a.sb("sel", [TC, TCH, STEPS])
    dst = a.sb("dst_of_step", [P, STEPS])
    dstB = a.sb("dst_over_heads", [P, 2, TB, SB, HEADS])
    dstTs = a.sb("dst_T", [P, 2, TB, P])
    differs = a.sb("differs", [P, 2, TB, P])
    prev = a.sb("prev_of_step", [P, STEPS])
    rel = a.sb("rel", [P, STEPS])
    t1 = a.sb("t1", [P, STEPS])
    t2 = a.sb("t2", [P, STEPS])
    iotaI = a.sb("iotaI", [P, P], I32)
    psCount = a.ps("psCount", [P, 512])
    psSel = [a.ps(f"psSel{i}", [P, 512]) for i in range(5)]
    psDT = [a.ps(f"psDT{i}", [P, TB, P]) for i in range(2)]

    x_pad = a.sem("x_pad")
    x_in = a.sem("x_in")
    w_in = a.sem("w_in")
    ident0 = a.sem("ident0")
    ident_ready = a.sem("ident_ready")
    var_ready = a.sem("var_ready")
    std_ready = a.sem("std_ready")
    rstd_ready = a.sem("rstd_ready")
    pads = a.sem("pads")
    idx_in = a.sem("idx_in")
    iotas = a.sem("iotas")
    chain = a.sem("chain")
    key_ready = a.sem("key_ready")
    counted = a.sem("counted")
    sel_ready = a.sem("sel_ready")
    selected = a.sem("selected")
    dst_ready = a.sem("dst_ready")
    dstB_ready = a.sem("dstB_ready")
    dT_done = a.sem("dT_done")
    dT_copied = a.sem("dT_copied")
    differs_ready = a.sem("differs_ready")
    edge_ready = a.sem("edge_ready")

    block = a.ctx.enter_context(nc.Block())
    LASTP = ET - 1 - (TCH - 1) * TC

    @block.sync
    def _(sp):
        sp.wait_ge(pads, 3)
        for name, t in (("src", srcI), ("dst", dstI)):
            full = (TCH - 1) * TC * P
            sp.dma_start(t[:, 0:TCH - 1, :], io[name][0:full].rearrange("(c t e) -> t c e", c=TCH - 1, e=P)).then_inc(idx_in, 16)
            sp.dma_start(t[0:LASTP, TCH - 1, :], io[name][full:full + LASTP * P].rearrange("(t e) -> t e", e=P)).then_inc(idx_in, 16)
            sp.dma_start(t[LASTP:LASTP + 1, TCH - 1, 0:ETAIL], io[name][full + LASTP * P:E].rearrange("(t e) -> t e", t=1)).then_inc(idx_in, 16)
        ends = io["dst"][0:(ET - 1) * P].rearrange("(t e) -> t e", e=P)[:, P - 1:P]
        with nc.allow_non_contiguous_dma(reason="one element of each tile"):
            for c in range(TCH):
                lo, hi = max(1, c * TC), min(ET, (c + 1) * TC)
                sp.dma_start(prevI[lo - c * TC:hi - c * TC, c:c + 1], ends[lo - 1:hi - 1, :]).then_inc(idx_in, 16)
        sp.dma_start(xN[:, 0:NT - 1, :], io["x"][0:(NT - 1) * P, :].rearrange("(j p) d -> p j d", p=P)).then_inc(x_in, 16)
        sp.wait_ge(x_pad, 1)
        sp.dma_start(xN[0:NTAIL, NT - 1, :], io["x"][(NT - 1) * P:N, :]).then_inc(x_in, 16)
        for n, w in enumerate(("Wq", "Wk", "Wv")):
            sp.dma_start(wqkv[:, :, n * D:(n + 1) * D], io[w].rearrange("(c p) n -> p c n", p=P)).then_inc(w_in, 16)
        for n, b in enumerate(("bq", "bk", "bv")):
            sp.dma_start(bias[:, n * D:(n + 1) * D], io[b].partition_broadcast(P)).then_inc(w_in, 16)
        sp.wait_ge(w_in, 96)

    @block.gpsimd
    def _(pool):
        nc.gpsimd.iota(tileI[:], pattern=[[TC, TCH]], base=0, channel_multiplier=1).then_inc(iotas, 1)
        nc.gpsimd.iota(stepI[:], pattern=[[1, STEPS]], base=0, channel_multiplier=0).then_inc(iotas, 1)
        nc.gpsimd.iota(iotaI[:], pattern=[[1, P]], base=0, channel_multiplier=0).then_inc(iotas, 1)
        nc.gpsimd.memset(plan["eye"][:], 0.0).then_inc(iotas, 1)
        nc.gpsimd.memset(ident[:], 0.0).then_inc(ident0, 1)
        pool.wait_ge(iotas, 4)
        nc.gpsimd.affine_select(out=plan["eye"][:], in_=plan["eye"][:], compare_op=ALU.not_equal, fill=1.0, base=0,
                                pattern=[[1, SB], [-1, SB]], channel_multiplier=0).then_inc(iotas, 1)
        pool.wait_ge(ident0, 1)
        nc.gpsimd.affine_select(out=ident[:], in_=ident[:], compare_op=ALU.not_equal, fill=1.0, base=0,
                                pattern=[[-1, P]], channel_multiplier=1).then_inc(ident_ready, 1)

    groups = [range(b, min(b + TB, BATCHES)) for b in range(0, BATCHES, TB)]

    def spread_heads(g):
        k, n = g % 2, len(groups[g])
        cols = dst[:, groups[g][0] * SB:(groups[g][-1] + 1) * SB].rearrange("p (b s) -> p b s", s=SB)
        nc.scalar.copy(dstB[:, k, 0:n, :, :], bcast(cols.unsqueeze(3), [P, n, SB, HEADS])).then_inc(dstB_ready, 1)

    @block.scalar
    def _(act):
        act.wait_ge(var_ready, 1)
        nc.scalar.activation(xstd[:], xvar[:], ACT.Sqrt).then_inc(std_ready, 1)
        act.wait_ge(dst_ready, 1)
        spread_heads(0)
        spread_heads(1)
        for g, members in enumerate(groups):
            k, n = g % 2, len(members)
            act.wait_ge(dT_done, g + 1)
            if g >= 2:
                act.wait_ge(differs_ready, g - 1)
            nc.scalar.copy(dstTs[:, k, 0:n, :], psDT[k][:, 0:n, :]).then_inc(dT_copied, 1)
            if g + 2 < len(groups):
                spread_heads(g + 2)
            act.wait_ge(differs_ready, g + 1)
            nc.scalar.activation(plan["edgeBack"][:, members[0]:members[-1] + 1, P - 1:0:-1], differs[:, k, 0:n, 0:P - 1],
                                 ACT.Copy, scale=-BIG).then_inc(edge_ready, 1)

    @block.vector
    def _(dve):
        c = Chain(dve, chain)
        nc.vector.memset(xN[:, NT - 1, :], 0.0).then_inc(x_pad, 1)
        nc.vector.memset(srcI[:], 0).then_inc(pads, 1)
        nc.vector.memset(dstI[:], int(FAR)).then_inc(pads, 1)
        nc.vector.memset(prevI[:], -1).then_inc(pads, 1)
        c.mark(nc.vector.memset(ones[:], 1.0))
        c.mark(nc.vector.memset(dstF[:, :, P:P + 1], -5.0))
        c.mark(nc.vector.memset(plan["edge"][:, :, 0:1], -BIG))
        c.mark(nc.vector.memset(plan["edgeBack"][:, :, 0:1], -BIG))
        dve.wait_ge(iotas, 5)
        c.mark(nc.vector.tensor_copy(tileF[:], tileI[:]))
        c.mark(nc.vector.tensor_copy(stepF[:], stepI[:]))
        c.mark(nc.vector.tensor_copy(plan["iota"][:], iotaI[:]))
        c.mark(nc.vector.tensor_copy(plan["iota16"][:], iotaI[:]))
        c.join()
        c.mark(nc.vector.tensor_scalar(bound[:], stepF[:], float(P), float(P), ALU.mult, ALU.add))
        dve.wait_ge(idx_in, 160)
        c.mark(nc.vector.tensor_copy(srcF[:], srcI[:]))
        c.mark(nc.vector.tensor_copy(prevF[:], prevI[:]))
        c.link(nc.vector.tensor_copy(dstF[:, :, 0:P], dstI[:]))
        c.mark(nc.vector.tensor_copy(prevB[:], bcast(prevF[:].unsqueeze(2), [TC, TCH, P])))
        c.mark(nc.vector.tensor_copy(firstB[:], bcast(dstF[:, :, 0:1], [TC, TCH, P])))
        c.link(nc.vector.scalar_tensor_tensor(firstKey[:], tileF[:], float(P), dstF[:, :, 0], ALU.mult, ALU.add))
        for k in range(TCH):
            nc.vector.tensor_scalar(started[:, k, :], bound[0:TC, :], firstKey[:, k:k + 1], None, ALU.is_gt).then_inc(key_ready, 1)
        dve.wait_ge(counted, 1)
        c.link(nc.vector.tensor_scalar(tp[:], psCount[:, 0:STEPS], -1.0, 0.0, ALU.add, ALU.max))
        for k in range(TCH):
            c.mark(nc.vector.tensor_scalar(sel[:, k, :], tp[0:TC, :], tileF[:, k:k + 1], None, ALU.is_equal))
        c.join()
        nc.vector.tensor_tensor(wp[:], stepF[:], tp[:], ALU.subtract).then_inc(sel_ready, 1)
        dve.wait_ge(sel_ready, 1)
        c.mark(nc.vector.tensor_copy(plan["windowI"][:], wp[0:1, :]))
        c.mark(nc.vector.tensor_scalar(wp128[:], wp[:], float(P), None, ALU.mult))
        dve.wait_ge(x_in, 32)
        for j in range(NT):
            c.mark(nc.vector.bn_stats(xstats[:, j, :], xN[:, j, :]))
        c.join()
        for j in range(NT):
            c.mark(nc.vector.bn_aggr(meanvar[:, j, :], xstats[:, j, :]))
        c.join()
        nc.vector.tensor_scalar(xvar[:], meanvar[:, :, 1], EPS, None, ALU.add).then_inc(var_ready, 1)
        dve.wait_ge(selected, 5)
        c.link(nc.vector.tensor_copy(dst[:], psSel[1][:, 0:STEPS]))
        c.mark(nc.vector.tensor_copy(plan["srcI"][:], psSel[0][:, 0:STEPS]))
        nc.vector.tensor_copy(prev[:], psSel[3][:, 0:STEPS]).then_inc(dst_ready, 1)
        dve.wait_ge(dst_ready, 1)
        c.mark(nc.vector.tensor_tensor(plan["isLast"][:], dst[:], psSel[2][:, 0:STEPS], ALU.not_equal))
        c.link(nc.vector.tensor_tensor(rel[:], dst[:], wp128[:], ALU.subtract))
        c.mark(nc.vector.tensor_copy(plan["rel16"][:], rel[:]))
        c.link(nc.vector.tensor_tensor(t1[:], dst[:], prev[:], ALU.is_equal))
        c.mark(nc.vector.scalar_tensor_tensor(plan["relHome"][:], t1[:], -1e6, rel[:], ALU.mult, ALU.add))
        c.link(nc.vector.scalar_tensor_tensor(t2[:], rel[:], 0.0, t1[:], ALU.is_ge, ALU.mult))
        c.link(nc.vector.scalar_tensor_tensor(plan["isCarry"][:], rel[:], float(P), t2[:], ALU.is_lt, ALU.mult))
        c.link(nc.vector.tensor_tensor(t1[:], prev[:], psSel[4][:, 0:STEPS], ALU.is_equal))
        c.link(nc.vector.tensor_tensor(rel[:], prev[:], wp128[:], ALU.subtract))
        c.link(nc.vector.scalar_tensor_tensor(t2[:], rel[:], 0.0, t1[:], ALU.is_ge, ALU.mult))
        c.link(nc.vector.scalar_tensor_tensor(t1[:], rel[:], float(P), t2[:], ALU.is_lt, ALU.mult))
        c.link(nc.vector.scalar_tensor_tensor(t2[:], prev[:], 1.0, t1[:], ALU.add, ALU.mult))
        c.mark(nc.vector.tensor_scalar(plan["target"][:], t2[:], -1.0, None, ALU.add))
        dve.wait_ge(std_ready, 1)
        nc.vector.reciprocal(rstd[:], xstd[:]).then_inc(rstd_ready, 1)
        for g, members in enumerate(groups):
            k, n = g % 2, len(members)
            dve.wait_ge(dT_copied, g + 1)
            if g >= 2:
                dve.wait_ge(edge_ready, g - 1)
                c.join()
            nc.vector.tensor_tensor(differs[:, k, 0:n, 0:P - 1], dstTs[:, k, 0:n, 1:P], dstTs[:, k, 0:n, 0:P - 1], ALU.not_equal).then_inc(differs_ready, 1)
            dve.wait_ge(differs_ready, g + 1)
            c.mark(nc.vector.tensor_scalar(plan["edge"][:, members[0]:members[-1] + 1, 1:P], differs[:, k, 0:n, 0:P - 1], -BIG, None, ALU.mult))

    @block.tensor
    def _(pe):
        pe.wait_ge(key_ready, TCH)
        for k in range(TCH):
            last = nc.tensor.matmul(psCount[:, 0:STEPS], ones[:], started[:, k, :], start=(k == 0), stop=(k == TCH - 1))
        last.then_inc(counted, 1)
        pe.wait_ge(sel_ready, 1)
        for n, rows in enumerate((srcF[:], dstF[:, :, 0:P], dstF[:, :, 1:P + 1], prevB[:], firstB[:])):
            for k in range(TCH):
                last = nc.tensor.matmul(psSel[n][:, 0:STEPS], rows[:, k, :], sel[:, k, :], start=(k == 0), stop=(k == TCH - 1))
            last.then_inc(selected, 1)
        pe.wait_ge(ident_ready, 1)
        for g, members in enumerate(groups):
            pe.wait_ge(dstB_ready, g + 1)
            if g >= 2:
                pe.wait_ge(dT_copied, g - 1)
            for i in range(len(members)):
                last = nc.tensor.transpose(psDT[g % 2][:, i, :], dstB[:, g % 2, i, :, :].rearrange("p s h -> p (s h)"), ident[:])
            last.then_inc(dT_done, 1)


def load_dense_weights(nc, sp, sem, io, wts):
    for name, key in (("Wo", "wo"), ("W1", "w1"), ("W2", "w2"), ("router_w1", "rw1")):
        sp.dma_start(wts[key][:], io[name].rearrange("(c p) n -> p c n", p=P)).then_inc(sem, 16)
    sp.dma_start(wts["rw2"][:], io["router_w2"]).then_inc(sem, 16)
    sp.dma_start(wts["rb2"][:], io["router_b2"].partition_broadcast(P)).then_inc(sem, 16)
    sp.dma_start(wts["eb3"][:], io["expert_b3"]).then_inc(sem, 16)
    with nc.allow_non_contiguous_dma(reason="columns of biases"):
        for name, key in (("bo", "bo"), ("b1", "b1"), ("b2", "b2"), ("bn1_g", "g1"), ("bn1_b", "c1"), ("bn2_g", "g2"), ("bn2_b", "c2")):
            sp.dma_start(wts[key][:], io[name].rearrange("(c p) -> p c", p=P)).then_inc(sem, 16)
        sp.dma_start(wts["rb1"][:], io["router_b1"].rearrange("(p c) -> p c", c=1)).then_inc(sem, 16)
        for name, key in (("expert_b1", "eb1"), ("expert_b2", "eb2")):
            for e in range(NEXP):
                sp.dma_start(wts[key][:, e, :], io[name][e, :].rearrange("(c p) -> p c", p=P)).then_inc(sem, 16)


def run_steps(nc, a, io, keep, plan, home, wts):
    ident, sTab = keep["ident"], keep["sTab"]
    rows = [a.sb(f"rows{i}", [P, SB, AGG]) for i in range(RING)]
    srcS = a.sb("src_slots", [P, RING, SB], I32)
    hot16 = a.sb("hot16", [P, NG, G, P], BF16)
    hotT = a.sb("hotT", [P, 2, G, P], BF16)
    sParts = a.sb("s_parts", [P, NT + 1, PARTS, HEADS], BF16)
    sRest = a.sb("s_rest", [P, NT + 1, HEADS])
    hotHome = a.sb("hotHome", [P, 2, G, P])
    carryEye = a.sb("carryEye", [P, RING, SB, SB])
    ss = a.sb("ss", [P, SB, HEADS])
    ssT = a.sb("ssT", [P, P])
    sd = a.sb("sd", [P, SB, HEADS])
    fwd = a.sb("fwd", [P, P])
    bwd = a.sb("bwd", [P, P])
    runT = a.sb("runT", [P, P])
    al = a.sb("al", [P, SB, HEADS])
    am = a.sb("am", [P, SB, HEADS])
    at = a.sb("at", [P, SB, HEADS])
    ar = a.sb("ar", [P, SB, HEADS])
    carrySb = a.sb("carrySb", [SB, RING, AGG])
    ident16 = a.sb("ident16", [P, P], BF16)

    psHot = [a.ps(f"psHot{i}", [P, G, P], BF16) for i in range(2)]
    psS = a.ps("psS", [P, P])
    psM = psS[:].rearrange("p (s h) -> p s h", h=HEADS)
    psD = a.ps("psD", [P, SB, PARTS * HEADS])
    psHome = [a.ps(f"psHome{i}", [P, 512]) for i in range(BANKS)]
    psCarry = a.ps("psCarry", [P, 512])

    gathered = [[a.sem(f"gathered{i}_{g}") for g in range(NG)] for i in range(RING)]
    weights_in = a.sem("weights_in")
    slots_ready = a.sem("slots_ready")
    go = a.sem("pool_passed")
    start = a.sem("start")
    hot_ready = a.sem("hot_ready")
    hotT_done = a.sem("hotT_done")
    hotT_ready = a.sem("hotT_ready")
    sd_done = a.sem("sd_done")
    sd_ready = a.sem("sd_ready")
    ss_ready = a.sem("ss_ready")
    ssT_done = a.sem("ssT_done")
    ssT_ready = a.sem("ssT_ready")
    runT_ready = a.sem("runT_ready")
    run_done = a.sem("run_done")
    arg_ready = a.sem("arg_ready")
    exp_ready = a.sem("exp_ready")
    eye_ready = a.sem("eye_ready")
    msg_ready = a.sem("msg_ready")
    home_done = a.sem("home_done")
    agg_done = a.sem("agg_done")
    home_added = a.sem("home_added")
    carry_copied = a.sem("carry_copied")
    carry_out = [a.sem(f"carry_out{i}") for i in range(RING)]
    chain = a.sem("dve_chain")

    block = a.ctx.enter_context(nc.Block())

    def past(b, first=1):
        return not isinstance(b, int) or b >= first

    def more(b, n):
        return not isinstance(b, int) or b + n < BATCHES

    def in_rounds(eng, body):
        for b in range(RING):
            body(b, b % RING, b // RING)
        with eng.Fori(1, BATCHES // RING) as i:
            for k in range(RING):
                body(i * RING + k, k, i)
        for b in range(BATCHES // RING * RING, BATCHES):
            body(b, b % RING, b // RING)

    def windows(engine, b, g):
        _, w = nc.values_load_multi_w_load_instructions(
            plan["windowI"][0:1, bass.ds(b * SB + g * G, G)], engines=[engine], min_val=0, max_val=NT,
            skip_runtime_bounds_check_because="a step minus its tile is a window")
        return w

    @block.gpsimd
    def _(pool):
        def batch(b, k, r):
            if past(b, RING):
                pool.wait_ge(agg_done, b * SB - RING * SB + G)
                apart(pool, go)
            nc.gpsimd.tensor_copy(srcS[:, k, :], plan["srcI"][:, bass.ds(b * SB, SB)]).then_inc(slots_ready, 1)
            pool.wait_ge(slots_ready, b + 1)
            apart(pool, go)
            for s in range(SB):
                if past(b, RING) and s and s % G == 0:
                    pool.wait_ge(agg_done, b * SB - RING * SB + s + G)
                    apart(pool, go)
                pool.indirect_dma_start(rows[k][:, s, 0:ROW], None, io["table"],
                                        bass.IndirectOffsetOnAxis(srcS[:, k, s:s + 1], 0)).then_inc(gathered[k][s // G], 16)
        in_rounds(pool, batch)

    @block.sync
    def _(sp):
        load_dense_weights(nc, sp, weights_in, io, wts)

        def store_carry(b, k, r):
            sp.wait_ge(carry_copied, b + 1)
            sp.dma_start(io["carries"][bass.ds(b * SB, SB), :], carrySb[:, k, :]).then_inc(carry_out[k], 16)
        in_rounds(sp, store_carry)
        for k in range(RING):
            sp.wait_ge(carry_out[k], 16 * len(range(k, BATCHES, RING)))
        sp.wait_ge(weights_in, 16 * (15 + 2 * NEXP))

    @block.scalar
    def _(act):
        def copy_scores(x, k, r):
            for g in range(NG):
                act.wait_ge(gathered[k][g], r * (16 * G) + 16 * G)
            if past(x):
                act.wait_ge(arg_ready, x)
            nc.scalar.copy(ss[:], rows[k][:, :, D:ROW]).then_inc(ss_ready, 1)

        def copy_scores_T(x):
            act.wait_ge(ssT_done, x + 1)
            nc.scalar.copy(ssT[:], psS[:]).then_inc(ssT_ready, 1)

        def copy_hot(x, g):
            act.wait_ge(hotT_done, x * NG + g + 1)
            if past(x) or g >= 2:
                act.wait_ge(sd_done, x * NG + g - 1)
            nc.scalar.copy(hotT[:, g % 2, :, :], psHot[g % 2][:]).then_inc(hotT_ready, 1)

        def exponent(x, k):
            act.wait_ge(arg_ready, x + 1)
            nc.scalar.activation(rows[k][:, :, D:ROW], ar[:], ACT.Exp).then_inc(exp_ready, 1)

        def prepare(x, k, r):
            copy_hot(x, 0)
            copy_hot(x, 1)
            copy_scores(x, k, r)
            copy_scores_T(x)
            copy_hot(x, 2)
            copy_hot(x, 3)
            exponent(x, k)

        def batch(b, k, r):
            if more(b, 1):
                prepare(b + 1, (k + 1) % RING, r + (k + 1) // RING)
            act.wait_ge(agg_done, b * SB + SB)
            if past(b, RING):
                act.wait_ge(carry_out[k], r * 16)
            nc.scalar.copy(carrySb[:, k, :], psCarry[0:SB, 0:AGG]).then_inc(carry_copied, 1)
        prepare(0, 0, 0)
        in_rounds(act, batch)

    LINKS = 8

    @block.vector
    def _(dve):
        c = Chain(dve, chain)
        nc.vector.tensor_copy(ident16[:], ident[:]).then_inc(start, 1)
        c.mark(nc.vector.memset(home[:], 0.0))
        c.link(nc.vector.tensor_copy(sParts[:, :, 0, :], sTab[:]))
        c.link(nc.vector.tensor_tensor(sRest[:], sTab[:], sParts[:, :, 0, :], ALU.subtract))
        c.link(nc.vector.tensor_copy(sParts[:, :, 1, :], sRest[:]))
        c.link(nc.vector.tensor_tensor(sRest[:], sRest[:], sParts[:, :, 1, :], ALU.subtract))
        nc.vector.tensor_copy(sParts[:, :, 2, :], sRest[:]).then_inc(start, 1)
        base = c.n

        def add_home(b, k, s, w):
            n = b * SB + s
            dve.wait_ge(home_done, n + 1)
            if past(b) or s:
                dve.wait_ge(home_added, n)
            h = home[:, bass.ds(w, 1), :].rearrange("p a d -> p (a d)")
            nc.vector.tensor_tensor(h, h, psHome[(k * SB + s) % BANKS][:, 0:HOME], ALU.add).then_inc(home_added, 1)

        def one_hot(x, g):
            if past(x):
                dve.wait_ge(hotT_done, x * NG + g + 1 - NG)
            nc.vector.tensor_tensor(hot16[:, g, :, :], bcast(plan["iota16"][:].unsqueeze(1), [P, G, P]),
                                    bcast(plan["rel16"][:, bass.ds(x * SB + g * G, G)].unsqueeze(2), [P, G, P]),
                                    ALU.is_equal).then_inc(hot_ready, 1)

        def run_maxima(x):
            c.n = base + x * LINKS
            dve.wait_ge(ssT_ready, x + 1)
            edge = plan["edge"][:, bass.ds(x, 1), :].rearrange("p a e -> p (a e)")
            back = plan["edgeBack"][:, bass.ds(x, 1), :].rearrange("p a e -> p (a e)")
            c.mark(nc.vector.tensor_tensor_scan(fwd[:], edge, ssT[:], -BIG, ALU.add, ALU.max))
            c.link(nc.vector.tensor_tensor_scan(bwd[:, ::-1], back, ssT[:, ::-1], -BIG, ALU.add, ALU.max))
            if past(x):
                dve.wait_ge(run_done, x)
            nc.vector.tensor_tensor(runT[:], fwd[:], bwd[:], ALU.max).then_inc(runT_ready, 1)

        def dst_scores(x):
            dve.wait_ge(sd_done, x * NG + NG)
            nc.vector.tensor_reduce(sd[:], psD[:].rearrange("p s (t h) -> p s h t", t=PARTS), X, ALU.add).then_inc(sd_ready, 1)

        def edge_scores(x):
            c.n = base + x * LINKS + 2
            dve.wait_ge(sd_ready, x + 1)
            dve.wait_ge(ss_ready, x + 1)
            if past(x):
                dve.wait_ge(exp_ready, x)
            c.mark(nc.vector.tensor_tensor(at[:], ss[:], sd[:], ALU.add))
            dve.wait_ge(run_done, x + 1)
            c.mark(nc.vector.tensor_tensor(am[:], psM, sd[:], ALU.add))

        def leaky_scores(x, k):
            c.n = base + x * LINKS + 4
            c.join()
            c.mark(nc.vector.scalar_tensor_tensor(al[:], at[:], NEG_SLOPE, at[:], ALU.mult, ALU.max))
            c.mark(nc.vector.scalar_tensor_tensor(am[:], am[:], NEG_SLOPE, am[:], ALU.mult, ALU.max))
            last = bcast(plan["isLast"][:, bass.ds(x * SB, SB)].unsqueeze(2), [P, SB, HEADS])
            c.mark(nc.vector.tensor_tensor(rows[k][:, :, ROW:ROW + HEADS], psM, last, ALU.mult))
            c.mark(nc.vector.tensor_tensor(rows[k][:, :, ROW + HEADS:], sd[:], last, ALU.mult))

        def exponents(x):
            c.n = base + x * LINKS + 8
            c.join()
            nc.vector.tensor_tensor(ar[:], al[:], am[:], ALU.subtract).then_inc(arg_ready, 1)

        def carry_masks(x, k):
            nc.vector.tensor_tensor(carryEye[:, k, :, :], plan["eye"][:],
                                    bcast(plan["isCarry"][:, bass.ds(x * SB, SB)].unsqueeze(2), [P, SB, SB]),
                                    ALU.mult).then_inc(eye_ready, 1)

        def home_one_hot(b, g):
            if past(b) or g >= 2:
                dve.wait_ge(agg_done, b * SB + g * G - G)
            nc.vector.tensor_tensor(hotHome[:, g % 2, :, :], bcast(plan["iota"][:].unsqueeze(1), [P, G, P]),
                                    bcast(plan["relHome"][:, bass.ds(b * SB + g * G, G)].unsqueeze(2), [P, G, P]),
                                    ALU.is_equal).then_inc(msg_ready, 1)

        def messages(b, k, g):
            if g == 0:
                dve.wait_ge(exp_ready, b + 1)
            v = rows[k][:, g * G:g * G + G, 0:D].rearrange("p s (h c) -> p s h c", h=HEADS)
            ex = bcast(rows[k][:, g * G:g * G + G, D:ROW].unsqueeze(3), [P, G, HEADS, HD])
            nc.vector.tensor_tensor(v, v, ex, ALU.mult).then_inc(msg_ready, 1)

        def batch(b, k, r):
            x, kx = b + 1, (k + 1) % RING
            w = windows(mybir.EngineType.DVE, b, 0)
            home_one_hot(b, 1)
            add_home(b, k, 0, w[0])
            messages(b, k, 1)
            add_home(b, k, 1, w[1])
            if more(b, 1):
                one_hot(x, 2)
            add_home(b, k, 2, w[2])
            if more(b, 1):
                one_hot(x, 3)
            add_home(b, k, 3, w[3])

            home_one_hot(b, 2)
            w = windows(mybir.EngineType.DVE, b, 1)
            add_home(b, k, 4, w[0])
            messages(b, k, 2)
            add_home(b, k, 5, w[1])
            if more(b, 1):
                run_maxima(x)
            add_home(b, k, 6, w[2])
            home_one_hot(b, 3)
            w2 = windows(mybir.EngineType.DVE, b, 2)
            add_home(b, k, 7, w[3])

            add_home(b, k, 8, w2[0])
            messages(b, k, 3)
            add_home(b, k, 9, w2[1])
            if more(b, 1):
                dst_scores(x)
            add_home(b, k, 10, w2[2])
            if more(b, 1):
                edge_scores(x)
            add_home(b, k, 11, w2[3])
            if more(b, 1):
                leaky_scores(x, kx)

            w = windows(mybir.EngineType.DVE, b, 3)
            add_home(b, k, 12, w[0])
            if more(b, 1):
                exponents(x)
                carry_masks(x, kx)
                home_one_hot(x, 0)
            add_home(b, k, 13, w[1])
            if more(b, 1):
                messages(x, kx, 0)
            add_home(b, k, 14, w[2])
            if more(b, 2):
                one_hot(b + 2, 0)
            add_home(b, k, 15, w[3])
            if more(b, 2):
                one_hot(b + 2, 1)

        for g in range(NG):
            one_hot(0, g)
        run_maxima(0)
        dst_scores(0)
        edge_scores(0)
        leaky_scores(0, 0)
        exponents(0)
        assert c.n == base + LINKS
        carry_masks(0, 0)
        home_one_hot(0, 0)
        messages(0, 0, 0)
        one_hot(1, 0)
        one_hot(1, 1)
        in_rounds(dve, batch)

    @block.tensor
    def _(pe):
        def transpose_scores(x):
            pe.wait_ge(ss_ready, x + 1)
            if past(x):
                pe.wait_ge(arg_ready, x)
            nc.tensor.transpose(psS[:], ss[:].rearrange("p s h -> p (s h)"), ident[:]).then_inc(ssT_done, 1)

        def transpose_hot(x, g):
            pe.wait_ge(hot_ready, x * NG + g + 1)
            if past(x) or g >= 2:
                pe.wait_ge(hotT_ready, x * NG + g - 1)
            for s in range(G):
                last = nc.tensor.transpose(psHot[g % 2][:, s, :], hot16[:, g, s, :], ident16[:])
            last.then_inc(hotT_done, 1)

        def look_up(x, g):
            w = windows(mybir.EngineType.PE, x, g)
            pe.wait_ge(hotT_ready, x * NG + g + 1)
            if g == 0 and past(x):
                pe.wait_ge(sd_ready, x)
            for s in range(g * G, g * G + G):
                last = nc.tensor.matmul(psD[:, s, :], hotT[:, g % 2, s % G, :],
                                        sParts[:, bass.ds(w[s % G], 1), :, :].rearrange("p a t h -> p (a t h)"), start=True, stop=True)
            last.then_inc(sd_done, 1)

        def transpose_back(x):
            pe.wait_ge(runT_ready, x + 1)
            nc.tensor.transpose(psS[:], runT[:], ident[:]).then_inc(run_done, 1)

        def sum_steps(b, k, first, last):
            if first % G == 0:
                pe.wait_ge(msg_ready, b * NG * 2 + first // G * 2 + 2)
            for s in range(first, last):
                n = b * SB + s
                if past(b) or s >= BANKS:
                    pe.wait_ge(home_added, n + 1 - BANKS)
                nc.tensor.matmul(psHome[(k * SB + s) % BANKS][:, 0:AGG], hotHome[:, s // G % 2, s % G, :], rows[k][:, s, :],
                                 start=True, stop=True).then_inc(home_done, 1)
                if s == 0:
                    pe.wait_ge(eye_ready, b + 1)
                    if past(b):
                        pe.wait_ge(carry_copied, b)
                nc.tensor.matmul(psCarry[0:SB, 0:AGG], carryEye[:, k, s, :], rows[k][:, s, :],
                                 start=(s == 0), stop=(s == SB - 1)).then_inc(agg_done, 1)

        def batch(b, k, r):
            x = b + 1
            if not more(b, 1):
                for g in range(NG):
                    sum_steps(b, k, g * G, g * G + G)
                return
            sum_steps(b, k, 0, 2)
            transpose_hot(x, 0)
            transpose_hot(x, 1)
            sum_steps(b, k, 2, 4)
            transpose_scores(x)
            look_up(x, 0)
            transpose_hot(x, 2)
            sum_steps(b, k, 4, 6)
            look_up(x, 1)
            transpose_hot(x, 3)
            sum_steps(b, k, 6, 8)
            look_up(x, 2)
            sum_steps(b, k, 8, 10)
            look_up(x, 3)
            transpose_back(x)
            sum_steps(b, k, 10, 12)
            sum_steps(b, k, 12, 16)

        pe.wait_ge(start, 2)
        transpose_hot(0, 0)
        transpose_hot(0, 1)
        transpose_scores(0)
        look_up(0, 0)
        transpose_hot(0, 2)
        look_up(0, 1)
        transpose_hot(0, 3)
        look_up(0, 2)
        look_up(0, 3)
        transpose_back(0)
        in_rounds(pe, batch)


MC = 4
W = MC * P
CHUNKS = -(-NT // MC)
LASTT = NT - (CHUNKS - 1) * MC
LASTN = N - (CHUNKS - 1) * W


def in_chunks(eng, body):
    full = CHUNKS - 1
    for m in range(2):
        body(m, m % 2, MC, W)
    with eng.Fori(1, full // 2) as i:
        body(i * 2, 0, MC, W)
        body(i * 2 + 1, 1, MC, W)
    body(full, full % 2, LASTT, LASTN)


def later(m, first):
    return not isinstance(m, int) or m >= first


def merge_attention(nc, a, io, keep, home, target, wts):
    ident, sTab, xnT = keep["ident"], keep["sTab"], keep["xnT"]
    cr = a.sb("carry_rows", [CP, CCH, AGG])
    vself = a.sb("vself", [P, NT, D])
    merged = a.sb("carry_sums", [P, NT, HOME])
    edge = a.sb("carry_edge", [HEADS, STEPS])
    back = a.sb("carry_edge_back", [HEADS, STEPS])
    mT = a.sb("carry_maxT", [HEADS, STEPS])
    fwd = a.sb("carry_fwd", [HEADS, STEPS])
    bwd = a.sb("carry_bwd", [HEADS, STEPS])
    run = a.sb("carry_run", [HEADS, STEPS])
    lastRow = a.sb("lastRow", [1, STEPS])
    one = a.sb("one", [1, 1])
    targetP = a.sb("targetP", [CP, CCH])
    lastP = a.sb("lastP", [CP, CCH])
    startI = a.sb("startI", [CP, NT], I32)
    startF = a.sb("startF", [CP, NT])
    iotaI = a.sb("iotaI", [P, P], I32)
    iota = a.sb("iotaM", [P, P])
    relC = a.sb("relC", [CP, NT, CCH])
    c1 = a.sb("c1", [CP, CCH, HEADS])
    c2 = a.sb("c2", [CP, CCH, HEADS])
    c3 = a.sb("c3", [CP, CCH, HEADS])
    c4 = a.sb("c4", [CP, CCH, HEADS])
    hotC = a.sb("hotC", [CP, 2, CCH, P])
    al = [a.sb(f"alpha{n}", [P, NT, HEADS]) for n in range(3)]
    ex = [a.sb(f"expo{n}", [P, NT, HEADS]) for n in range(3)]
    tmp = a.sb("tmp", [P, NT, HEADS])
    mx = a.sb("mx", [P, NT, HEADS])
    den = a.sb("den", [P, NT, HEADS])
    attn = a.sb("attn", [P, 2, MC, D])
    part = a.sb("part", [P, 2, MC, D])
    selfp = a.sb("selfp", [P, 2, MC, D])
    attnT = a.sb("attnT", [P, 2, DC, W])
    stats = wts["stats1"]

    psA = a.ps("psA", [P, 512])
    psB = a.ps("psB", [P, 512])
    psC = [a.ps(f"psC{i}", [P, 512]) for i in range(2)]
    psT = [a.ps(f"psAT{i}", [P, 512]) for i in range(2)]
    psO = [a.ps(f"psO{i}", [P, 512]) for i in range(2)]

    loads = a.sem("loads")
    v_in = a.sem("v_in")
    iotas = a.sem("iotas")
    chain = a.sem("chain")
    cT_done = a.sem("cT_done")
    cT_ready = a.sem("cT_ready")
    run_ready = a.sem("run_ready")
    back_done = a.sem("back_done")
    carg_ready = a.sem("carg_ready")
    cexp_ready = a.sem("cexp_ready")
    rows_ready = a.sem("rows_ready")
    hot_ready = a.sem("hot_ready")
    sum_done = a.sem("sum_done")
    sum_kept = a.sem("sum_kept")
    arg_ready = a.sem("arg_ready")
    exp_ready = a.sem("exp_ready")
    scales_ready = a.sem("scales_ready")
    self_ready = a.sem("self_ready")
    attn_ready = a.sem("attn_ready")
    aT_done = a.sem("aT_done")
    aT_ready = a.sem("aT_ready")
    proj_done = a.sem("proj_done")
    resid_done = a.sem("resid_done")
    go = a.sem("passed")
    passed = a.sem("dve_passed")

    block = a.ctx.enter_context(nc.Block())

    @block.sync
    def _(sp):
        sp.dma_start(cr[:], io["carries"].rearrange("(c p) n -> p c n", p=CP)).then_inc(loads, 16)
        sp.dma_start(vself[:], io["table"].rearrange("(j p) n -> p j n", p=P)[:, :, 0:D]).then_inc(v_in, 16)

    @block.gpsimd
    def _(pool):
        nc.gpsimd.iota(startI[:], pattern=[[P, NT]], base=0, channel_multiplier=0).then_inc(iotas, 1)
        nc.gpsimd.iota(iotaI[:], pattern=[[1, P]], base=0, channel_multiplier=0).then_inc(iotas, 1)
        pool.wait_ge(v_in, 16)
        pool.wait_ge(scales_ready, 3)

        def self_part(m, k, tiles, nodes):
            if later(m, 2):
                pool.wait_ge(attn_ready, m - 1)
            apart(pool, go)
            nc.gpsimd.tensor_tensor(selfp[:, k, 0:tiles, :].rearrange("p j (h c) -> p j h c", h=HEADS),
                                    vself[:, bass.ds(m * MC, tiles), :].rearrange("p j (h c) -> p j h c", h=HEADS),
                                    bcast(ex[2][:, bass.ds(m * MC, tiles), :].unsqueeze(3), [P, tiles, HEADS, HD]),
                                    ALU.mult).then_inc(self_ready, 1)
        in_chunks(pool, self_part)

    @block.scalar
    def _(act):
        act.wait_ge(cT_done, 1)
        nc.scalar.copy(mT[:], psA[0:HEADS, 0:STEPS]).then_inc(cT_ready, 1)
        act.wait_ge(carg_ready, 1)
        nc.scalar.activation(c3[:], c4[:], ACT.Exp).then_inc(cexp_ready, 1)

        def keep_sum(j, k):
            act.wait_ge(sum_done, j + 1)
            apart(act, go)
            nc.scalar.copy(merged[:, bass.ds(j, 1), :].rearrange("p a d -> p (a d)"), psC[k][:, 0:HOME]).then_inc(sum_kept, 1)
        in_pairs(act, NT, keep_sum)
        act.wait_ge(arg_ready, 3)
        for n in range(3):
            nc.scalar.activation(ex[n][:], al[n][:], ACT.Exp).then_inc(exp_ready, 1)

        def evacuate(m, k, tiles, nodes):
            for c in range(DC):
                act.wait_ge(aT_done, m * DC + c + 1)
                if later(m, 2) and c == 0:
                    act.wait_ge(proj_done, m * DC - DC)
                nc.scalar.copy(attnT[:, k, c, 0:tiles * P], psT[c][:, 0:tiles * P]).then_inc(aT_ready, 1)
        in_chunks(act, evacuate)

    @block.tensor
    def _(pe):
        pe.wait_ge(loads, 16)
        for c in range(CCH):
            last = nc.tensor.transpose(psA[0:HEADS, c * CP:(c + 1) * CP], cr[:, c, ROW:ROW + HEADS], ident[0:CP, 0:CP])
        last.then_inc(cT_done, 1)
        pe.wait_ge(run_ready, 1)
        for c in range(CCH):
            nc.tensor.transpose(psB[0:CP, c * HEADS:(c + 1) * HEADS], run[:, c * CP:(c + 1) * CP], ident[0:HEADS, 0:HEADS])
        for c in range(CCH):
            nc.tensor.matmul(psB[0:CP, 64 + c:65 + c], target[0:1, c * CP:(c + 1) * CP], one[:], start=True, stop=True)
            last = nc.tensor.matmul(psB[0:CP, 80 + c:81 + c], lastRow[:, c * CP:(c + 1) * CP], one[:], start=True, stop=True)
        last.then_inc(back_done, 1)
        pe.wait_ge(rows_ready, 2)

        def sum_carries(j, k):
            pe.wait_ge(hot_ready, j + 1)
            if not isinstance(j, int) or j >= 2:
                pe.wait_ge(sum_kept, j - 1)
            for c in range(CCH):
                last = nc.tensor.matmul(psC[k][:, 0:HOME], hotC[:, k, c, :], cr[:, c, 0:HOME], start=(c == 0), stop=(c == CCH - 1))
            last.then_inc(sum_done, 1)
        in_pairs(pe, NT, sum_carries)

        def project(m, k, tiles, nodes):
            pe.wait_ge(attn_ready, m + 1)
            for c in range(DC):
                if later(m, 1):
                    pe.wait_ge(aT_ready, m * DC + c + 1 - DC)
                for j in range(tiles):
                    last = nc.tensor.transpose(psT[c][:, j * P:(j + 1) * P], attn[:, k, j, c * P:(c + 1) * P], ident[:])
                last.then_inc(aT_done, 1)
            pe.wait_ge(aT_ready, m * DC + DC)
            for o in range(DC):
                if later(m, 1):
                    pe.wait_ge(resid_done, m * DC + o + 1 - DC)
                for c in range(DC):
                    last = nc.tensor.matmul(psO[o][:, 0:tiles * P], wts["wo"][:, c, o * P:(o + 1) * P],
                                            attnT[:, k, c, 0:tiles * P], start=(c == 0), stop=(c == DC - 1))
                last.then_inc(proj_done, 1)
        in_chunks(pe, project)

    @block.vector
    def _(dve):
        c = Chain(dve, chain)
        c.mark(nc.vector.memset(one[:], 1.0))
        c.mark(nc.vector.memset(edge[:, 0:1], -BIG))
        c.mark(nc.vector.memset(back[:, 0:1], -BIG))
        c.mark(nc.vector.memset(lastRow[:, STEPS - 1:STEPS], 1.0))
        c.mark(nc.vector.tensor_tensor(lastRow[:, 0:STEPS - 1], target[0:1, 1:STEPS], target[0:1, 0:STEPS - 1], ALU.not_equal))
        c.link(nc.vector.tensor_tensor(fwd[:, 1:STEPS], target[0:HEADS, 1:STEPS], target[0:HEADS, 0:STEPS - 1], ALU.not_equal))
        c.mark(nc.vector.tensor_scalar(edge[:, 1:STEPS], fwd[:, 1:STEPS], -BIG, None, ALU.mult))
        c.link(nc.vector.tensor_scalar(back[:, STEPS - 1:0:-1], fwd[:, 1:STEPS], -BIG, None, ALU.mult))
        dve.wait_ge(iotas, 2)
        c.mark(nc.vector.tensor_copy(startF[:], startI[:]))
        c.mark(nc.vector.tensor_copy(iota[:], iotaI[:]))
        dve.wait_ge(cT_ready, 1)
        c.mark(nc.vector.tensor_tensor_scan(fwd[:], edge[:], mT[:], -BIG, ALU.add, ALU.max))
        c.link(nc.vector.tensor_tensor_scan(bwd[:, ::-1], back[:], mT[:, ::-1], -BIG, ALU.add, ALU.max))
        nc.vector.tensor_tensor(run[:], fwd[:], bwd[:], ALU.max).then_inc(run_ready, 1)
        dve.wait_ge(back_done, 1)
        dve.wait_ge(loads, 16)
        c.mark(nc.vector.tensor_copy(targetP[:], psB[0:CP, 64:64 + CCH]))
        c.link(nc.vector.tensor_copy(lastP[:], psB[0:CP, 80:80 + CCH]))
        c.mark(nc.vector.tensor_tensor(relC[:], bcast(targetP[:].unsqueeze(1), [CP, NT, CCH]),
                                       bcast(startF[:].unsqueeze(2), [CP, NT, CCH]), ALU.subtract))
        crun = psB[0:CP, 0:CCH * HEADS].rearrange("p (c h) -> p c h", h=HEADS)
        cmax, csd = cr[:, :, ROW:ROW + HEADS], cr[:, :, ROW + HEADS:AGG]
        c.mark(nc.vector.tensor_tensor(c1[:], cmax, csd, ALU.add))
        c.link(nc.vector.tensor_tensor(c2[:], crun, csd, ALU.add))
        c.mark(nc.vector.scalar_tensor_tensor(c3[:], c1[:], NEG_SLOPE, c1[:], ALU.mult, ALU.max))
        c.link(nc.vector.scalar_tensor_tensor(c4[:], c2[:], NEG_SLOPE, c2[:], ALU.mult, ALU.max))
        c.link(nc.vector.tensor_tensor(cmax, crun, bcast(lastP[:].unsqueeze(2), [CP, CCH, HEADS]), ALU.mult))
        nc.vector.tensor_tensor(c4[:], c3[:], c4[:], ALU.subtract).then_inc(carg_ready, 1)
        dve.wait_ge(cexp_ready, 1)
        v = cr[:, :, 0:D].rearrange("p s (h c) -> p s h c", h=HEADS)
        nc.vector.tensor_tensor(v, v, bcast(c3[:].unsqueeze(3), [CP, CCH, HEADS, HD]), ALU.mult).then_inc(rows_ready, 1)
        nc.vector.tensor_tensor(cr[:, :, D:ROW], cr[:, :, D:ROW], c3[:], ALU.mult).then_inc(rows_ready, 1)

        def one_hot(j, k):
            if not isinstance(j, int) or j >= 2:
                dve.wait_ge(sum_done, j - 1)
            nc.vector.tensor_tensor(hotC[:, k, :, :], bcast(iota[0:CP, :].unsqueeze(1), [CP, CCH, P]),
                                    bcast(relC[:, bass.ds(j, 1), :].rearrange("p a c -> p (a c)").unsqueeze(2), [CP, CCH, P]),
                                    ALU.is_equal).then_inc(hot_ready, 1)
        in_pairs(dve, NT, one_hot)

        sd = sTab[:, 0:NT, :]
        dve.wait_ge(sum_kept, NT)
        for n, t in enumerate((home[:, 0:NT, :], merged[:])):
            c.link(nc.vector.tensor_scalar(tmp[:], t[:, :, D:ROW], 0.5, -BIG, ALU.is_lt, ALU.mult))
            c.link(nc.vector.tensor_tensor(tmp[:], tmp[:], t[:, :, ROW:HOME], ALU.add))
            c.link(nc.vector.tensor_tensor(tmp[:], tmp[:], sd, ALU.add))
            c.link(nc.vector.scalar_tensor_tensor(al[n][:], tmp[:], NEG_SLOPE, tmp[:], ALU.mult, ALU.max))
        c.link(nc.vector.tensor_scalar(tmp[:], sd, 2.0, None, ALU.mult))
        c.link(nc.vector.scalar_tensor_tensor(al[2][:], tmp[:], NEG_SLOPE, tmp[:], ALU.mult, ALU.max))
        c.link(nc.vector.tensor_tensor(mx[:], al[0][:], al[1][:], ALU.max))
        c.link(nc.vector.tensor_tensor(mx[:], mx[:], al[2][:], ALU.max))
        for n in range(3):
            nc.vector.tensor_tensor(al[n][:], al[n][:], mx[:], ALU.subtract).then_inc(arg_ready, 1)
        dve.wait_ge(exp_ready, 3)
        c.mark(nc.vector.tensor_tensor(den[:], home[:, 0:NT, D:ROW], ex[0][:], ALU.mult))
        c.link(nc.vector.tensor_tensor(mx[:], merged[:, :, D:ROW], ex[1][:], ALU.mult))
        c.link(nc.vector.tensor_tensor(den[:], den[:], mx[:], ALU.add))
        c.link(nc.vector.tensor_tensor(den[:], den[:], ex[2][:], ALU.add))
        c.link(nc.vector.reciprocal(mx[:], den[:]))
        for n in range(3):
            nc.vector.tensor_tensor(ex[n][:], ex[n][:], mx[:], ALU.mult).then_inc(scales_ready, 1)
        dve.wait_ge(scales_ready, 3)
        base = c.n
        LINKS = 3 + DC

        def combine(m, k, tiles, nodes):
            c.n = base + m * LINKS
            t = bass.ds(m * MC, tiles)
            heads = lambda v: v.rearrange("p j (h c) -> p j h c", h=HEADS)
            out, other = attn[:, k, 0:tiles, :], part[:, k, 0:tiles, :]
            if later(m, 2):
                dve.wait_ge(aT_done, m * DC - DC)
            c.mark(nc.vector.tensor_tensor(heads(out), heads(home[:, t, 0:D]), bcast(ex[0][:, t, :].unsqueeze(3), [P, tiles, HEADS, HD]), ALU.mult))
            c.link(nc.vector.tensor_tensor(heads(other), heads(merged[:, t, 0:D]), bcast(ex[1][:, t, :].unsqueeze(3), [P, tiles, HEADS, HD]), ALU.mult))
            c.link(nc.vector.tensor_tensor(out, out, other, ALU.add))
            dve.wait_ge(self_ready, m + 1)
            nc.vector.tensor_tensor(out, out, selfp[:, k, 0:tiles, :], ALU.add).then_inc(attn_ready, 1)

        def residual(m, k, tiles, nodes):
            c.n = base + m * LINKS + 3
            for o in range(DC):
                dve.wait_ge(proj_done, m * DC + o + 1)
                h = xnT[:, o, bass.ds(m * W, tiles * P)]
                nc.vector.scalar_tensor_tensor(h, psO[o][:, 0:tiles * P], wts["bo"][:, o:o + 1], h, ALU.add, ALU.add).then_inc(resid_done, 1)
                dve.wait_ge(resid_done, m * DC + o + 1)
                apart(dve, passed)
                c.link(nc.vector.bn_stats(stats[:, o, bass.ds(m, 1), :].rearrange("p a s -> p (a s)"), xnT[:, o, bass.ds(m * W, nodes)]))

        def both(m, k, tiles, nodes):
            combine(m, k, tiles, nodes)
            residual(m, k, tiles, nodes)
        in_chunks(dve, both)


def batch_norm_scale(nc, c, dve, act_sems, stats, norm, gain, shift):
    var_ready, std_ready = act_sems
    for o in range(DC):
        c.mark(nc.vector.bn_aggr(norm["mv"][:, o, :], stats[:, o, :, :]))
    c.join()
    nc.vector.tensor_scalar(norm["var"][:], norm["mv"][:, :, 1], EPS, None, ALU.add).then_inc(var_ready, 1)
    dve.wait_ge(std_ready, 1)
    c.link(nc.vector.reciprocal(norm["var"][:], norm["std"][:]))
    c.link(nc.vector.tensor_tensor(norm["scale"][:], norm["var"][:], gain, ALU.mult))
    c.link(nc.vector.tensor_tensor(norm["var"][:], norm["mv"][:, :, 0], norm["scale"][:], ALU.mult))
    c.link(nc.vector.tensor_tensor(norm["shift"][:], shift, norm["var"][:], ALU.subtract))


def feed_forward(nc, a, io, keep, wts):
    xnT = keep["xnT"]
    hidden = a.sb("hidden", [P, 2, FC, W])
    norm = {n: a.sb(f"norm_{n}", [P, DC]) for n in ("var", "std", "scale", "shift")}
    norm["mv"] = a.sb("norm_mv", [P, DC, 2])
    scratch = a.sb("scratch", [P, 1])
    psF = [a.ps(f"psF{i}", [P, 512]) for i in range(4)]
    psY = [a.ps(f"psY{i}", [P, 512]) for i in range(4)]
    chain = a.sem("chain")
    var_ready = a.sem("var_ready")
    std_ready = a.sem("std_ready")
    h_ready = a.sem("h_ready")
    ff_done = a.sem("ff_done")
    relu_done = a.sem("relu_done")
    y_done = a.sem("y_done")
    y_added = a.sem("y_added")
    passed = a.sem("passed")
    loads = a.sem("expert_loads")
    tail_zero = a.sem("tail_zero")
    block = a.ctx.enter_context(nc.Block())

    @block.sync
    def _(sp):
        sp.dma_start(wts["xN"][:, 0:NT - 1, :], io["x"][0:(NT - 1) * P, :].rearrange("(j p) d -> p j d", p=P)).then_inc(loads, 16)
        for name, key in (("expert_w1", "ew1"), ("expert_w2", "ew2"), ("expert_w3", "ew3")):
            sp.dma_start(wts[key][:], io[name].rearrange("e (c p) n -> p e c n", p=P)).then_inc(loads, 16)
        sp.wait_ge(tail_zero, 1)
        sp.dma_start(wts["xN"][0:NTAIL, NT - 1, :], io["x"][(NT - 1) * P:N, :]).then_inc(loads, 16)
        sp.wait_ge(loads, 80)

    @block.gpsimd
    def _(pool):
        nc.gpsimd.memset(wts["xN"][:, NT - 1, :], 0.0).then_inc(tail_zero, 1)

    @block.scalar
    def _(act):
        act.wait_ge(var_ready, 1)
        nc.scalar.activation(norm["std"][:], norm["var"][:], ACT.Sqrt).then_inc(std_ready, 1)

        def relu(m, k, tiles, nodes):
            for f in range(FC):
                act.wait_ge(ff_done, m * FC + f + 1)
                if later(m, 2) and f == 0:
                    act.wait_ge(y_done, m * DC - DC)
                nc.scalar.activation(hidden[:, k, f, 0:nodes], psF[f][:, 0:nodes], ACT.Relu,
                                     bias=wts["b1"][:, f:f + 1]).then_inc(relu_done, 1)
        in_chunks(act, relu)

    @block.tensor
    def _(pe):
        def up(m, k, tiles, nodes):
            pe.wait_ge(h_ready, m + 1)
            for f in range(FC):
                if later(m, 1):
                    pe.wait_ge(relu_done, m * FC + f + 1 - FC)
                for c in range(DC):
                    last = nc.tensor.matmul(psF[f][:, 0:nodes], wts["w1"][:, c, f * P:(f + 1) * P],
                                            xnT[:, c, bass.ds(m * W, nodes)], start=(c == 0), stop=(c == DC - 1))
                last.then_inc(ff_done, 1)

        def down(m, k, tiles, nodes):
            for o in range(DC):
                if later(m, 2):
                    pe.wait_ge(y_added, m * DC + o + 1 - 2 * DC)
                for f in range(FC):
                    if o == 0:
                        pe.wait_ge(relu_done, m * FC + f + 1)
                    last = nc.tensor.matmul(psY[2 * k + o][:, 0:nodes], wts["w2"][:, f, o * P:(o + 1) * P],
                                            hidden[:, k, f, 0:nodes], start=(f == 0), stop=(f == FC - 1))
                last.then_inc(y_done, 1)

        def chunk(m, k, tiles, nodes):
            up(m, k, tiles, nodes)
            down(m, k, tiles, nodes)
        in_chunks(pe, chunk)

    @block.vector
    def _(dve):
        c = Chain(dve, chain)
        batch_norm_scale(nc, c, dve, (var_ready, std_ready), wts["stats1"], norm, wts["g1"][:], wts["c1"][:])
        base = c.n

        def normalize(m, k, tiles, nodes):
            for o in range(DC):
                h = xnT[:, o, bass.ds(m * W, nodes)]
                last = nc.vector.tensor_scalar(h, h, norm["scale"][:, o:o + 1], norm["shift"][:, o:o + 1], ALU.mult, ALU.add)
            last.then_inc(h_ready, 1)
        in_chunks(dve, normalize)

        def add(m, k, tiles, nodes):
            for o in range(DC):
                dve.wait_ge(y_done, m * DC + o + 1)
                h = xnT[:, o, bass.ds(m * W, nodes)]
                nc.vector.scalar_tensor_tensor(h, psY[2 * k + o][:, 0:nodes], wts["b2"][:, o:o + 1], h, ALU.add, ALU.add).then_inc(y_added, 1)
                dve.wait_ge(y_added, m * DC + o + 1)
                apart(dve, passed)
                last = nc.vector.bn_stats(wts["stats2"][:, o, bass.ds(m, 1), :].rearrange("p a s -> p (a s)"), h)
        in_chunks(dve, add)


def route_and_mix(nc, a, io, keep, wts):
    xN, xnT, ident = wts["xN"], keep["xnT"], keep["ident"]
    norm = {n: a.sb(f"norm2_{n}", [P, DC]) for n in ("var", "std", "scale", "shift")}
    norm["mv"] = a.sb("norm2_mv", [P, DC, 2])
    y = a.sb("y", [P, 2, DC, W])
    st = a.sb("ln_stats", [P, 2, MC, 6])
    mv = a.sb("ln_mv", [P, 2, MC, 2])
    va = a.sb("ln_var", [P, 2, MC])
    sdv = a.sb("ln_std", [P, 2, MC])
    rs = a.sb("ln_rstd", [P, 2, MC])
    x2 = a.sb("x2", [P, 2, MC, D])
    x2T = a.sb("x2T", [P, 2, DC, W])
    rh = a.sb("rh", [P, 2, W])
    lg = a.sb("lg", [P, MC, 8])
    le = a.sb("le", [P, MC, 8])
    pr = a.sb("pr", [P, MC, 8])
    red = a.sb("red", [P, MC])
    top = a.sb("top", [P, MC, 8])
    topi = a.sb("topi", [P, MC, 8], mybir.dt.uint32)
    topf = a.sb("topf", [P, MC, 8])
    dw = a.sb("dw", [P, MC])
    ew = a.sb("ew", [P, MC])
    w0 = a.sb("w0", [P, MC])
    w1 = a.sb("w1_", [P, MC])
    hit = a.sb("hit", [P, MC, NEXP])
    gate = a.sb("gate", [P, 2, MC, NEXP])
    gateT = a.sb("gateT", [NEXP, 2, W])
    iotaI = a.sb("iotaE", [P, NEXP], I32)
    iotaF = a.sb("iotaEf", [P, NEXP])
    h1 = a.sb("h1", [P, 2, DC, W])
    h2 = a.sb("h2", [P, 2, DC, W])

    psT = [a.ps(f"psX{i}", [P, 512]) for i in range(2)]
    psR = a.ps("psR", [P, 512])
    psL = a.ps("psL", [P, 512])
    psH = [a.ps(f"psH{i}", [P, 512]) for i in range(2)]
    psE = [a.ps(f"psE{i}", [P, 512]) for i in range(2)]

    chain = a.sem("chain")
    var_ready = a.sem("var_ready")
    std_ready = a.sem("std_ready")
    iotas = a.sem("iotas")
    y_ready = a.sem("y_ready")
    yT_done = a.sem("yT_done")
    yT_added = a.sem("yT_added")
    lnvar_ready = a.sem("lnvar_ready")
    lnstd_ready = a.sem("lnstd_ready")
    x2_ready = a.sem("x2_ready")
    x2T_done = a.sem("x2T_done")
    x2T_ready = a.sem("x2T_ready")
    r_done = a.sem("router_done")
    r_relu = a.sem("router_relu")
    l_done = a.sem("logits_done")
    larg_ready = a.sem("larg_ready")
    lexp_ready = a.sem("lexp_ready")
    warg_ready = a.sem("warg_ready")
    wexp_ready = a.sem("wexp_ready")
    gate_ready = a.sem("gate_ready")
    gT_done = a.sem("gT_done")
    gT_ready = a.sem("gT_ready")
    hid_done = a.sem("hid_done")
    hid_relu = a.sem("hid_relu")
    e_done = a.sem("e_done")
    e_added = a.sem("e_added")
    out_done = a.sem("out_done")
    passed = a.sem("passed")
    block = a.ctx.enter_context(nc.Block())
    HALVES = MC // 2
    STORES = NEXP + 1

    def halves(tiles):
        return -(-tiles // 2)

    @block.sync
    def _(sp):
        def store(m, k, tiles, nodes):
            if tiles == MC:
                sp.wait_ge(e_added, (m + 1) * STORES * HALVES)
                sp.dma_start(io["out"][bass.ds(m * W, W), :].rearrange("(j p) d -> p j d", p=P), xN[:, bass.ds(m * MC, MC), :]).then_inc(out_done, 16)
            else:
                sp.wait_ge(e_added, (CHUNKS - 1) * STORES * HALVES + STORES * halves(tiles))
                sp.dma_start(io["out"][m * W:N, :], xN[0:nodes, m * MC, :]).then_inc(out_done, 16)
        in_chunks(sp, store)
        sp.wait_ge(out_done, 16 * CHUNKS)

    @block.gpsimd
    def _(pool):
        nc.gpsimd.iota(iotaI[:], pattern=[[1, NEXP]], base=0, channel_multiplier=0).then_inc(iotas, 1)


    def in_order(eng, body, prologue):
        full = CHUNKS - 1
        prologue(0, 0, MC, W)
        body(0, 0, MC, W, (1, 1, MC, W))
        with eng.Fori(0, (full - 2) // 2) as i:
            body(i * 2 + 1, 1, MC, W, (i * 2 + 2, 0, MC, W))
            body(i * 2 + 2, 0, MC, W, (i * 2 + 3, 1, MC, W))
        body(full - 1, (full - 1) % 2, MC, W, (full, full % 2, LASTT, LASTN))
        body(full, full % 2, LASTT, LASTN, None)
    assert CHUNKS % 2 and CHUNKS >= 5

    @block.scalar
    def _(act):
        act.wait_ge(var_ready, 1)
        nc.scalar.activation(norm["std"][:], norm["var"][:], ACT.Sqrt).then_inc(std_ready, 1)

        def ln_std(x, k, tiles, nodes):
            act.wait_ge(lnvar_ready, x + 1)
            nc.scalar.activation(sdv[:, k, 0:tiles], va[:, k, 0:tiles], ACT.Sqrt).then_inc(lnstd_ready, 1)

        def copy_x2T(x, k, tiles, nodes):
            for c in range(DC):
                act.wait_ge(x2T_done, x * DC + c + 1)
                if later(x, 2) and c == 0:
                    act.wait_ge(hid_done, (x - 1) * (NEXP * 2 * DC))
                nc.scalar.copy(x2T[:, k, c, 0:tiles * P], psT[c][:, 0:tiles * P]).then_inc(x2T_ready, 1)

        def router_relu(x, k, tiles, nodes):
            act.wait_ge(r_done, x + 1)
            nc.scalar.activation(rh[:, k, 0:tiles * P], psR[:, 0:tiles * P], ACT.Relu, bias=wts["rb1"][:, 0:1]).then_inc(r_relu, 1)

        def logit_exp(x, k, tiles, nodes):
            act.wait_ge(larg_ready, x + 1)
            nc.scalar.activation(le[:, 0:tiles, 0:NEXP], lg[:, 0:tiles, 0:NEXP], ACT.Exp).then_inc(lexp_ready, 1)

        def weight_exp(x, k, tiles, nodes):
            act.wait_ge(warg_ready, x + 1)
            nc.scalar.activation(ew[:, 0:tiles], dw[:, 0:tiles], ACT.Exp).then_inc(wexp_ready, 1)

        def copy_gate(x, k, tiles, nodes):
            act.wait_ge(gT_done, x + 1)
            nc.scalar.copy(gateT[:, k, 0:tiles * P], psR[0:NEXP, 0:tiles * P]).then_inc(gT_ready, 1)

        def hidden(m, e, layer, tiles):
            h, b = ((h1, "eb1"), (h2, "eb2"))[layer]
            for o in range(DC):
                act.wait_ge(hid_done, ((m * NEXP + e) * 2 + layer) * DC + o + 1)
                if layer == 1 and o == 0 and (later(m, 1) or e >= 2):
                    act.wait_ge(e_done, m * STORES * HALVES + e * halves(tiles) if e >= 2 else m * STORES * HALVES - (1 - e) * HALVES)
                nc.scalar.activation(h[:, e % 2, o, 0:tiles * P], psH[o][:, 0:tiles * P], ACT.Relu,
                                     bias=wts[b][:, e, o:o + 1]).then_inc(hid_relu, 1)

        pieces = {(1, 0): ln_std, (1, 1): copy_x2T, (2, 0): router_relu, (2, 1): logit_exp, (3, 0): weight_exp, (4, 1): copy_gate}

        def chunk(m, k, tiles, nodes, then):
            for e in range(NEXP):
                for layer in range(2):
                    hidden(m, e, layer, tiles)
                    if then and (e, layer) in pieces:
                        pieces[e, layer](*then)

        def prologue(*x):
            for piece in pieces.values():
                piece(*x)
        in_order(act, chunk, prologue)

    @block.tensor
    def _(pe):
        def transpose_y(x, k, tiles, nodes):
            pe.wait_ge(y_ready, x + 1)
            for b in range(halves(tiles)):
                if later(x, 1):
                    pe.wait_ge(x2T_ready, x * DC)
                for j in range(2 * b, min(2 * b + 2, tiles)):
                    for c in range(DC):
                        last = nc.tensor.transpose(psT[b][:, (j % 2) * D + c * P:(j % 2) * D + (c + 1) * P], y[:, k, c, j * P:(j + 1) * P], ident[:])
            last.then_inc(yT_done, 1)

        def transpose_x2(x, k, tiles, nodes):
            pe.wait_ge(x2_ready, x + 1)
            for c in range(DC):
                for j in range(tiles):
                    last = nc.tensor.transpose(psT[c][:, j * P:(j + 1) * P], x2[:, k, j, c * P:(c + 1) * P], ident[:])
                last.then_inc(x2T_done, 1)

        def router(x, k, tiles, nodes):
            pe.wait_ge(x2T_ready, x * DC + DC)
            if later(x, 1):
                pe.wait_ge(gT_ready, x)
            for c in range(DC):
                last = nc.tensor.matmul(psR[:, 0:tiles * P], wts["rw1"][:, c, :], x2T[:, k, c, 0:tiles * P], start=(c == 0), stop=(c == DC - 1))
            last.then_inc(r_done, 1)

        def logits(x, k, tiles, nodes):
            pe.wait_ge(r_relu, x + 1)
            if later(x, 1):
                pe.wait_ge(larg_ready, x)
            for j in range(tiles):
                last = nc.tensor.matmul(psL[:, j * 8:j * 8 + NEXP], rh[:, k, j * P:(j + 1) * P], wts["rw2"][:], start=True, stop=True)
            last.then_inc(l_done, 1)

        def transpose_gate(x, k, tiles, nodes):
            pe.wait_ge(gate_ready, x + 1)
            for j in range(tiles):
                last = nc.tensor.transpose(psR[0:NEXP, j * P:(j + 1) * P], gate[:, k, j, :], ident[:])
            last.then_inc(gT_done, 1)

        def node_rows(m, group, tiles, lhs, rhs_list):
            for b in range(halves(tiles)):
                prior = m * STORES * HALVES + group * halves(tiles) + b
                if later(m, 1) or group * halves(tiles) + b >= 2:
                    pe.wait_ge(e_added, prior - 1 if halves(tiles) == HALVES else prior)
                for j in range(2 * b, min(2 * b + 2, tiles)):
                    for i, r in enumerate(rhs_list):
                        last = nc.tensor.matmul(psE[b][:, (j % 2) * D:(j % 2 + 1) * D], lhs(i, j), r, start=(i == 0), stop=(i == len(rhs_list) - 1))
                last.then_inc(e_done, 1)

        def hidden(m, k, e, layer, n):
            src, w = ((x2T[:, k], "ew1"), (h1[:, e % 2], "ew2"))[layer]
            for o in range(DC):
                idx = ((m * NEXP + e) * 2 + layer) * DC + o
                if later(m, 1) or idx >= DC:
                    pe.wait_ge(hid_relu, idx + 1 - DC if not (layer == 1 and o == 0) else idx)
                for c in range(DC):
                    last = nc.tensor.matmul(psH[o][:, 0:n], wts[w][:, e, c, o * P:(o + 1) * P], src[:, c, 0:n], start=(c == 0), stop=(c == DC - 1))
                last.then_inc(hid_done, 1)

        def chunk(m, k, tiles, nodes, then):
            n = tiles * P

            def out(e):
                pe.wait_ge(hid_relu, ((m * NEXP + e) * 2 + 2) * DC)
                node_rows(m, 1 + e, tiles, lambda i, j: h2[:, e % 2, i, j * P:(j + 1) * P], [wts["ew3"][:, e, c, :] for c in range(DC)])

            hidden(m, k, 0, 0, n)
            pe.wait_ge(gT_ready, m + 1)
            node_rows(m, 0, tiles, lambda i, j: gateT[:, k, j * P:(j + 1) * P], [wts["eb3"][:]])
            hidden(m, k, 0, 1, n)
            if then:
                transpose_y(*then)
            for e in range(1, NEXP):
                hidden(m, k, e, 0, n)
                if then and e == 2:
                    router(*then)
                out(e - 1)
                if then and e == 2:
                    logits(*then)
                hidden(m, k, e, 1, n)
                if then and e == 1:
                    transpose_x2(*then)
                if then and e == 4:
                    transpose_gate(*then)
            out(NEXP - 1)

        def prologue(*x):
            for piece in (transpose_y, transpose_x2, router, logits, transpose_gate):
                piece(*x)
        in_order(pe, chunk, prologue)

    @block.vector
    def _(dve):
        c = Chain(dve, chain)
        batch_norm_scale(nc, c, dve, (var_ready, std_ready), wts["stats2"], norm, wts["g2"][:], wts["c2"][:])
        c.mark(nc.vector.memset(pr[:], -1.0))
        dve.wait_ge(iotas, 1)
        c.link(nc.vector.tensor_copy(iotaF[:], iotaI[:]))
        base = c.n
        NORM_LINKS = HALVES + 2 * MC + 1
        GATE_LINKS = 9 + 4 * MC
        LINKS = NORM_LINKS + GATE_LINKS

        def add_y(x, k, tiles, nodes):
            if later(x, 2):
                dve.wait_ge(yT_done, x - 1)
            for o in range(DC):
                last = nc.vector.tensor_scalar(y[:, k, o, 0:tiles * P], xnT[:, o, bass.ds(x * W, tiles * P)], norm["scale"][:, o:o + 1],
                                               norm["shift"][:, o:o + 1], ALU.mult, ALU.add)
            last.then_inc(y_ready, 1)

        def layer_norm(x, k, tiles, nodes):
            c.n = base + x * LINKS
            dve.wait_ge(yT_done, x + 1)
            for b in range(halves(tiles)):
                w = min(2, tiles - 2 * b)
                v = xN[:, bass.ds(x * MC + 2 * b, w), :].rearrange("p j d -> p (j d)")
                c.mark(nc.vector.tensor_tensor(v, v, psT[b][:, 0:w * D], ALU.add))
            c.join()
            apart(dve, passed)
            for j in range(tiles):
                c.mark(nc.vector.bn_stats(st[:, k, j, :], xN[:, bass.ds(x * MC + j, 1), :].rearrange("p a d -> p (a d)")))
            c.join()
            apart(dve, passed)
            for j in range(tiles):
                c.mark(nc.vector.bn_aggr(mv[:, k, j, :], st[:, k, j, :]))
            c.join()
            nc.vector.tensor_scalar(va[:, k, 0:tiles], mv[:, k, 0:tiles, 1], EPS, None, ALU.add).then_inc(lnvar_ready, 1)
            dve.wait_ge(lnstd_ready, x + 1)
            c.link(nc.vector.reciprocal(rs[:, k, 0:tiles], sdv[:, k, 0:tiles]))
            if later(x, 2):
                dve.wait_ge(x2T_done, x * DC - DC)
            for j in range(tiles):
                last = nc.vector.tensor_scalar(x2[:, k, j, :], xN[:, bass.ds(x * MC + j, 1), :].rearrange("p a d -> p (a d)"), mv[:, k, j, 0:1],
                                               rs[:, k, j:j + 1], ALU.subtract, ALU.mult)
            last.then_inc(x2_ready, 1)
            assert tiles < MC or not isinstance(x, int) or c.n == base + x * LINKS + NORM_LINKS

        def softmax(x, k, tiles, nodes):
            c.n = base + x * LINKS + (NORM_LINKS if tiles == MC else halves(tiles) + 2 * tiles + 1)
            dve.wait_ge(l_done, x + 1)
            L = lg[:, 0:tiles, 0:NEXP]
            r3 = bcast(red[:, 0:tiles].unsqueeze(2), [P, tiles, NEXP])
            c.link(nc.vector.tensor_tensor(L, psL[:, 0:tiles * 8].rearrange("p (j e) -> p j e", e=8)[:, :, 0:NEXP], bcast(wts["rb2"][:].unsqueeze(1), [P, tiles, NEXP]), ALU.add))
            c.link(nc.vector.tensor_reduce(red[:, 0:tiles], L, X, ALU.max))
            nc.vector.tensor_tensor(L, L, r3, ALU.subtract).then_inc(larg_ready, 1)
            dve.wait_ge(lexp_ready, x + 1)
            c.link(nc.vector.tensor_reduce(red[:, 0:tiles], le[:, 0:tiles, 0:NEXP], X, ALU.add))
            c.link(nc.vector.reciprocal(red[:, 0:tiles], red[:, 0:tiles]))
            c.link(nc.vector.tensor_tensor(pr[:, 0:tiles, 0:NEXP], le[:, 0:tiles, 0:NEXP], r3, ALU.mult))
            apart(dve, passed)
            for j in range(tiles):
                c.mark(nc.vector.max(top[:, j, :], pr[:, j, :]))
            c.join()
            apart(dve, passed)
            for j in range(tiles):
                c.mark(nc.vector.max_index(topi[:, j, :], top[:, j, :], pr[:, j, :]))
            c.join()
            nc.vector.tensor_tensor(dw[:, 0:tiles], top[:, 0:tiles, 1], top[:, 0:tiles, 0], ALU.subtract).then_inc(warg_ready, 1)
            c.mark(nc.vector.tensor_copy(topf[:, 0:tiles, 0:2], topi[:, 0:tiles, 0:2]))
            dve.wait_ge(wexp_ready, x + 1)
            c.link(nc.vector.tensor_scalar(w1[:, 0:tiles], ew[:, 0:tiles], 1.0, None, ALU.add))
            c.link(nc.vector.reciprocal(w0[:, 0:tiles], w1[:, 0:tiles]))
            for j in range(tiles):
                c.mark(nc.vector.tensor_scalar(gate[:, k, j, :], iotaF[:], topf[:, j, 0:1], w0[:, j:j + 1], ALU.is_equal, ALU.mult))
            c.join()
            c.link(nc.vector.tensor_tensor(w1[:, 0:tiles], ew[:, 0:tiles], w0[:, 0:tiles], ALU.mult))
            for j in range(tiles):
                c.mark(nc.vector.tensor_scalar(hit[:, j, :], iotaF[:], topf[:, j, 1:2], w1[:, j:j + 1], ALU.is_equal, ALU.mult))
            c.join()
            nc.vector.tensor_tensor(gate[:, k, 0:tiles, :], gate[:, k, 0:tiles, :], hit[:, 0:tiles, :], ALU.add).then_inc(gate_ready, 1)
            assert tiles < MC or not isinstance(x, int) or c.n == base + x * LINKS + LINKS, c.n

        def add_group(m, k, tiles, group):
            for b in range(halves(tiles)):
                seq = m * STORES * HALVES + group * halves(tiles) + b
                dve.wait_ge(e_done, seq + 1)
                if group == 0:
                    w = min(2, tiles - 2 * b)
                    x = xN[:, bass.ds(m * MC + 2 * b, w), :].rearrange("p j d -> p (j d)")
                    nc.vector.tensor_tensor(x, x, psE[b][:, 0:w * D], ALU.add).then_inc(e_added, 1)
                    continue
                dve.wait_ge(e_added, seq + 1 - halves(tiles))
                for j in range(2 * b, min(2 * b + 2, tiles)):
                    x = xN[:, bass.ds(m * MC + j, 1), :].rearrange("p a d -> p (a d)")
                    last = nc.vector.scalar_tensor_tensor(x, psE[b][:, (j % 2) * D:(j % 2 + 1) * D], gate[:, k, j, group - 1:group], x, ALU.mult, ALU.add)
                last.then_inc(e_added, 1)

        def chunk(m, k, tiles, nodes, then):
            if then:
                add_y(*then)
            dve.wait_ge(gate_ready, m + 1)
            for group in range(STORES):
                add_group(m, k, tiles, group)
                if then and group == 0:
                    layer_norm(*then)
                if then and group == 2:
                    softmax(*then)

        def prologue(*x):
            for piece in (add_y, layer_norm, softmax):
                piece(*x)
        in_order(dve, chunk, prologue)


def build(nc, io):
    with ExitStack() as ctx:
        a = Alloc(nc, ctx, "all")
        io["table"] = nc.dram_tensor("node_table", [NT * P, ROW], F32, kind="Internal").ap()
        io["carries"] = nc.dram_tensor("carries", [STEPS, AGG], F32, kind="Internal").ap()
        keep = dict(xnT=a.sb("xnT", [P, DC, NT * P]), sTab=a.sb("sTab", [P, NT + 1, HEADS]), ident=a.sb("ident", [P, P]))
        wts = dict(wo=a.sb("wo", [P, DC, D]), w1=a.sb("w1", [P, DC, FF]), w2=a.sb("w2", [P, FC, D]),
                   rw1=a.sb("rw1", [P, DC, RH]), rw2=a.sb("rw2", [RH, NEXP]), rb1=a.sb("rb1", [RH, 1]),
                   rb2=a.sb("rb2", [P, NEXP]), eb1=a.sb("eb1", [P, NEXP, DC]), eb2=a.sb("eb2", [P, NEXP, DC]),
                   eb3=a.sb("eb3", [NEXP, D]), b1=a.sb("b1", [P, FC]),
                   stats1=a.sb("stats1", [P, DC, CHUNKS, 6]), stats2=a.sb("stats2", [P, DC, CHUNKS, 6]),
                   **{n: a.sb(n, [P, DC]) for n in ("bo", "b2", "g1", "c1", "g2", "c2")})
        with ExitStack() as edges:
            b = Alloc(nc, edges, "edges")
            home = b.sb("home", [P, NT + 1, HOME])
            target = b.sb("target", [P, STEPS])
            with ExitStack() as steps:
                b = Alloc(nc, steps, "plan")
                plan = dict(srcI=b.sb("step_srcI", [P, STEPS], I32), windowI=b.sb("windowI", [1, STEPS], I32),
                            rel16=b.sb("rel16", [P, STEPS], BF16), relHome=b.sb("relHome", [P, STEPS]),
                            isLast=b.sb("isLast", [P, STEPS]), isCarry=b.sb("isCarry", [P, STEPS]), target=target,
                            edge=b.sb("edge", [P, BATCHES, P]), edgeBack=b.sb("edgeBack", [P, BATCHES, P]),
                            iota=b.sb("iota", [P, P]), iota16=b.sb("iota16", [P, P], BF16), eye=b.sb("eye", [P, SB, SB]))
                with ExitStack() as first:
                    b = Alloc(nc, first, "nodes")
                    nodes = dict(xN=b.sb("x_rows", [P, NT, D]), wqkv=b.sb("wqkv", [P, DC, 3 * D]), bias=b.sb("qkv_bias", [P, 3 * D]),
                                 meanvar=b.sb("meanvar", [P, NT, 2]), rstd=b.sb("rstd", [P, NT]))
                    with ExitStack() as phase:
                        plan_steps(nc, Alloc(nc, phase, "planning"), io, keep, plan, nodes)
                    with ExitStack() as phase:
                        project_nodes(nc, Alloc(nc, phase, "project"), io, keep, nodes)
                with ExitStack() as phase:
                    run_steps(nc, Alloc(nc, phase, "steps"), io, keep, plan, home, wts)
            with ExitStack() as phase:
                merge_attention(nc, Alloc(nc, phase, "merge"), io, keep, home, target, wts)
        with ExitStack() as dense:
            b = Alloc(nc, dense, "dense")
            wts |= {n: b.sb(n, [P, NEXP, DC, D]) for n in ("ew1", "ew2", "ew3")} | {"xN": b.sb("xN", [P, NT, D])}
            with ExitStack() as phase:
                feed_forward(nc, Alloc(nc, phase, "ffn"), io, keep, wts)
            with ExitStack() as phase:
                route_and_mix(nc, Alloc(nc, phase, "experts"), io, keep, wts)


_GNN = ["Wq", "bq", "Wk", "bk", "Wv", "bv", "Wo", "bo", "W1", "b1", "W2", "b2", "bn1_g", "bn1_b", "bn2_g", "bn2_b"]
_FFN = ["router_w1", "router_b1", "router_w2", "router_b2", "expert_w1", "expert_b1", "expert_w2", "expert_b2",
        "expert_w3", "expert_b3"]
_INS = {"x": "x", "src": "src", "dst": "dst"} | {f"L0_gnn_{n}": n for n in _GNN} | {f"L0_ffn_{n}": n for n in _FFN}


def kernel(**inputs):
    import numpy as _np
    import concourse.bacc as _bacc
    from concourse import mybir as _mybir
    from concourse.bass_utils import run_bass_kernel_spmd as _run

    nc = _bacc.Bacc("TRN2", target_bir_lowering=False, num_devices=1)
    arrays, io = {}, {}
    for name, short in _INS.items():
        a = _np.ascontiguousarray(inputs[name])
        arrays[f"in_{name}_dram"] = a
        io[short] = nc.dram_tensor(f"in_{name}_dram", a.shape, _mybir.dt.from_np(a.dtype), kind="ExternalInput").ap()
    io["out"] = nc.dram_tensor("out_0_dram", (N, D), _mybir.dt.float32, kind="ExternalOutput").ap()
    build(nc, io)
    r = _run(nc, [arrays], core_ids=[0])
    return r.results[0]["out_0_dram"]
```

```python
from contextlib import ExitStack

import concourse.bass as bass
from concourse import mybir

F32 = mybir.dt.float32
BF16 = mybir.dt.bfloat16
I32 = mybir.dt.int32
ALU = mybir.AluOpType
ACT = mybir.ActivationFunctionType
X = mybir.AxisListType.X

P = 128
N = 3125
D = 256
DC = D // P
HEADS = 8
HD = D // HEADS
E = 50000
NT = -(-N // P)
NTAIL = N - (NT - 1) * P
ET = -(-E // P)
ETAIL = E - (ET - 1) * P
SB = 16
BATCHES = -(-(ET + NT - 1) // SB)
STEPS = BATCHES * SB
TC = 98
TCH = -(-ET // TC)
TB = 4
CP = STEPS // 4
CCH = STEPS // CP
ROW = D + HEADS
AGG = ROW + 2 * HEADS
HOME = ROW + HEADS
G = 4
NG = SB // G
PARTS = 3
RING = 3
BANKS = 3
BIG = 1e30
FAR = 65536.0
EPS = 1e-5
NEG_SLOPE = 0.2
NC = 448
NCH = -(-N // NC)
NCT = N - (NCH - 1) * NC
FF = 512
FC = FF // P
NEXP = 6
RH = 128


def bcast(ap, shape):
    return ap.to_broadcast(shape)


def in_pairs(eng, n, body, peel=1):
    for j in range(min(2 * peel, n)):
        body(j, j % 2)
    if n // 2 > peel:
        with eng.Fori(peel, n // 2) as i:
            body(i * 2, 0)
            body(i * 2 + 1, 1)
    if n % 2 and n > 2 * peel:
        body(n - 1, 0)


class Alloc:

    def __init__(self, nc, ctx, phase):
        self.nc, self.ctx, self.phase = nc, ctx, phase

    def sb(self, name, shape, dt=F32):
        return self.ctx.enter_context(self.nc.sbuf_tensor(f"{self.phase}_{name}", shape, dt))

    def ps(self, name, shape, dt=F32):
        return self.ctx.enter_context(self.nc.psum_tensor(f"{self.phase}_{name}", shape, dt))

    def sem(self, name):
        return self.ctx.enter_context(self.nc.semaphore(f"{self.phase}_{name}"))


def apart(eng, passed):
    eng.sem_inc(passed, 1)


class Chain:

    def __init__(self, eng, sem):
        self.eng, self.sem, self.n = eng, sem, 0

    def link(self, ins):
        self.mark(ins)
        self.join()

    def mark(self, ins):
        ins.then_inc(self.sem, 1)
        self.n = self.n + 1

    def join(self):
        self.eng.wait_ge(self.sem, self.n)


def project_nodes(nc, a, io, keep, nodes):
    xnT, sTab, ident = keep["xnT"], keep["sTab"], keep["ident"]
    xN, wqkv, bias, meanvar, rstd = (nodes[n] for n in ("xN", "wqkv", "bias", "meanvar", "rstd"))
    xn = a.sb("xn", [P, 2, D])
    xnT_ring = a.sb("xnT_ring", [P, 2, D])
    qkv = a.sb("qkv", [P, 2, 3 * D + HEADS])
    qk = a.sb("qk", [P, 2, D])
    offset = a.sb("offset", [P, NT])
    psT = [a.ps(f"psT{i}", [P, 512]) for i in range(2)]
    psQKV = [a.ps(f"psQKV{i}", [P, 1024]) for i in range(2)]

    chain = a.sem("dve_chain")
    xn_ready = a.sem("xn_ready")
    xnT_done = a.sem("xnT_transposed")
    xnT_ready = a.sem("xnT_ready")
    xnT_kept = a.sem("xnT_kept")
    offset_ready = a.sem("offset_ready")
    s_kept = a.sem("s_kept")
    act_passed = a.sem("act_passed")
    go = a.sem("pool_passed")
    qkv_done = a.sem("qkv_product")
    row_ready = a.sem("row_ready")
    row_out = [a.sem(f"row_out{i}") for i in range(2)]

    block = a.ctx.enter_context(nc.Block())

    @block.sync
    def _(sp):
        def store_row(j, k):
            sp.wait_ge(row_ready, j + 1)
            sp.dma_start(io["table"][bass.ds(j * P, P), :], qkv[:, k, 2 * D:]).then_inc(row_out[k], 16)

        in_pairs(sp, NT, store_row)
        sp.wait_ge(row_out[0], 16 * ((NT + 1) // 2))
        sp.wait_ge(row_out[1], 16 * (NT // 2))

    @block.gpsimd
    def _(pool):
        def keep_xnT(j, k):
            pool.wait_ge(xnT_ready, j + 1)
            apart(pool, go)
            nc.gpsimd.tensor_copy(xnT[:, :, bass.ds(j * P, P)],
                                  xnT_ring[:, k, :].rearrange("p (c n) -> p c n", c=DC)).then_inc(xnT_kept, 1)

        in_pairs(pool, NT, keep_xnT)

    @block.scalar
    def _(act):
        def normalize(j, k):
            if not isinstance(j, int) or j >= 2:
                act.wait_ge(xnT_done, j - 1)
                apart(act, act_passed)
            row = bass.ds(j, 1)
            nc.scalar.activation(xn[:, k, :], xN[:, row, :].rearrange("p a d -> p (a d)"), ACT.Identity,
                                 bias=offset[:, row], scale=rstd[:, row]).then_inc(xn_ready, 1)

        def evacuate(j, k):
            act.wait_ge(xnT_done, j + 1)
            if not isinstance(j, int) or j >= 2:
                act.wait_ge(xnT_kept, j - 1)
                act.wait_ge(qkv_done, j - 1)
            nc.scalar.copy(xnT_ring[:, k, :], psT[k][:, 0:D]).then_inc(xnT_ready, 1)

        def keep_s(j, k):
            act.wait_ge(row_ready, j + 1)
            apart(act, act_passed)
            nc.scalar.copy(sTab[:, bass.ds(j, 1), :].rearrange("p a h -> p (a h)"), qkv[:, k, 3 * D:]).then_inc(s_kept, 1)

        def step(j, k):
            evacuate(j, k)
            normalize(j + 2, k)
            keep_s(j - 2, k)
        act.wait_ge(offset_ready, 1)
        normalize(0, 0)
        normalize(1, 1)
        for j in range(2):
            evacuate(j, j)
            normalize(j + 2, j)
        with act.Fori(1, (NT - 3) // 2) as i:
            step(i * 2, 0)
            step(i * 2 + 1, 1)
        for j in range((NT - 3) // 2 * 2, NT - 2):
            step(j, j % 2)
        for j in (NT - 2, NT - 1):
            evacuate(j, j % 2)
            keep_s(j - 2, j % 2)
        for j in (NT - 2, NT - 1):
            keep_s(j, j % 2)

    @block.vector
    def _(dve):
        c = Chain(dve, chain)
        c.link(nc.vector.tensor_tensor(offset[:], meanvar[:, :, 0], rstd[:], ALU.mult))
        nc.vector.tensor_scalar(offset[:], offset[:], -1.0, None, ALU.mult).then_inc(offset_ready, 1)
        c.mark(nc.vector.memset(sTab[:, NT, :], 0.0))
        base = c.n

        def heads(j, k):
            c.n = base + 2 * j
            dve.wait_ge(qkv_done, j + 1)
            if not isinstance(j, int) or j >= 2:
                dve.wait_ge(row_out[k], (j - k) * 8)
                dve.wait_ge(s_kept, j - 1)
            c.link(nc.vector.tensor_tensor(qkv[:, k, 0:3 * D], psQKV[k][:, 0:3 * D], bias[:], ALU.add))
            c.link(nc.vector.scalar_tensor_tensor(qk[:, k, :], qkv[:, k, 0:D], float(HD) ** -0.5, qkv[:, k, D:2 * D], ALU.mult, ALU.mult))
            nc.vector.tensor_reduce(qkv[:, k, 3 * D:], qk[:, k, :].rearrange("p (h c) -> p h c", h=HEADS), X, ALU.add).then_inc(row_ready, 1)

        in_pairs(dve, NT, heads)

    @block.tensor
    def _(pe):
        def transpose(j, k):
            pe.wait_ge(xn_ready, j + 1)
            if not isinstance(j, int) or j >= 2:
                pe.wait_ge(xnT_ready, j - 1)
            for c in range(DC):
                last = nc.tensor.transpose(psT[k][:, c * P:(c + 1) * P], xn[:, k, c * P:(c + 1) * P], ident[:])
            last.then_inc(xnT_done, 1)

        def product(j, k):
            pe.wait_ge(xnT_ready, j + 1)
            if not isinstance(j, int) or j >= 2:
                pe.wait_ge(row_ready, j - 1)
            for lo, hi in ((0, 512), (512, 768)):
                for c in range(DC):
                    last = nc.tensor.matmul(psQKV[k][:, lo:hi], xnT_ring[:, k, c * P:(c + 1) * P],
                                            wqkv[:, c, lo:hi], start=(c == 0), stop=(c == DC - 1))
            last.then_inc(qkv_done, 1)

        transpose(0, 0)
        def step(j, k):
            if not isinstance(j, int) or j + 1 < NT:
                transpose(j + 1, 1 - k)
            product(j, k)
        in_pairs(pe, NT, step)


def plan_steps(nc, a, io, keep, plan, nodes, home):
    ident = keep["ident"]
    xN, wqkv, bias, meanvar, rstd = (nodes[n] for n in ("xN", "wqkv", "bias", "meanvar", "rstd"))
    xstats = a.sb("x_stats", [P, NT, 6])
    xvar = a.sb("x_var", [P, NT])
    xstd = a.sb("x_std", [P, NT])
    srcI = a.sb("srcI", [TC, TCH, P], I32)
    dstI = a.sb("dstI", [TC, TCH, P], I32)
    srcF = a.sb("srcF", [TC, TCH, P])
    dstF = a.sb("dstF", [TC, TCH, P + 1])
    prevI = a.sb("prevI", [TC, TCH], I32)
    prevF = a.sb("prevF", [TC, TCH])
    prevB = a.sb("prevB", [TC, TCH, P])
    firstB = a.sb("firstB", [TC, TCH, P])
    tileI = a.sb("tileI", [TC, TCH], I32)
    tileF = a.sb("tileF", [TC, TCH])
    firstKey = a.sb("firstKey", [TC, TCH])
    stepI = a.sb("stepI", [P, STEPS], I32)
    stepF = a.sb("stepF", [P, STEPS])
    bound = a.sb("bound", [P, STEPS])
    started = a.sb("started", [TC, TCH, STEPS], BF16)
    ones = a.sb("ones", [TC, P], BF16)
    tp = a.sb("tile_of_step", [P, STEPS])
    wp = a.sb("window_of_step", [P, STEPS])
    wp128 = a.sb("window_start", [P, STEPS])
    sel = a.sb("sel", [TC, TCH, STEPS])
    dst = plan["dst"]
    prev = a.sb("prev_of_step", [P, STEPS])
    rel = a.sb("rel", [P, STEPS])
    t1 = a.sb("t1", [P, STEPS])
    t2 = a.sb("t2", [P, STEPS])
    iotaI = a.sb("iotaI", [P, P], I32)
    psCount = a.ps("psCount", [P, 512])
    psSel = [a.ps(f"psSel{i}", [P, 512]) for i in range(5)]

    x_pad = a.sem("x_pad")
    x_in = a.sem("x_in")
    w_in = a.sem("w_in")
    ident0 = a.sem("ident0")
    var_ready = a.sem("var_ready")
    std_ready = a.sem("std_ready")
    pads = a.sem("pads")
    idx_in = a.sem("idx_in")
    iotas = a.sem("iotas")
    chain = a.sem("chain")
    key_ready = a.sem("key_ready")
    counted = a.sem("counted")
    sel_ready = a.sem("sel_ready")
    selected = a.sem("selected")

    block = a.ctx.enter_context(nc.Block())
    LASTP = ET - 1 - (TCH - 1) * TC

    @block.sync
    def _(sp):
        sp.wait_ge(pads, 3)
        for name, t in (("src", srcI), ("dst", dstI)):
            full = (TCH - 1) * TC * P
            sp.dma_start(t[:, 0:TCH - 1, :], io[name][0:full].rearrange("(c t e) -> t c e", c=TCH - 1, e=P)).then_inc(idx_in, 16)
            sp.dma_start(t[0:LASTP, TCH - 1, :], io[name][full:full + LASTP * P].rearrange("(t e) -> t e", e=P)).then_inc(idx_in, 16)
            sp.dma_start(t[LASTP:LASTP + 1, TCH - 1, 0:ETAIL], io[name][full + LASTP * P:E].rearrange("(t e) -> t e", t=1)).then_inc(idx_in, 16)
        ends = io["dst"][0:(ET - 1) * P].rearrange("(t e) -> t e", e=P)[:, P - 1:P]
        with nc.allow_non_contiguous_dma(reason="one element of each tile"):
            for c in range(TCH):
                lo, hi = max(1, c * TC), min(ET, (c + 1) * TC)
                sp.dma_start(prevI[lo - c * TC:hi - c * TC, c:c + 1], ends[lo - 1:hi - 1, :]).then_inc(idx_in, 16)
        sp.dma_start(xN[:, 0:NT - 1, :], io["x"][0:(NT - 1) * P, :].rearrange("(j p) d -> p j d", p=P)).then_inc(x_in, 16)
        sp.wait_ge(x_pad, 1)
        sp.dma_start(xN[0:NTAIL, NT - 1, :], io["x"][(NT - 1) * P:N, :]).then_inc(x_in, 16)
        for n, w in enumerate(("Wq", "Wk", "Wv")):
            sp.dma_start(wqkv[:, :, n * D:(n + 1) * D], io[w].rearrange("(c p) n -> p c n", p=P)).then_inc(w_in, 16)
        for n, b in enumerate(("bq", "bk", "bv")):
            sp.dma_start(bias[:, n * D:(n + 1) * D], io[b].partition_broadcast(P)).then_inc(w_in, 16)
        sp.wait_ge(w_in, 96)

    @block.gpsimd
    def _(pool):
        nc.gpsimd.iota(tileI[:], pattern=[[TC, TCH]], base=0, channel_multiplier=1).then_inc(iotas, 1)
        nc.gpsimd.iota(stepI[:], pattern=[[1, STEPS]], base=0, channel_multiplier=0).then_inc(iotas, 1)
        nc.gpsimd.iota(iotaI[:], pattern=[[1, P]], base=0, channel_multiplier=0).then_inc(iotas, 1)
        nc.gpsimd.memset(ident[:], 0.0).then_inc(ident0, 1)
        nc.gpsimd.memset(home[:], 0.0)
        pool.wait_ge(ident0, 1)
        nc.gpsimd.affine_select(out=ident[:], in_=ident[:], compare_op=ALU.not_equal, fill=1.0, base=0,
                                pattern=[[-1, P]], channel_multiplier=1)

    @block.scalar
    def _(act):
        act.wait_ge(var_ready, 1)
        nc.scalar.activation(xstd[:], xvar[:], ACT.Sqrt).then_inc(std_ready, 1)

    @block.vector
    def _(dve):
        c = Chain(dve, chain)
        nc.vector.memset(xN[:, NT - 1, :], 0.0).then_inc(x_pad, 1)
        nc.vector.memset(srcI[:], 0).then_inc(pads, 1)
        nc.vector.memset(dstI[:], int(FAR)).then_inc(pads, 1)
        nc.vector.memset(prevI[:], -1).then_inc(pads, 1)
        c.mark(nc.vector.memset(ones[:], 1.0))
        c.mark(nc.vector.memset(dstF[:, :, P:P + 1], -5.0))
        c.mark(nc.vector.memset(plan["edge"][:, :, 0:1], -BIG))
        c.mark(nc.vector.memset(plan["edgeBack"][:, :, 0:1], -BIG))
        dve.wait_ge(iotas, 3)
        c.mark(nc.vector.tensor_copy(tileF[:], tileI[:]))
        c.mark(nc.vector.tensor_copy(stepF[:], stepI[:]))
        c.mark(nc.vector.tensor_copy(plan["iota16"][:], iotaI[:]))
        c.join()
        c.mark(nc.vector.tensor_scalar(bound[:], stepF[:], float(P), float(P), ALU.mult, ALU.add))
        dve.wait_ge(idx_in, 160)
        c.mark(nc.vector.tensor_copy(srcF[:], srcI[:]))
        c.mark(nc.vector.tensor_copy(prevF[:], prevI[:]))
        c.link(nc.vector.tensor_copy(dstF[:, :, 0:P], dstI[:]))
        c.mark(nc.vector.tensor_copy(prevB[:], bcast(prevF[:].unsqueeze(2), [TC, TCH, P])))
        c.mark(nc.vector.tensor_copy(firstB[:], bcast(dstF[:, :, 0:1], [TC, TCH, P])))
        c.link(nc.vector.scalar_tensor_tensor(firstKey[:], tileF[:], float(P), dstF[:, :, 0], ALU.mult, ALU.add))
        for k in range(TCH):
            nc.vector.tensor_scalar(started[:, k, :], bound[0:TC, :], firstKey[:, k:k + 1], None, ALU.is_gt).then_inc(key_ready, 1)
        dve.wait_ge(counted, 1)
        c.link(nc.vector.tensor_scalar(tp[:], psCount[:, 0:STEPS], -1.0, 0.0, ALU.add, ALU.max))
        for k in range(TCH):
            c.mark(nc.vector.tensor_scalar(sel[:, k, :], tp[0:TC, :], tileF[:, k:k + 1], None, ALU.is_equal))
        c.join()
        nc.vector.tensor_tensor(wp[:], stepF[:], tp[:], ALU.subtract).then_inc(sel_ready, 1)
        dve.wait_ge(sel_ready, 1)
        c.mark(nc.vector.tensor_copy(plan["windowI"][:], wp[0:1, :]))
        c.mark(nc.vector.tensor_scalar(wp128[:], wp[:], float(P), None, ALU.mult))
        dve.wait_ge(x_in, 32)
        for j in range(NT):
            c.mark(nc.vector.bn_stats(xstats[:, j, :], xN[:, j, :]))
        c.join()
        for j in range(NT):
            c.mark(nc.vector.bn_aggr(meanvar[:, j, :], xstats[:, j, :]))
        c.join()
        nc.vector.tensor_scalar(xvar[:], meanvar[:, :, 1], EPS, None, ALU.add).then_inc(var_ready, 1)
        dve.wait_ge(selected, 1)
        c.link(nc.vector.tensor_copy(dst[:], psSel[0][:, 0:STEPS]))
        c.link(nc.vector.tensor_tensor(rel[:], dst[:], wp128[:], ALU.subtract))
        c.mark(nc.vector.tensor_copy(plan["rel16"][:], rel[:]))
        dve.wait_ge(selected, 2)
        c.link(nc.vector.tensor_copy(prev[:], psSel[1][:, 0:STEPS]))
        c.link(nc.vector.tensor_tensor(t1[:], dst[:], prev[:], ALU.is_equal))
        c.link(nc.vector.scalar_tensor_tensor(t2[:], rel[:], 0.0, t1[:], ALU.is_ge, ALU.mult))
        c.mark(nc.vector.tensor_scalar(plan["notCarry"][:], t1[:], -1.0, 1.0, ALU.mult, ALU.add))
        c.link(nc.vector.scalar_tensor_tensor(plan["isCarry"][:], rel[:], float(P), t2[:], ALU.is_lt, ALU.mult))
        dve.wait_ge(selected, 3)
        c.mark(nc.vector.tensor_tensor(t1[:], prev[:], psSel[2][:, 0:STEPS], ALU.is_equal))
        c.link(nc.vector.tensor_tensor(rel[:], prev[:], wp128[:], ALU.subtract))
        c.link(nc.vector.scalar_tensor_tensor(t2[:], rel[:], 0.0, t1[:], ALU.is_ge, ALU.mult))
        c.link(nc.vector.scalar_tensor_tensor(t1[:], rel[:], float(P), t2[:], ALU.is_lt, ALU.mult))
        c.link(nc.vector.scalar_tensor_tensor(t2[:], prev[:], 1.0, t1[:], ALU.add, ALU.mult))
        c.mark(nc.vector.tensor_scalar(plan["target"][:], t2[:], -1.0, None, ALU.add))
        dve.wait_ge(selected, 4)
        c.mark(nc.vector.tensor_tensor(plan["isLast"][:], dst[:], psSel[3][:, 0:STEPS], ALU.not_equal))
        dve.wait_ge(selected, 5)
        c.mark(nc.vector.tensor_copy(plan["srcI"][:], psSel[4][:, 0:STEPS]))
        dve.wait_ge(std_ready, 1)
        nc.vector.reciprocal(rstd[:], xstd[:])

    @block.tensor
    def _(pe):
        pe.wait_ge(key_ready, TCH)
        for k in range(TCH):
            last = nc.tensor.matmul(psCount[:, 0:STEPS], ones[:], started[:, k, :], start=(k == 0), stop=(k == TCH - 1))
        last.then_inc(counted, 1)
        pe.wait_ge(sel_ready, 1)
        for n, rows in enumerate((dstF[:, :, 0:P], prevB[:], firstB[:], dstF[:, :, 1:P + 1], srcF[:])):
            for k in range(TCH):
                last = nc.tensor.matmul(psSel[n][:, 0:STEPS], rows[:, k, :], sel[:, k, :], start=(k == 0), stop=(k == TCH - 1))
            last.then_inc(selected, 1)


def load_dense_weights(nc, sp, sem, io, wts):
    for name, key in (("Wo", "wo"), ("W1", "w1"), ("W2", "w2"), ("router_w1", "rw1")):
        sp.dma_start(wts[key][:], io[name].rearrange("(c p) n -> p c n", p=P)).then_inc(sem, 16)
    sp.dma_start(wts["rw2"][:], io["router_w2"]).then_inc(sem, 16)
    sp.dma_start(wts["rb2"][:], io["router_b2"].partition_broadcast(P)).then_inc(sem, 16)
    sp.dma_start(wts["eb3"][:], io["expert_b3"].partition_broadcast(P)).then_inc(sem, 16)
    with nc.allow_non_contiguous_dma(reason="columns of biases"):
        for name, key in (("bo", "bo"), ("b1", "b1"), ("b2", "b2"), ("bn1_g", "g1"), ("bn1_b", "c1"), ("bn2_g", "g2"), ("bn2_b", "c2")):
            sp.dma_start(wts[key][:], io[name].rearrange("(c p) -> p c", p=P)).then_inc(sem, 16)
        sp.dma_start(wts["rb1"][:], io["router_b1"].rearrange("(p c) -> p c", c=1)).then_inc(sem, 16)
        for name, key in (("expert_b1", "eb1"), ("expert_b2", "eb2")):
            for e in range(NEXP):
                sp.dma_start(wts[key][:, e, :], io[name][e, :].rearrange("(c p) -> p c", p=P)).then_inc(sem, 16)


def run_steps(nc, a, io, keep, plan, home, wts):
    ident, sTab = keep["ident"], keep["sTab"]
    rows = [a.sb(f"rows{i}", [P, SB, AGG]) for i in range(RING)]
    srcS = a.sb("src_slots", [P, RING, SB], I32)
    hot16 = a.sb("hot16", [P, RING, NG, G, P], BF16)
    mask = a.sb("batch_mask", [P, SB])
    hotT = a.sb("hotT", [P, 2, G, P], BF16)
    sParts = a.sb("s_parts", [P, NT + 1, PARTS, HEADS], BF16)
    sRest = a.sb("s_rest", [P, NT + 1, HEADS])
    hotHome = a.sb("hotHome", [P, 2, G, P])
    carryEye = a.sb("carryEye", [P, RING, SB, SB])
    ss = a.sb("ss", [P, SB, HEADS])
    ssT = a.sb("ssT", [P, P])
    sd = a.sb("sd", [P, SB, HEADS])
    fwd = a.sb("fwd", [P, P])
    bwd = a.sb("bwd", [P, P])
    runT = a.sb("runT", [P, P])
    al = a.sb("al", [P, SB, HEADS])
    am = a.sb("am", [P, SB, HEADS])
    at = a.sb("at", [P, SB, HEADS])
    ar = a.sb("ar", [P, SB, HEADS])
    carrySb = a.sb("carrySb", [SB, RING, AGG])
    ident16 = a.sb("ident16", [P, P], BF16)
    dst = plan["dst"]
    dstB = a.sb("dst_over_heads", [P, 2, TB, SB, HEADS])
    dstTs = a.sb("dst_T", [P, 2, TB, P])
    differs = a.sb("differs", [P, 2, TB, P])

    psHot = [a.ps(f"psHot{i}", [P, G, P], BF16) for i in range(2)]
    psS = a.ps("psS", [P, P])
    psM = psS[:].rearrange("p (s h) -> p s h", h=HEADS)
    psD = a.ps("psD", [P, SB, PARTS * HEADS])
    psHome = [a.ps(f"psHome{i}", [P, 512]) for i in range(BANKS)]
    psCarry = a.ps("psCarry", [P, 512])
    psDT = [psHome[i][:].rearrange("p (b e) -> p b e", e=P) for i in range(2)]

    dstB_ready = a.sem("dstB_ready")
    dT_done = a.sem("dT_done")
    dT_copied = a.sem("dT_copied")
    differs_ready = a.sem("differs_ready")
    edge_ready = a.sem("edge_ready")
    gathered = [[a.sem(f"gathered{i}_{g}") for g in range(NG)] for i in range(RING)]
    weights_in = a.sem("weights_in")
    slots_ready = a.sem("slots_ready")
    go = a.sem("pool_passed")
    start = a.sem("start")
    masks_ready = a.sem("masks_ready")
    act_passed = a.sem("act_passed")
    home_hot_ready = a.sem("home_hot_ready")
    hot_ready = a.sem("hot_ready")
    hotT_done = a.sem("hotT_done")
    hotT_ready = a.sem("hotT_ready")
    sd_done = a.sem("sd_done")
    sd_ready = a.sem("sd_ready")
    ss_ready = a.sem("ss_ready")
    ssT_done = a.sem("ssT_done")
    ssT_ready = a.sem("ssT_ready")
    runT_ready = a.sem("runT_ready")
    run_done = a.sem("run_done")
    arg_ready = a.sem("arg_ready")
    exp_ready = a.sem("exp_ready")
    eye_ready = a.sem("eye_ready")
    msg_ready = a.sem("msg_ready")
    home_done = a.sem("home_done")
    agg_done = a.sem("agg_done")
    home_added = a.sem("home_added")
    carry_copied = a.sem("carry_copied")
    carry_out = [a.sem(f"carry_out{i}") for i in range(RING)]
    chain = a.sem("dve_chain")

    block = a.ctx.enter_context(nc.Block())

    def past(b, first=1):
        return not isinstance(b, int) or b >= first

    def more(b, n):
        return not isinstance(b, int) or b + n < BATCHES

    def in_rounds(eng, body):
        for b in range(RING):
            body(b, b % RING, b // RING)
        with eng.Fori(1, BATCHES // RING) as i:
            for k in range(RING):
                body(i * RING + k, k, i)
        for b in range(BATCHES // RING * RING, BATCHES):
            body(b, b % RING, b // RING)

    def windows(engine, b, g):
        _, w = nc.values_load_multi_w_load_instructions(
            plan["windowI"][0:1, bass.ds(b * SB + g * G, G)], engines=[engine], min_val=0, max_val=NT,
            skip_runtime_bounds_check_because="a step minus its tile is a window")
        return w

    @block.gpsimd
    def _(pool):
        def batch(b, k, r):
            if past(b, RING):
                pool.wait_ge(agg_done, b * SB - RING * SB + G)
                apart(pool, go)
            nc.gpsimd.tensor_copy(srcS[:, k, :], plan["srcI"][:, bass.ds(b * SB, SB)]).then_inc(slots_ready, 1)
            pool.wait_ge(slots_ready, b + 1)
            apart(pool, go)
            for s in range(SB):
                if past(b, RING) and s and s % G == 0:
                    pool.wait_ge(agg_done, b * SB - RING * SB + s + G)
                    apart(pool, go)
                pool.indirect_dma_start(rows[k][:, s, 0:ROW], None, io["table"],
                                        bass.IndirectOffsetOnAxis(srcS[:, k, s:s + 1], 0)).then_inc(gathered[k][s // G], 16)
        in_rounds(pool, batch)

    @block.sync
    def _(sp):
        load_dense_weights(nc, sp, weights_in, io, wts)

        def store_carry(b, k, r):
            sp.wait_ge(carry_copied, b + 1)
            sp.dma_start(io["carries"][bass.ds(b * SB, SB), :], carrySb[:, k, :]).then_inc(carry_out[k], 16)
        in_rounds(sp, store_carry)
        for k in range(RING):
            sp.wait_ge(carry_out[k], 16 * len(range(k, BATCHES, RING)))
        sp.wait_ge(weights_in, 16 * (15 + 2 * NEXP))

    groups = [range(b, min(b + TB, BATCHES)) for b in range(0, BATCHES, TB)]

    def spread_heads(g):
        k, n = g % 2, len(groups[g])
        cols = dst[:, groups[g][0] * SB:(groups[g][-1] + 1) * SB].rearrange("p (b s) -> p b s", s=SB)
        nc.scalar.copy(dstB[:, k, 0:n, :, :], bcast(cols.unsqueeze(3), [P, n, SB, HEADS])).then_inc(dstB_ready, 1)

    def run_edges(act):
        spread_heads(0)
        spread_heads(1)
        for g, members in enumerate(groups):
            k, n = g % 2, len(members)
            act.wait_ge(dT_done, g + 1)
            if g >= 2:
                act.wait_ge(differs_ready, g - 1)
            nc.scalar.copy(dstTs[:, k, 0:n, :], psDT[k][:, 0:n, :]).then_inc(dT_copied, 1)
            if g + 2 < len(groups):
                spread_heads(g + 2)
            act.wait_ge(differs_ready, g + 1)
            nc.scalar.activation(plan["edgeBack"][:, members[0]:members[-1] + 1, P - 1:0:-1], differs[:, k, 0:n, 0:P - 1],
                                 ACT.Copy, scale=-BIG).then_inc(edge_ready, 1)

    @block.scalar
    def _(act):
        def copy_scores(x, k, r):
            for g in range(NG):
                act.wait_ge(gathered[k][g], r * (16 * G) + 16 * G)
            if past(x):
                act.wait_ge(arg_ready, x)
            nc.scalar.copy(ss[:], rows[k][:, :, D:ROW]).then_inc(ss_ready, 1)

        def copy_scores_T(x):
            act.wait_ge(ssT_done, x + 1)
            nc.scalar.copy(ssT[:], psS[:]).then_inc(ssT_ready, 1)

        def copy_hot(x, g):
            act.wait_ge(hotT_done, x * NG + g + 1)
            if past(x) or g >= 2:
                act.wait_ge(sd_done, x * NG + g - 1)
            nc.scalar.copy(hotT[:, g % 2, :, :], psHot[g % 2][:]).then_inc(hotT_ready, 1)

        def exponent(x, k):
            act.wait_ge(arg_ready, x + 1)
            nc.scalar.activation(rows[k][:, :, D:ROW], ar[:], ACT.Exp).then_inc(exp_ready, 1)

        def batch_masks(x, k):
            if past(x):
                act.wait_ge(home_hot_ready, x * NG)
            apart(act, act_passed)
            nc.scalar.copy(mask[:], plan["notCarry"][:, bass.ds(x * SB, SB)]).then_inc(masks_ready, 1)
            nc.scalar.copy(carryEye[:, k, :, :].rearrange("p a c -> p (a c)")[:, ::SB + 1],
                           plan["isCarry"][:, bass.ds(x * SB, SB)]).then_inc(eye_ready, 1)

        def home_hot(b, k, g):
            if past(b) or g >= 2:
                act.wait_ge(agg_done, b * SB + g * G - G)
            act.wait_ge(masks_ready, b + 1)
            act.wait_ge(hot_ready, b * NG + g + 1)
            for s in range(G):
                last = nc.scalar.activation(hotHome[:, g % 2, s, :], hot16[:, k, g, s, :], ACT.Copy, scale=mask[:, g * G + s:g * G + s + 1])
            last.then_inc(home_hot_ready, 1)

        def batch(b, k, r):
            x, kx = b + 1, (k + 1) % RING
            home_hot(b, k, 1)
            if more(b, 1):
                copy_hot(x, 0)
                copy_hot(x, 1)
                copy_scores(x, kx, r + (k + 1) // RING)
                copy_scores_T(x)
            home_hot(b, k, 2)
            if more(b, 1):
                copy_hot(x, 2)
                copy_hot(x, 3)
            home_hot(b, k, 3)
            if more(b, 1):
                exponent(x, kx)
                batch_masks(x, kx)
                home_hot(x, kx, 0)
            act.wait_ge(agg_done, b * SB + SB)
            if past(b, RING):
                act.wait_ge(carry_out[k], r * 16)
            nc.scalar.copy(carrySb[:, k, :], psCarry[0:SB, 0:AGG]).then_inc(carry_copied, 1)
        run_edges(act)
        for g in range(NG):
            copy_hot(0, g)
        copy_scores(0, 0, 0)
        copy_scores_T(0)
        exponent(0, 0)
        act.wait_ge(start, 3)
        batch_masks(0, 0)
        home_hot(0, 0, 0)
        in_rounds(act, batch)

    LINKS = 8

    @block.vector
    def _(dve):
        c = Chain(dve, chain)
        nc.vector.tensor_copy(ident16[:], ident[:]).then_inc(start, 1)
        c.link(nc.vector.tensor_copy(sParts[:, :, 0, :], sTab[:]))
        c.link(nc.vector.tensor_tensor(sRest[:], sTab[:], sParts[:, :, 0, :], ALU.subtract))
        c.link(nc.vector.tensor_copy(sParts[:, :, 1, :], sRest[:]))
        c.link(nc.vector.tensor_tensor(sRest[:], sRest[:], sParts[:, :, 1, :], ALU.subtract))
        nc.vector.tensor_copy(sParts[:, :, 2, :], sRest[:]).then_inc(start, 1)
        nc.vector.memset(carryEye[:], 0.0).then_inc(start, 1)
        for g, members in enumerate(groups):
            k, n = g % 2, len(members)
            dve.wait_ge(dT_copied, g + 1)
            if g >= 2:
                dve.wait_ge(edge_ready, g - 1)
                c.join()
            nc.vector.tensor_tensor(differs[:, k, 0:n, 0:P - 1], dstTs[:, k, 0:n, 1:P], dstTs[:, k, 0:n, 0:P - 1], ALU.not_equal).then_inc(differs_ready, 1)
            dve.wait_ge(differs_ready, g + 1)
            c.mark(nc.vector.tensor_scalar(plan["edge"][:, members[0]:members[-1] + 1, 1:P], differs[:, k, 0:n, 0:P - 1], -BIG, None, ALU.mult))
        dve.wait_ge(edge_ready, len(groups))
        c.join()
        base = c.n

        def add_home(b, k, s, w):
            n = b * SB + s
            dve.wait_ge(home_done, n + 1)
            if past(b) or s:
                dve.wait_ge(home_added, n)
            h = home[:, bass.ds(w, 1), :].rearrange("p a d -> p (a d)")
            nc.vector.tensor_tensor(h, h, psHome[(k * SB + s) % BANKS][:, 0:HOME], ALU.add).then_inc(home_added, 1)

        def one_hot(x, k, g):
            nc.vector.tensor_tensor(hot16[:, k, g, :, :], bcast(plan["iota16"][:].unsqueeze(1), [P, G, P]),
                                    bcast(plan["rel16"][:, bass.ds(x * SB + g * G, G)].unsqueeze(2), [P, G, P]),
                                    ALU.is_equal).then_inc(hot_ready, 1)

        def run_maxima(x):
            c.n = base + x * LINKS
            dve.wait_ge(ssT_ready, x + 1)
            edge = plan["edge"][:, bass.ds(x, 1), :].rearrange("p a e -> p (a e)")
            back = plan["edgeBack"][:, bass.ds(x, 1), :].rearrange("p a e -> p (a e)")
            c.mark(nc.vector.tensor_tensor_scan(fwd[:], edge, ssT[:], -BIG, ALU.add, ALU.max))
            c.link(nc.vector.tensor_tensor_scan(bwd[:, ::-1], back, ssT[:, ::-1], -BIG, ALU.add, ALU.max))
            if past(x):
                dve.wait_ge(run_done, x)
            nc.vector.tensor_tensor(runT[:], fwd[:], bwd[:], ALU.max).then_inc(runT_ready, 1)

        def dst_scores(x):
            dve.wait_ge(sd_done, x * NG + NG)
            nc.vector.tensor_reduce(sd[:], psD[:].rearrange("p s (t h) -> p s h t", t=PARTS), X, ALU.add).then_inc(sd_ready, 1)

        def edge_scores(x):
            c.n = base + x * LINKS + 2
            dve.wait_ge(sd_ready, x + 1)
            dve.wait_ge(ss_ready, x + 1)
            if past(x):
                dve.wait_ge(exp_ready, x)
            c.mark(nc.vector.tensor_tensor(at[:], ss[:], sd[:], ALU.add))
            dve.wait_ge(run_done, x + 1)
            c.mark(nc.vector.tensor_tensor(am[:], psM, sd[:], ALU.add))

        def leaky_scores(x, k):
            c.n = base + x * LINKS + 4
            c.join()
            c.mark(nc.vector.scalar_tensor_tensor(al[:], at[:], NEG_SLOPE, at[:], ALU.mult, ALU.max))
            c.mark(nc.vector.scalar_tensor_tensor(am[:], am[:], NEG_SLOPE, am[:], ALU.mult, ALU.max))
            last = bcast(plan["isLast"][:, bass.ds(x * SB, SB)].unsqueeze(2), [P, SB, HEADS])
            c.mark(nc.vector.tensor_tensor(rows[k][:, :, ROW:ROW + HEADS], psM, last, ALU.mult))
            c.mark(nc.vector.tensor_tensor(rows[k][:, :, ROW + HEADS:], sd[:], last, ALU.mult))

        def exponents(x):
            c.n = base + x * LINKS + 8
            c.join()
            nc.vector.tensor_tensor(ar[:], al[:], am[:], ALU.subtract).then_inc(arg_ready, 1)

        def messages(b, k, g):
            if g == 0:
                dve.wait_ge(exp_ready, b + 1)
            v = rows[k][:, g * G:g * G + G, 0:D].rearrange("p s (h c) -> p s h c", h=HEADS)
            ex = bcast(rows[k][:, g * G:g * G + G, D:ROW].unsqueeze(3), [P, G, HEADS, HD])
            nc.vector.tensor_tensor(v, v, ex, ALU.mult).then_inc(msg_ready, 1)

        def batch(b, k, r):
            x, kx = b + 1, (k + 1) % RING
            w = windows(mybir.EngineType.DVE, b, 0)
            add_home(b, k, 0, w[0])
            messages(b, k, 1)
            add_home(b, k, 1, w[1])
            if more(b, 1):
                one_hot(x, kx, 2)
            add_home(b, k, 2, w[2])
            if more(b, 1):
                one_hot(x, kx, 3)
            add_home(b, k, 3, w[3])

            w = windows(mybir.EngineType.DVE, b, 1)
            add_home(b, k, 4, w[0])
            messages(b, k, 2)
            add_home(b, k, 5, w[1])
            add_home(b, k, 6, w[2])
            w2 = windows(mybir.EngineType.DVE, b, 2)
            add_home(b, k, 7, w[3])
            if more(b, 1):
                run_maxima(x)

            add_home(b, k, 8, w2[0])
            messages(b, k, 3)
            add_home(b, k, 9, w2[1])
            if more(b, 1):
                dst_scores(x)
            add_home(b, k, 10, w2[2])
            if more(b, 1):
                edge_scores(x)
            add_home(b, k, 11, w2[3])
            if more(b, 1):
                leaky_scores(x, kx)

            w = windows(mybir.EngineType.DVE, b, 3)
            add_home(b, k, 12, w[0])
            if more(b, 1):
                exponents(x)
            add_home(b, k, 13, w[1])
            if more(b, 1):
                messages(x, kx, 0)
            add_home(b, k, 14, w[2])
            if more(b, 2):
                one_hot(b + 2, (k + 2) % RING, 0)
            add_home(b, k, 15, w[3])
            if more(b, 2):
                one_hot(b + 2, (k + 2) % RING, 1)

        for g in range(NG):
            one_hot(0, 0, g)
        one_hot(1, 1, 0)
        one_hot(1, 1, 1)
        dst_scores(0)
        run_maxima(0)
        edge_scores(0)
        leaky_scores(0, 0)
        exponents(0)
        assert c.n == base + LINKS
        messages(0, 0, 0)
        in_rounds(dve, batch)

    @block.tensor
    def _(pe):
        def transpose_scores(x):
            pe.wait_ge(ss_ready, x + 1)
            if past(x):
                pe.wait_ge(arg_ready, x)
            nc.tensor.transpose(psS[:], ss[:].rearrange("p s h -> p (s h)"), ident[:]).then_inc(ssT_done, 1)

        def transpose_hot(x, k, g):
            pe.wait_ge(hot_ready, x * NG + g + 1)
            if past(x) or g >= 2:
                pe.wait_ge(hotT_ready, x * NG + g - 1)
            for s in range(G):
                last = nc.tensor.transpose(psHot[g % 2][:, s, :], hot16[:, k, g, s, :], ident16[:])
            last.then_inc(hotT_done, 1)

        def look_up(x, g):
            w = windows(mybir.EngineType.PE, x, g)
            pe.wait_ge(hotT_ready, x * NG + g + 1)
            if g == 0 and past(x):
                pe.wait_ge(sd_ready, x)
            for s in range(g * G, g * G + G):
                last = nc.tensor.matmul(psD[:, s, :], hotT[:, g % 2, s % G, :],
                                        sParts[:, bass.ds(w[s % G], 1), :, :].rearrange("p a t h -> p (a t h)"), start=True, stop=True)
            last.then_inc(sd_done, 1)

        def transpose_back(x):
            pe.wait_ge(runT_ready, x + 1)
            nc.tensor.transpose(psS[:], runT[:], ident[:]).then_inc(run_done, 1)

        def sum_steps(b, k, first, last):
            if first % G == 0:
                pe.wait_ge(msg_ready, b * NG + first // G + 1)
                pe.wait_ge(home_hot_ready, b * NG + first // G + 1)
            for s in range(first, last):
                n = b * SB + s
                if past(b) or s >= BANKS:
                    pe.wait_ge(home_added, n + 1 - BANKS)
                nc.tensor.matmul(psHome[(k * SB + s) % BANKS][:, 0:HOME], hotHome[:, s // G % 2, s % G, :], rows[k][:, s, 0:HOME],
                                 start=True, stop=True).then_inc(home_done, 1)
                if s == 0:
                    pe.wait_ge(eye_ready, b + 1)
                    if past(b):
                        pe.wait_ge(carry_copied, b)
                nc.tensor.matmul(psCarry[0:SB, 0:AGG], carryEye[:, k, s, :], rows[k][:, s, :],
                                 start=(s == 0), stop=(s == SB - 1)).then_inc(agg_done, 1)

        def batch(b, k, r):
            x, kx = b + 1, (k + 1) % RING
            if not more(b, 1):
                for g in range(NG):
                    sum_steps(b, k, g * G, g * G + G)
                return
            sum_steps(b, k, 0, 2)
            transpose_hot(x, kx, 0)
            transpose_hot(x, kx, 1)
            sum_steps(b, k, 2, 4)
            look_up(x, 0)
            sum_steps(b, k, 4, 6)
            transpose_scores(x)
            transpose_hot(x, kx, 2)
            look_up(x, 1)
            transpose_hot(x, kx, 3)
            sum_steps(b, k, 6, 8)
            look_up(x, 2)
            sum_steps(b, k, 8, 10)
            look_up(x, 3)
            transpose_back(x)
            sum_steps(b, k, 10, 12)
            sum_steps(b, k, 12, 16)

        pe.wait_ge(start, 2)
        for g, members in enumerate(groups):
            pe.wait_ge(dstB_ready, g + 1)
            if g >= 2:
                pe.wait_ge(dT_copied, g - 1)
            for i in range(len(members)):
                last = nc.tensor.transpose(psDT[g % 2][:, i, :], dstB[:, g % 2, i, :, :].rearrange("p s h -> p (s h)"), ident[:])
            last.then_inc(dT_done, 1)
        pe.wait_ge(dT_copied, len(groups))
        transpose_hot(0, 0, 0)
        transpose_hot(0, 0, 1)
        look_up(0, 0)
        transpose_hot(0, 0, 2)
        look_up(0, 1)
        transpose_hot(0, 0, 3)
        look_up(0, 2)
        look_up(0, 3)
        transpose_scores(0)
        transpose_back(0)
        in_rounds(pe, batch)


MC = 4
W = MC * P
CHUNKS = -(-NT // MC)
LASTT = NT - (CHUNKS - 1) * MC
LASTN = N - (CHUNKS - 1) * W


def in_chunks(eng, body):
    full = CHUNKS - 1
    for m in range(2):
        body(m, m % 2, MC, W)
    with eng.Fori(1, full // 2) as i:
        body(i * 2, 0, MC, W)
        body(i * 2 + 1, 1, MC, W)
    body(full, full % 2, LASTT, LASTN)


def in_chunks_ahead(eng, prologue, body):
    full = CHUNKS - 1
    assert CHUNKS % 2 and CHUNKS >= 5
    prologue(0, 0, MC, W)
    body((0, 0, MC, W), (1, 1, MC, W))
    with eng.Fori(0, (full - 2) // 2) as i:
        body((i * 2 + 1, 1, MC, W), (i * 2 + 2, 0, MC, W))
        body((i * 2 + 2, 0, MC, W), (i * 2 + 3, 1, MC, W))
    body((full - 1, (full - 1) % 2, MC, W), (full, full % 2, LASTT, LASTN))
    body((full, full % 2, LASTT, LASTN), None)


def later(m, first):
    return not isinstance(m, int) or m >= first


def merge_attention(nc, a, io, keep, home, target, wts):
    ident, sTab, xnT = keep["ident"], keep["sTab"], keep["xnT"]
    cr = a.sb("carry_rows", [CP, CCH, AGG])
    vself = a.sb("vself", [P, NT, D])
    merged = a.sb("carry_sums", [P, NT, HOME])
    edge = a.sb("carry_edge", [HEADS, STEPS])
    back = a.sb("carry_edge_back", [HEADS, STEPS])
    mT = a.sb("carry_maxT", [HEADS, STEPS])
    fwd = a.sb("carry_fwd", [HEADS, STEPS])
    bwd = a.sb("carry_bwd", [HEADS, STEPS])
    run = a.sb("carry_run", [HEADS, STEPS])
    lastRow = a.sb("lastRow", [1, STEPS])
    one = a.sb("one", [1, 1])
    targetP = a.sb("targetP", [CP, CCH])
    lastP = a.sb("lastP", [CP, CCH])
    startI = a.sb("startI", [CP, NT], I32)
    startF = a.sb("startF", [CP, NT])
    iotaI = a.sb("iotaI", [P, P], I32)
    iota = a.sb("iotaM", [P, P])
    relC = a.sb("relC", [CP, NT, CCH])
    c1 = a.sb("c1", [CP, CCH, HEADS])
    c2 = a.sb("c2", [CP, CCH, HEADS])
    c3 = a.sb("c3", [CP, CCH, HEADS])
    c4 = a.sb("c4", [CP, CCH, HEADS])
    hotC = a.sb("hotC", [CP, 2, MC, CCH, P])
    al = a.sb("alpha", [P, 3, MC, HEADS])
    ex = a.sb("expo", [P, 2, 3, MC, HEADS])
    mx = a.sb("mx", [P, MC, HEADS])
    den = a.sb("den", [P, 3, MC, HEADS])
    attn = a.sb("attn", [P, 2, MC, D])
    part = a.sb("part", [P, 2, MC, D])
    selfp = a.sb("selfp", [P, 2, MC, D])
    attnT = a.sb("attnT", [P, 2, DC, W])
    stats = wts["stats1"]

    psA = a.ps("psA", [P, 512])
    psB = a.ps("psB", [P, 512])
    psC = [a.ps(f"psC{i}", [P, 512]) for i in range(2)]
    psT = [a.ps(f"psAT{i}", [P, 512]) for i in range(2)]
    psO = [a.ps(f"psO{i}", [P, 512]) for i in range(2)]

    loads = a.sem("loads")
    v_in = a.sem("v_in")
    iotas = a.sem("iotas")
    chain = a.sem("chain")
    last_ready = a.sem("last_ready")
    cT_done = a.sem("cT_done")
    target_done = a.sem("target_done")
    cT_ready = a.sem("cT_ready")
    run_ready = a.sem("run_ready")
    back_done = a.sem("back_done")
    carg_ready = a.sem("carg_ready")
    cexp_ready = a.sem("cexp_ready")
    rows_ready = a.sem("rows_ready")
    hot_ready = a.sem("hot_ready")
    sum_done = a.sem("sum_done")
    sum_kept = a.sem("sum_kept")
    arg_ready = a.sem("arg_ready")
    exp_ready = a.sem("exp_ready")
    scales_ready = a.sem("scales_ready")
    self_ready = a.sem("self_ready")
    attn_ready = a.sem("attn_ready")
    aT_done = a.sem("aT_done")
    aT_ready = a.sem("aT_ready")
    proj_done = a.sem("proj_done")
    resid_done = a.sem("resid_done")
    go = a.sem("passed")
    passed = a.sem("dve_passed")

    block = a.ctx.enter_context(nc.Block())

    @block.sync
    def _(sp):
        sp.dma_start(cr[:], io["carries"].rearrange("(c p) n -> p c n", p=CP)).then_inc(loads, 16)
        sp.dma_start(vself[:], io["table"].rearrange("(j p) n -> p j n", p=P)[:, :, 0:D]).then_inc(v_in, 16)

    @block.gpsimd
    def _(pool):
        nc.gpsimd.iota(startI[:], pattern=[[P, NT]], base=0, channel_multiplier=0).then_inc(iotas, 1)
        nc.gpsimd.iota(iotaI[:], pattern=[[1, P]], base=0, channel_multiplier=0).then_inc(iotas, 1)
        pool.wait_ge(v_in, 16)

        def self_part(m, k, tiles, nodes):
            pool.wait_ge(scales_ready, m + 1)
            if later(m, 2):
                pool.wait_ge(attn_ready, m - 1)
            apart(pool, go)
            nc.gpsimd.tensor_tensor(selfp[:, k, 0:tiles, :].rearrange("p j (h c) -> p j h c", h=HEADS),
                                    vself[:, bass.ds(m * MC, tiles), :].rearrange("p j (h c) -> p j h c", h=HEADS),
                                    bcast(ex[:, k, 2, 0:tiles, :].unsqueeze(3), [P, tiles, HEADS, HD]),
                                    ALU.mult).then_inc(self_ready, 1)
        in_chunks(pool, self_part)

    @block.scalar
    def _(act):
        act.wait_ge(cT_done, 1)
        nc.scalar.copy(mT[:], psA[0:HEADS, 0:STEPS]).then_inc(cT_ready, 1)
        act.wait_ge(carg_ready, 1)
        nc.scalar.activation(c3[:], c4[:], ACT.Exp).then_inc(cexp_ready, 1)

        def keep_sum(x, i):
            act.wait_ge(sum_done, x * MC + i + 1)
            apart(act, go)
            nc.scalar.copy(merged[:, bass.ds(x * MC + i, 1), :].rearrange("p a d -> p (a d)"), psC[i % 2][:, 0:HOME]).then_inc(sum_kept, 1)

        def exponents(m, k, tiles, nodes):
            act.wait_ge(arg_ready, m + 1)
            nc.scalar.activation(ex[:, k, :, 0:tiles, :], al[:, :, 0:tiles, :], ACT.Exp).then_inc(exp_ready, 1)

        def evacuate(m, k, tiles, nodes):
            for c in range(DC):
                act.wait_ge(aT_done, m * DC + c + 1)
                nc.scalar.copy(attnT[:, k, c, 0:tiles * P], psT[c][:, 0:tiles * P]).then_inc(aT_ready, 1)

        def first(*x):
            for i in range(MC):
                keep_sum(x[0], i)

        def chunk(this, then):
            exponents(*this)
            if then:
                for i in range(then[2]):
                    keep_sum(then[0], i)
            evacuate(*this)
        in_chunks_ahead(act, first, chunk)

    @block.tensor
    def _(pe):
        pe.wait_ge(last_ready, 2)
        for c in range(CCH):
            nc.tensor.matmul(psB[0:CP, 64 + c:65 + c], target[0:1, c * CP:(c + 1) * CP], one[:], start=True, stop=True)
            last = nc.tensor.matmul(psB[0:CP, 80 + c:81 + c], lastRow[:, c * CP:(c + 1) * CP], one[:], start=True, stop=True)
        last.then_inc(target_done, 1)
        pe.wait_ge(loads, 16)
        for c in range(CCH):
            last = nc.tensor.transpose(psA[0:HEADS, c * CP:(c + 1) * CP], cr[:, c, ROW:ROW + HEADS], ident[0:CP, 0:CP])
        last.then_inc(cT_done, 1)
        pe.wait_ge(run_ready, 1)
        for c in range(CCH):
            last = nc.tensor.transpose(psB[0:CP, c * HEADS:(c + 1) * HEADS], run[:, c * CP:(c + 1) * CP], ident[0:HEADS, 0:HEADS])
        last.then_inc(back_done, 1)
        pe.wait_ge(rows_ready, 2)

        def sum_carries(x, k, tiles, nodes):
            for i in range(tiles):
                pe.wait_ge(hot_ready, x * MC + i + 1)
                if later(x, 1) or i >= 2:
                    pe.wait_ge(sum_kept, x * MC + i - 1)
                for c in range(CCH):
                    last = nc.tensor.matmul(psC[i % 2][:, 0:HOME], hotC[:, k, i, c, :], cr[:, c, 0:HOME], start=(c == 0), stop=(c == CCH - 1))
                last.then_inc(sum_done, 1)

        def project(m, k, tiles, nodes):
            pe.wait_ge(attn_ready, m + 1)
            for c in range(DC):
                if later(m, 1):
                    pe.wait_ge(aT_ready, m * DC + c + 1 - DC)
                for j in range(tiles):
                    last = nc.tensor.transpose(psT[c][:, j * P:(j + 1) * P], attn[:, k, j, c * P:(c + 1) * P], ident[:])
                last.then_inc(aT_done, 1)
            pe.wait_ge(aT_ready, m * DC + DC)
            for o in range(DC):
                if later(m, 1):
                    pe.wait_ge(resid_done, m * DC + o + 1 - DC)
                for c in range(DC):
                    last = nc.tensor.matmul(psO[o][:, 0:tiles * P], wts["wo"][:, c, o * P:(o + 1) * P],
                                            attnT[:, k, c, 0:tiles * P], start=(c == 0), stop=(c == DC - 1))
                last.then_inc(proj_done, 1)

        def chunk(this, then):
            if then:
                sum_carries(*then)
            project(*this)
        in_chunks_ahead(pe, sum_carries, chunk)

    @block.vector
    def _(dve):
        c = Chain(dve, chain)
        nc.vector.memset(one[:], 1.0).then_inc(last_ready, 1)
        c.mark(nc.vector.memset(lastRow[:, STEPS - 1:STEPS], 1.0))
        c.join()
        nc.vector.tensor_tensor(lastRow[:, 0:STEPS - 1], target[0:1, 1:STEPS], target[0:1, 0:STEPS - 1], ALU.not_equal).then_inc(last_ready, 1)
        c.mark(nc.vector.memset(edge[:, 0:1], -BIG))
        c.mark(nc.vector.memset(back[:, 0:1], -BIG))
        c.link(nc.vector.tensor_tensor(fwd[:, 1:STEPS], target[0:HEADS, 1:STEPS], target[0:HEADS, 0:STEPS - 1], ALU.not_equal))
        c.mark(nc.vector.tensor_scalar(edge[:, 1:STEPS], fwd[:, 1:STEPS], -BIG, None, ALU.mult))
        c.mark(nc.vector.tensor_scalar(back[:, STEPS - 1:0:-1], fwd[:, 1:STEPS], -BIG, None, ALU.mult))
        dve.wait_ge(iotas, 2)
        c.mark(nc.vector.tensor_copy(startF[:], startI[:]))
        c.mark(nc.vector.tensor_copy(iota[:], iotaI[:]))
        dve.wait_ge(target_done, 1)
        c.mark(nc.vector.tensor_copy(targetP[:], psB[0:CP, 64:64 + CCH]))
        c.link(nc.vector.tensor_copy(lastP[:], psB[0:CP, 80:80 + CCH]))
        c.link(nc.vector.tensor_tensor(relC[:], bcast(targetP[:].unsqueeze(1), [CP, NT, CCH]),
                                       bcast(startF[:].unsqueeze(2), [CP, NT, CCH]), ALU.subtract))
        dve.wait_ge(cT_ready, 1)
        c.mark(nc.vector.tensor_tensor_scan(fwd[:], edge[:], mT[:], -BIG, ALU.add, ALU.max))
        c.link(nc.vector.tensor_tensor_scan(bwd[:, ::-1], back[:], mT[:, ::-1], -BIG, ALU.add, ALU.max))
        nc.vector.tensor_tensor(run[:], fwd[:], bwd[:], ALU.max).then_inc(run_ready, 1)

        def one_hots(x, k, tiles, nodes):
            if later(x, 2):
                dve.wait_ge(sum_done, x * MC - MC)
            for i in range(tiles):
                nc.vector.tensor_tensor(hotC[:, k, i, :, :], bcast(iota[0:CP, :].unsqueeze(1), [CP, CCH, P]),
                                        bcast(relC[:, bass.ds(x * MC + i, 1), :].rearrange("p a c -> p (a c)").unsqueeze(2), [CP, CCH, P]),
                                        ALU.is_equal).then_inc(hot_ready, 1)

        def carry_factors():
            dve.wait_ge(back_done, 1)
            dve.wait_ge(loads, 16)
            crun = psB[0:CP, 0:CCH * HEADS].rearrange("p (c h) -> p c h", h=HEADS)
            cmax, csd = cr[:, :, ROW:ROW + HEADS], cr[:, :, ROW + HEADS:AGG]
            c.mark(nc.vector.tensor_tensor(c1[:], cmax, csd, ALU.add))
            c.link(nc.vector.tensor_tensor(c2[:], crun, csd, ALU.add))
            c.mark(nc.vector.scalar_tensor_tensor(c3[:], c1[:], NEG_SLOPE, c1[:], ALU.mult, ALU.max))
            c.link(nc.vector.scalar_tensor_tensor(c4[:], c2[:], NEG_SLOPE, c2[:], ALU.mult, ALU.max))
            c.link(nc.vector.tensor_tensor(cmax, crun, bcast(lastP[:].unsqueeze(2), [CP, CCH, HEADS]), ALU.mult))
            nc.vector.tensor_tensor(c4[:], c3[:], c4[:], ALU.subtract).then_inc(carg_ready, 1)
            dve.wait_ge(cexp_ready, 1)
            v = cr[:, :, 0:D].rearrange("p s (h c) -> p s h c", h=HEADS)
            nc.vector.tensor_tensor(v, v, bcast(c3[:].unsqueeze(3), [CP, CCH, HEADS, HD]), ALU.mult).then_inc(rows_ready, 1)
            nc.vector.tensor_tensor(cr[:, :, D:ROW], cr[:, :, D:ROW], c3[:], ALU.mult).then_inc(rows_ready, 1)

        def first(*x):
            one_hots(*x)
            carry_factors()

        def scales(m, k, tiles, nodes):
            c.n = base + m * LINKS
            t = bass.ds(m * MC, tiles)
            A, Ex, M, S = al[:, :, 0:tiles, :], ex[:, k, :, 0:tiles, :], mx[:, 0:tiles, :], den[:, :, 0:tiles, :]
            sd = sTab[:, t, :]
            dve.wait_ge(sum_kept, m * MC + tiles)
            if later(m, 1):
                dve.wait_ge(exp_ready, m)
            for n, rows in enumerate((home, merged)):
                c.mark(nc.vector.tensor_scalar(A[:, n], rows[:, t, D:ROW], 0.5, -BIG, ALU.is_lt, ALU.mult))
            c.mark(nc.vector.tensor_tensor(A[:, 2], sd, sd, ALU.max))
            c.join()
            for n, rows in enumerate((home, merged)):
                c.mark(nc.vector.tensor_tensor(A[:, n], A[:, n], rows[:, t, ROW:HOME], ALU.add))
            c.join()
            c.link(nc.vector.tensor_tensor(A, A, bcast(sd.unsqueeze(1), [P, 3, tiles, HEADS]), ALU.add))
            c.link(nc.vector.scalar_tensor_tensor(A, A, NEG_SLOPE, A, ALU.mult, ALU.max))
            c.link(nc.vector.tensor_tensor(M, A[:, 0], A[:, 1], ALU.max))
            c.link(nc.vector.tensor_tensor(M, M, A[:, 2], ALU.max))
            nc.vector.tensor_tensor(A, A, bcast(M.unsqueeze(1), [P, 3, tiles, HEADS]), ALU.subtract).then_inc(arg_ready, 1)

        def divide(m, k, tiles, nodes):
            c.n = base + m * LINKS + 9
            t = bass.ds(m * MC, tiles)
            Ex, S = ex[:, k, :, 0:tiles, :], den[:, :, 0:tiles, :]
            dve.wait_ge(exp_ready, m + 1)
            for n, rows in enumerate((home, merged)):
                c.mark(nc.vector.tensor_tensor(S[:, n], rows[:, t, D:ROW], Ex[:, n], ALU.mult))
            c.join()
            c.link(nc.vector.tensor_tensor(S[:, 2], S[:, 0], S[:, 1], ALU.add))
            c.link(nc.vector.tensor_tensor(S[:, 2], S[:, 2], Ex[:, 2], ALU.add))
            c.link(nc.vector.reciprocal(S[:, 1], S[:, 2]))
            nc.vector.tensor_tensor(Ex, Ex, bcast(S[:, 1].unsqueeze(1), [P, 3, tiles, HEADS]), ALU.mult).then_inc(scales_ready, 1)
            dve.wait_ge(scales_ready, m + 1)

        def combine(m, k, tiles, nodes):
            c.n = base + m * LINKS + 14
            t = bass.ds(m * MC, tiles)
            heads = lambda v: v.rearrange("p j (h c) -> p j h c", h=HEADS)
            out, other = attn[:, k, 0:tiles, :], part[:, k, 0:tiles, :]
            c.mark(nc.vector.tensor_tensor(heads(out), heads(home[:, t, 0:D]), bcast(ex[:, k, 0, 0:tiles, :].unsqueeze(3), [P, tiles, HEADS, HD]), ALU.mult))
            c.link(nc.vector.tensor_tensor(heads(other), heads(merged[:, t, 0:D]), bcast(ex[:, k, 1, 0:tiles, :].unsqueeze(3), [P, tiles, HEADS, HD]), ALU.mult))
            c.link(nc.vector.tensor_tensor(out, out, other, ALU.add))
            dve.wait_ge(self_ready, m + 1)
            nc.vector.tensor_tensor(out, out, selfp[:, k, 0:tiles, :], ALU.add).then_inc(attn_ready, 1)

        def residual(m, tiles):
            for o in range(DC):
                dve.wait_ge(proj_done, m * DC + o + 1)
                h = xnT[:, o, bass.ds(m * W, tiles * P)]
                nc.vector.scalar_tensor_tensor(h, psO[o][:, 0:tiles * P], wts["bo"][:, o:o + 1], h, ALU.add, ALU.add).then_inc(resid_done, 1)

        def bn_stats(m, nodes):
            for o in range(DC):
                dve.wait_ge(resid_done, m * DC + o + 1)
                apart(dve, passed)
                nc.vector.bn_stats(stats[:, o, bass.ds(m, 1), :].rearrange("p a s -> p (a s)"), xnT[:, o, bass.ds(m * W, nodes)])

        def chunk(this, then):
            m, k, tiles, nodes = this
            if then:
                one_hots(*then)
            scales(*this)
            if later(m, 1):
                residual(m - 1, MC)
            divide(*this)
            combine(*this)
            if later(m, 1):
                bn_stats(m - 1, W)
            if not then:
                residual(m, tiles)
                bn_stats(m, nodes)

        LINKS = 17
        base = c.n + 5
        in_chunks_ahead(dve, first, chunk)


def batch_norm_scale(nc, c, dve, act_sems, stats, norm, gain, shift):
    var_ready, std_ready = act_sems
    for o in range(DC):
        c.mark(nc.vector.bn_aggr(norm["mv"][:, o, :], stats[:, o, :, :]))
    c.join()
    nc.vector.tensor_scalar(norm["var"][:], norm["mv"][:, :, 1], EPS, None, ALU.add).then_inc(var_ready, 1)
    dve.wait_ge(std_ready, 1)
    c.link(nc.vector.reciprocal(norm["var"][:], norm["std"][:]))
    c.link(nc.vector.tensor_tensor(norm["scale"][:], norm["var"][:], gain, ALU.mult))
    c.link(nc.vector.tensor_tensor(norm["var"][:], norm["mv"][:, :, 0], norm["scale"][:], ALU.mult))
    c.link(nc.vector.tensor_tensor(norm["shift"][:], shift, norm["var"][:], ALU.subtract))


def feed_forward(nc, a, io, keep, wts):
    xnT = keep["xnT"]
    hidden = a.sb("hidden", [P, 2, FC, W])
    norm = {n: a.sb(f"norm_{n}", [P, DC]) for n in ("var", "std", "scale", "shift")}
    norm["mv"] = a.sb("norm_mv", [P, DC, 2])
    psF = [a.ps(f"psF{i}", [P, 512]) for i in range(4)]
    psY = [a.ps(f"psY{i}", [P, 512]) for i in range(4)]
    chain = a.sem("chain")
    var_ready = a.sem("var_ready")
    std_ready = a.sem("std_ready")
    h_ready = a.sem("h_ready")
    ff_done = a.sem("ff_done")
    relu_done = a.sem("relu_done")
    y_done = a.sem("y_done")
    y_added = a.sem("y_added")
    passed = a.sem("passed")
    loads = a.sem("expert_loads")
    tail_zero = a.sem("tail_zero")
    block = a.ctx.enter_context(nc.Block())

    @block.sync
    def _(sp):
        sp.dma_start(wts["xN"][:, 0:NT - 1, :], io["x"][0:(NT - 1) * P, :].rearrange("(j p) d -> p j d", p=P)).then_inc(loads, 16)
        for name, key in (("expert_w1", "ew1"), ("expert_w2", "ew2"), ("expert_w3", "ew3")):
            sp.dma_start(wts[key][:], io[name].rearrange("e (c p) n -> p e c n", p=P)).then_inc(loads, 16)
        sp.wait_ge(tail_zero, 1)
        sp.dma_start(wts["xN"][0:NTAIL, NT - 1, :], io["x"][(NT - 1) * P:N, :]).then_inc(loads, 16)
        sp.wait_ge(loads, 80)

    @block.gpsimd
    def _(pool):
        nc.gpsimd.memset(wts["xN"][:, NT - 1, :], 0.0).then_inc(tail_zero, 1)

    @block.scalar
    def _(act):
        act.wait_ge(var_ready, 1)
        nc.scalar.activation(norm["std"][:], norm["var"][:], ACT.Sqrt).then_inc(std_ready, 1)

        def relu(m, k, tiles, nodes):
            for f in range(FC):
                act.wait_ge(ff_done, m * FC + f + 1)
                if later(m, 2) and f == 0:
                    act.wait_ge(y_done, m * DC - DC)
                nc.scalar.activation(hidden[:, k, f, 0:nodes], psF[f][:, 0:nodes], ACT.Relu,
                                     bias=wts["b1"][:, f:f + 1]).then_inc(relu_done, 1)
        in_chunks(act, relu)

    @block.tensor
    def _(pe):
        def up(m, k, tiles, nodes):
            pe.wait_ge(h_ready, m + 1)
            for f in range(FC):
                if later(m, 1):
                    pe.wait_ge(relu_done, m * FC + f + 1 - FC)
                for c in range(DC):
                    last = nc.tensor.matmul(psF[f][:, 0:nodes], wts["w1"][:, c, f * P:(f + 1) * P],
                                            xnT[:, c, bass.ds(m * W, nodes)], start=(c == 0), stop=(c == DC - 1))
                last.then_inc(ff_done, 1)

        def down(m, k, tiles, nodes):
            for o in range(DC):
                if later(m, 2):
                    pe.wait_ge(y_added, m * DC + o + 1 - 2 * DC)
                for f in range(FC):
                    if o == 0:
                        pe.wait_ge(relu_done, m * FC + f + 1)
                    last = nc.tensor.matmul(psY[2 * k + o][:, 0:nodes], wts["w2"][:, f, o * P:(o + 1) * P],
                                            hidden[:, k, f, 0:nodes], start=(f == 0), stop=(f == FC - 1))
                last.then_inc(y_done, 1)

        def chunk(m, k, tiles, nodes):
            up(m, k, tiles, nodes)
            down(m, k, tiles, nodes)
        in_chunks(pe, chunk)

    @block.vector
    def _(dve):
        c = Chain(dve, chain)
        batch_norm_scale(nc, c, dve, (var_ready, std_ready), wts["stats1"], norm, wts["g1"][:], wts["c1"][:])

        def normalize(m, k, tiles, nodes):
            for o in range(DC):
                h = xnT[:, o, bass.ds(m * W, nodes)]
                last = nc.vector.tensor_scalar(h, h, norm["scale"][:, o:o + 1], norm["shift"][:, o:o + 1], ALU.mult, ALU.add)
            last.then_inc(h_ready, 1)
        in_chunks(dve, normalize)

        def add(m, k, tiles, nodes):
            for o in range(DC):
                dve.wait_ge(y_done, m * DC + o + 1)
                h = xnT[:, o, bass.ds(m * W, nodes)]
                nc.vector.scalar_tensor_tensor(h, psY[2 * k + o][:, 0:nodes], wts["b2"][:, o:o + 1], h, ALU.add, ALU.add).then_inc(y_added, 1)
                dve.wait_ge(y_added, m * DC + o + 1)
                apart(dve, passed)
                last = nc.vector.bn_stats(wts["stats2"][:, o, bass.ds(m, 1), :].rearrange("p a s -> p (a s)"), h)
        in_chunks(dve, add)


def route_and_mix(nc, a, io, keep, wts):
    xN, xnT, ident = wts["xN"], keep["xnT"], keep["ident"]
    norm = {n: a.sb(f"norm2_{n}", [P, DC]) for n in ("var", "std", "scale", "shift")}
    norm["mv"] = a.sb("norm2_mv", [P, DC, 2])
    y = a.sb("y", [P, 2, DC, W])
    st = a.sb("ln_stats", [P, 2, MC, 6])
    mv = a.sb("ln_mv", [P, 2, MC, 2])
    va = a.sb("ln_var", [P, 2, MC])
    sdv = a.sb("ln_std", [P, 2, MC])
    rs = a.sb("ln_rstd", [P, 2, MC])
    x2 = a.sb("x2", [P, 2, MC, D])
    x2T = a.sb("x2T", [P, 2, DC, W])
    rh = a.sb("rh", [P, 2, W])
    lg = a.sb("lg", [P, MC, 8])
    le = a.sb("le", [P, MC, 8])
    pr = a.sb("pr", [P, MC, 8])
    red = a.sb("red", [P, MC])
    top = a.sb("top", [P, MC, 8])
    topi = a.sb("topi", [P, MC, 8], mybir.dt.uint32)
    topf = a.sb("topf", [P, MC, 8])
    dw = a.sb("dw", [P, MC])
    ew = a.sb("ew", [P, MC])
    w0 = a.sb("w0", [P, MC])
    w1 = a.sb("w1_", [P, MC])
    hit = a.sb("hit", [P, MC, NEXP])
    gate = a.sb("gate", [P, 2, MC, NEXP])
    iotaI = a.sb("iotaE", [P, NEXP], I32)
    iotaF = a.sb("iotaEf", [P, NEXP])
    h1 = a.sb("h1", [P, 2, DC, W])
    h2 = a.sb("h2", [P, 2, DC, W])

    psT = [a.ps(f"psX{i}", [P, 512]) for i in range(2)]
    psR = a.ps("psR", [P, 512])
    psL = a.ps("psL", [P, 512])
    psH = [a.ps(f"psH{i}", [P, 512]) for i in range(2)]
    psE = [a.ps(f"psE{i}", [P, 512]) for i in range(2)]

    chain = a.sem("chain")
    var_ready = a.sem("var_ready")
    std_ready = a.sem("std_ready")
    iotas = a.sem("iotas")
    y_ready = a.sem("y_ready")
    yT_done = a.sem("yT_done")
    lnvar_ready = a.sem("lnvar_ready")
    lnstd_ready = a.sem("lnstd_ready")
    x2_ready = a.sem("x2_ready")
    x2T_done = a.sem("x2T_done")
    x2T_ready = a.sem("x2T_ready")
    r_done = a.sem("router_done")
    r_relu = a.sem("router_relu")
    l_done = a.sem("logits_done")
    larg_ready = a.sem("larg_ready")
    lexp_ready = a.sem("lexp_ready")
    warg_ready = a.sem("warg_ready")
    wexp_ready = a.sem("wexp_ready")
    gate_ready = a.sem("gate_ready")
    hid_done = a.sem("hid_done")
    hid_relu = a.sem("hid_relu")
    e_done = a.sem("e_done")
    e_added = a.sem("e_added")
    bias_added = a.sem("bias_added")
    out_done = a.sem("out_done")
    passed = a.sem("passed")
    block = a.ctx.enter_context(nc.Block())
    HALVES = MC // 2

    def halves(tiles):
        return -(-tiles // 2)

    @block.sync
    def _(sp):
        def store(m, k, tiles, nodes):
            if tiles == MC:
                sp.wait_ge(e_added, (m + 1) * NEXP * HALVES)
                sp.dma_start(io["out"][bass.ds(m * W, W), :].rearrange("(j p) d -> p j d", p=P), xN[:, bass.ds(m * MC, MC), :]).then_inc(out_done, 16)
            else:
                sp.wait_ge(e_added, (CHUNKS - 1) * NEXP * HALVES + NEXP * halves(tiles))
                sp.dma_start(io["out"][m * W:N, :], xN[0:nodes, m * MC, :]).then_inc(out_done, 16)
        in_chunks(sp, store)
        sp.wait_ge(out_done, 16 * CHUNKS)

    @block.gpsimd
    def _(pool):
        nc.gpsimd.iota(iotaI[:], pattern=[[1, NEXP]], base=0, channel_multiplier=0).then_inc(iotas, 1)


    @block.scalar
    def _(act):
        act.wait_ge(var_ready, 1)
        nc.scalar.activation(norm["std"][:], norm["var"][:], ACT.Sqrt).then_inc(std_ready, 1)

        def ln_std(x, k, tiles, nodes):
            act.wait_ge(lnvar_ready, x + 1)
            nc.scalar.activation(sdv[:, k, 0:tiles], va[:, k, 0:tiles], ACT.Sqrt).then_inc(lnstd_ready, 1)

        def copy_x2T(x, k, tiles, nodes):
            for c in range(DC):
                act.wait_ge(x2T_done, x * DC + c + 1)
                if later(x, 2) and c == 0:
                    act.wait_ge(hid_done, (x - 1) * (NEXP * 2 * DC))
                nc.scalar.copy(x2T[:, k, c, 0:tiles * P], psT[c][:, 0:tiles * P]).then_inc(x2T_ready, 1)

        def router_relu(x, k, tiles, nodes):
            act.wait_ge(r_done, x + 1)
            nc.scalar.activation(rh[:, k, 0:tiles * P], psR[:, 0:tiles * P], ACT.Relu, bias=wts["rb1"][:, 0:1]).then_inc(r_relu, 1)

        def logit_exp(x, k, tiles, nodes):
            act.wait_ge(larg_ready, x + 1)
            nc.scalar.activation(le[:, 0:tiles, 0:NEXP], lg[:, 0:tiles, 0:NEXP], ACT.Exp).then_inc(lexp_ready, 1)

        def weight_exp(x, k, tiles, nodes):
            act.wait_ge(warg_ready, x + 1)
            nc.scalar.activation(ew[:, 0:tiles], dw[:, 0:tiles], ACT.Exp).then_inc(wexp_ready, 1)

        def hidden(m, e, layer, tiles):
            h, b = ((h1, "eb1"), (h2, "eb2"))[layer]
            for o in range(DC):
                act.wait_ge(hid_done, ((m * NEXP + e) * 2 + layer) * DC + o + 1)
                if layer == 1 and o == 0 and (later(m, 1) or e >= 2):
                    act.wait_ge(e_done, m * NEXP * HALVES + (e - 1) * halves(tiles) if e >= 2 else m * NEXP * HALVES - (1 - e) * HALVES)
                nc.scalar.activation(h[:, e % 2, o, 0:tiles * P], psH[o][:, 0:tiles * P], ACT.Relu,
                                     bias=wts[b][:, e, o:o + 1]).then_inc(hid_relu, 1)

        pieces = {(1, 0): ln_std, (1, 1): copy_x2T, (2, 0): router_relu, (2, 1): logit_exp, (3, 0): weight_exp}

        def chunk(this, then):
            m, k, tiles, nodes = this
            for e in range(NEXP):
                for layer in range(2):
                    hidden(m, e, layer, tiles)
                    if then and (e, layer) in pieces:
                        pieces[e, layer](*then)

        def prologue(*x):
            for piece in pieces.values():
                piece(*x)
        in_chunks_ahead(act, prologue, chunk)

    @block.tensor
    def _(pe):
        def transpose_y(x, k, tiles, nodes):
            pe.wait_ge(y_ready, x + 1)
            for b in range(halves(tiles)):
                if later(x, 1):
                    pe.wait_ge(x2T_ready, x * DC)
                for j in range(2 * b, min(2 * b + 2, tiles)):
                    for c in range(DC):
                        last = nc.tensor.transpose(psT[b][:, (j % 2) * D + c * P:(j % 2) * D + (c + 1) * P], y[:, k, c, j * P:(j + 1) * P], ident[:])
            last.then_inc(yT_done, 1)

        def transpose_x2(x, k, tiles, nodes):
            pe.wait_ge(x2_ready, x + 1)
            for c in range(DC):
                for j in range(tiles):
                    last = nc.tensor.transpose(psT[c][:, j * P:(j + 1) * P], x2[:, k, j, c * P:(c + 1) * P], ident[:])
                last.then_inc(x2T_done, 1)

        def router(x, k, tiles, nodes):
            pe.wait_ge(x2T_ready, x * DC + DC)
            if later(x, 1):
                pe.wait_ge(r_relu, x)
            for c in range(DC):
                last = nc.tensor.matmul(psR[:, 0:tiles * P], wts["rw1"][:, c, :], x2T[:, k, c, 0:tiles * P], start=(c == 0), stop=(c == DC - 1))
            last.then_inc(r_done, 1)

        def logits(x, k, tiles, nodes):
            pe.wait_ge(r_relu, x + 1)
            if later(x, 1):
                pe.wait_ge(larg_ready, x)
            for j in range(tiles):
                last = nc.tensor.matmul(psL[:, j * 8:j * 8 + NEXP], rh[:, k, j * P:(j + 1) * P], wts["rw2"][:], start=True, stop=True)
            last.then_inc(l_done, 1)

        def node_rows(m, group, tiles, lhs, rhs_list):
            for b in range(halves(tiles)):
                prior = m * NEXP * HALVES + group * halves(tiles) + b
                if later(m, 1) or group * halves(tiles) + b >= 2:
                    pe.wait_ge(e_added, prior - 1 if halves(tiles) == HALVES else prior)
                for j in range(2 * b, min(2 * b + 2, tiles)):
                    for i, r in enumerate(rhs_list):
                        last = nc.tensor.matmul(psE[b][:, (j % 2) * D:(j % 2 + 1) * D], lhs(i, j), r, start=(i == 0), stop=(i == len(rhs_list) - 1))
                last.then_inc(e_done, 1)

        def hidden(m, k, e, layer, n):
            src, w = ((x2T[:, k], "ew1"), (h1[:, e % 2], "ew2"))[layer]
            for o in range(DC):
                idx = ((m * NEXP + e) * 2 + layer) * DC + o
                if later(m, 1) or idx >= DC:
                    pe.wait_ge(hid_relu, idx + 1 - DC if not (layer == 1 and o == 0) else idx)
                for c in range(DC):
                    last = nc.tensor.matmul(psH[o][:, 0:n], wts[w][:, e, c, o * P:(o + 1) * P], src[:, c, 0:n], start=(c == 0), stop=(c == DC - 1))
                last.then_inc(hid_done, 1)

        def chunk(this, then):
            m, k, tiles, nodes = this
            n = tiles * P

            def out(m, e, tiles):
                pe.wait_ge(hid_relu, ((m * NEXP + e) * 2 + 2) * DC)
                node_rows(m, e, tiles, lambda i, j: h2[:, e % 2, i, j * P:(j + 1) * P], [wts["ew3"][:, e, c, :] for c in range(DC)])

            hidden(m, k, 0, 0, n)
            if later(m, 1):
                out(m - 1, NEXP - 1, MC)
            hidden(m, k, 0, 1, n)
            if then:
                transpose_y(*then)
            for e in range(1, NEXP):
                hidden(m, k, e, 0, n)
                if then and e == 2:
                    router(*then)
                out(m, e - 1, tiles)
                if then and e == 2:
                    logits(*then)
                hidden(m, k, e, 1, n)
                if then and e == 1:
                    transpose_x2(*then)
            if not then:
                out(m, NEXP - 1, tiles)

        def prologue(*x):
            for piece in (transpose_y, transpose_x2, router, logits):
                piece(*x)
        in_chunks_ahead(pe, prologue, chunk)

    @block.vector
    def _(dve):
        c = Chain(dve, chain)
        batch_norm_scale(nc, c, dve, (var_ready, std_ready), wts["stats2"], norm, wts["g2"][:], wts["c2"][:])
        c.mark(nc.vector.memset(pr[:], -1.0))
        dve.wait_ge(iotas, 1)
        c.link(nc.vector.tensor_copy(iotaF[:], iotaI[:]))
        base = c.n
        NORM_LINKS = HALVES + 2 * MC + 1
        GATE_LINKS = 9 + 4 * MC
        LINKS = NORM_LINKS + GATE_LINKS

        def add_y(x, k, tiles, nodes):
            if later(x, 2):
                dve.wait_ge(yT_done, x - 1)
            for o in range(DC):
                last = nc.vector.tensor_scalar(y[:, k, o, 0:tiles * P], xnT[:, o, bass.ds(x * W, tiles * P)], norm["scale"][:, o:o + 1],
                                               norm["shift"][:, o:o + 1], ALU.mult, ALU.add)
            last.then_inc(y_ready, 1)

        def layer_norm(x, k, tiles, nodes):
            c.n = base + x * LINKS
            dve.wait_ge(yT_done, x + 1)
            for b in range(halves(tiles)):
                w = min(2, tiles - 2 * b)
                v = xN[:, bass.ds(x * MC + 2 * b, w), :].rearrange("p j d -> p (j d)")
                c.mark(nc.vector.tensor_tensor(v, v, psT[b][:, 0:w * D], ALU.add))
            c.join()
            apart(dve, passed)
            for j in range(tiles):
                c.mark(nc.vector.bn_stats(st[:, k, j, :], xN[:, bass.ds(x * MC + j, 1), :].rearrange("p a d -> p (a d)")))
            c.join()
            apart(dve, passed)
            for j in range(tiles):
                c.mark(nc.vector.bn_aggr(mv[:, k, j, :], st[:, k, j, :]))
            c.join()
            nc.vector.tensor_scalar(va[:, k, 0:tiles], mv[:, k, 0:tiles, 1], EPS, None, ALU.add).then_inc(lnvar_ready, 1)
            dve.wait_ge(lnstd_ready, x + 1)
            c.link(nc.vector.reciprocal(rs[:, k, 0:tiles], sdv[:, k, 0:tiles]))
            if later(x, 2):
                dve.wait_ge(x2T_done, x * DC - DC)
            for j in range(tiles):
                last = nc.vector.tensor_scalar(x2[:, k, j, :], xN[:, bass.ds(x * MC + j, 1), :].rearrange("p a d -> p (a d)"), mv[:, k, j, 0:1],
                                               rs[:, k, j:j + 1], ALU.subtract, ALU.mult)
            last.then_inc(x2_ready, 1)
            assert tiles < MC or not isinstance(x, int) or c.n == base + x * LINKS + NORM_LINKS

        def softmax(x, k, tiles, nodes):
            c.n = base + x * LINKS + (NORM_LINKS if tiles == MC else halves(tiles) + 2 * tiles + 1)
            dve.wait_ge(l_done, x + 1)
            L = lg[:, 0:tiles, 0:NEXP]
            r3 = bcast(red[:, 0:tiles].unsqueeze(2), [P, tiles, NEXP])
            c.link(nc.vector.tensor_tensor(L, psL[:, 0:tiles * 8].rearrange("p (j e) -> p j e", e=8)[:, :, 0:NEXP], bcast(wts["rb2"][:].unsqueeze(1), [P, tiles, NEXP]), ALU.add))
            c.link(nc.vector.tensor_reduce(red[:, 0:tiles], L, X, ALU.max))
            nc.vector.tensor_tensor(L, L, r3, ALU.subtract).then_inc(larg_ready, 1)
            dve.wait_ge(lexp_ready, x + 1)
            c.link(nc.vector.tensor_reduce(red[:, 0:tiles], le[:, 0:tiles, 0:NEXP], X, ALU.add))
            c.link(nc.vector.reciprocal(red[:, 0:tiles], red[:, 0:tiles]))
            c.link(nc.vector.tensor_tensor(pr[:, 0:tiles, 0:NEXP], le[:, 0:tiles, 0:NEXP], r3, ALU.mult))
            apart(dve, passed)
            for j in range(tiles):
                c.mark(nc.vector.max(top[:, j, :], pr[:, j, :]))
            c.join()
            apart(dve, passed)
            for j in range(tiles):
                c.mark(nc.vector.max_index(topi[:, j, :], top[:, j, :], pr[:, j, :]))
            c.join()
            nc.vector.tensor_tensor(dw[:, 0:tiles], top[:, 0:tiles, 1], top[:, 0:tiles, 0], ALU.subtract).then_inc(warg_ready, 1)
            c.mark(nc.vector.tensor_copy(topf[:, 0:tiles, 0:2], topi[:, 0:tiles, 0:2]))
            dve.wait_ge(wexp_ready, x + 1)
            c.link(nc.vector.tensor_scalar(w1[:, 0:tiles], ew[:, 0:tiles], 1.0, None, ALU.add))
            c.link(nc.vector.reciprocal(w0[:, 0:tiles], w1[:, 0:tiles]))
            for j in range(tiles):
                c.mark(nc.vector.tensor_scalar(gate[:, k, j, :], iotaF[:], topf[:, j, 0:1], w0[:, j:j + 1], ALU.is_equal, ALU.mult))
            c.join()
            c.link(nc.vector.tensor_tensor(w1[:, 0:tiles], ew[:, 0:tiles], w0[:, 0:tiles], ALU.mult))
            for j in range(tiles):
                c.mark(nc.vector.tensor_scalar(hit[:, j, :], iotaF[:], topf[:, j, 1:2], w1[:, j:j + 1], ALU.is_equal, ALU.mult))
            c.join()
            nc.vector.tensor_tensor(gate[:, k, 0:tiles, :], gate[:, k, 0:tiles, :], hit[:, 0:tiles, :], ALU.add).then_inc(gate_ready, 1)
            assert tiles < MC or not isinstance(x, int) or c.n == base + x * LINKS + LINKS, c.n

        def add_bias(m, k, tiles, e):
            if e:
                dve.wait_ge(e_added, m * NEXP * HALVES + e * halves(tiles))
                apart(dve, passed)
            for j in range(tiles):
                x = xN[:, bass.ds(m * MC + j, 1), :].rearrange("p a d -> p (a d)")
                last = nc.vector.scalar_tensor_tensor(x, wts["eb3"][:, e, :], gate[:, k, j, e:e + 1], x, ALU.mult, ALU.add)
            last.then_inc(bias_added, 1)

        def add_group(m, k, tiles, group):
            for b in range(halves(tiles)):
                seq = m * NEXP * HALVES + group * halves(tiles) + b
                dve.wait_ge(e_done, seq + 1)
                dve.wait_ge(bias_added, m * NEXP + group + 1)
                for j in range(2 * b, min(2 * b + 2, tiles)):
                    x = xN[:, bass.ds(m * MC + j, 1), :].rearrange("p a d -> p (a d)")
                    last = nc.vector.scalar_tensor_tensor(x, psE[b][:, (j % 2) * D:(j % 2 + 1) * D], gate[:, k, j, group:group + 1], x, ALU.mult, ALU.add)
                last.then_inc(e_added, 1)

        def chunk(this, then):
            m, k, tiles, nodes = this
            if then:
                add_y(*then)
            dve.wait_ge(gate_ready, m + 1)
            add_bias(m, k, tiles, 0)
            if then:
                layer_norm(*then)
            for e in range(NEXP):
                add_group(m, k, tiles, e)
                if e + 1 < NEXP:
                    add_bias(m, k, tiles, e + 1)
                if then and e == 1:
                    softmax(*then)

        def prologue(*x):
            for piece in (add_y, layer_norm, softmax):
                piece(*x)
        in_chunks_ahead(dve, prologue, chunk)


def build(nc, io):
    with ExitStack() as ctx:
        a = Alloc(nc, ctx, "all")
        io["table"] = nc.dram_tensor("node_table", [NT * P, ROW], F32, kind="Internal").ap()
        io["carries"] = nc.dram_tensor("carries", [STEPS, AGG], F32, kind="Internal").ap()
        keep = dict(xnT=a.sb("xnT", [P, DC, NT * P]), sTab=a.sb("sTab", [P, NT + 1, HEADS]), ident=a.sb("ident", [P, P]))
        wts = dict(wo=a.sb("wo", [P, DC, D]), w1=a.sb("w1", [P, DC, FF]), w2=a.sb("w2", [P, FC, D]),
                   rw1=a.sb("rw1", [P, DC, RH]), rw2=a.sb("rw2", [RH, NEXP]), rb1=a.sb("rb1", [RH, 1]),
                   rb2=a.sb("rb2", [P, NEXP]), eb1=a.sb("eb1", [P, NEXP, DC]), eb2=a.sb("eb2", [P, NEXP, DC]),
                   eb3=a.sb("eb3", [P, NEXP, D]), b1=a.sb("b1", [P, FC]),
                   stats1=a.sb("stats1", [P, DC, CHUNKS, 6]), stats2=a.sb("stats2", [P, DC, CHUNKS, 6]),
                   **{n: a.sb(n, [P, DC]) for n in ("bo", "b2", "g1", "c1", "g2", "c2")})
        with ExitStack() as edges:
            b = Alloc(nc, edges, "edges")
            home = b.sb("home", [P, NT + 1, HOME])
            target = b.sb("target", [P, STEPS])
            with ExitStack() as steps:
                b = Alloc(nc, steps, "plan")
                plan = dict(srcI=b.sb("step_srcI", [P, STEPS], I32), windowI=b.sb("windowI", [1, STEPS], I32),
                            rel16=b.sb("rel16", [P, STEPS], BF16), notCarry=b.sb("notCarry", [P, STEPS]), dst=b.sb("dst_of_step", [P, STEPS]),
                            isLast=b.sb("isLast", [P, STEPS]), isCarry=b.sb("isCarry", [P, STEPS]), target=target,
                            edge=b.sb("edge", [P, BATCHES, P]), edgeBack=b.sb("edgeBack", [P, BATCHES, P]),
                            iota16=b.sb("iota16", [P, P], BF16))
                with ExitStack() as first:
                    b = Alloc(nc, first, "nodes")
                    nodes = dict(xN=b.sb("x_rows", [P, NT, D]), wqkv=b.sb("wqkv", [P, DC, 3 * D]), bias=b.sb("qkv_bias", [P, 3 * D]),
                                 meanvar=b.sb("meanvar", [P, NT, 2]), rstd=b.sb("rstd", [P, NT]))
                    with ExitStack() as phase:
                        plan_steps(nc, Alloc(nc, phase, "planning"), io, keep, plan, nodes, home)
                    with ExitStack() as phase:
                        project_nodes(nc, Alloc(nc, phase, "project"), io, keep, nodes)
                with ExitStack() as phase:
                    run_steps(nc, Alloc(nc, phase, "steps"), io, keep, plan, home, wts)
            with ExitStack() as phase:
                merge_attention(nc, Alloc(nc, phase, "merge"), io, keep, home, target, wts)
        with ExitStack() as dense:
            b = Alloc(nc, dense, "dense")
            wts |= {n: b.sb(n, [P, NEXP, DC, D]) for n in ("ew1", "ew2", "ew3")} | {"xN": b.sb("xN", [P, NT, D])}
            with ExitStack() as phase:
                feed_forward(nc, Alloc(nc, phase, "ffn"), io, keep, wts)
            with ExitStack() as phase:
                route_and_mix(nc, Alloc(nc, phase, "experts"), io, keep, wts)


_GNN = ["Wq", "bq", "Wk", "bk", "Wv", "bv", "Wo", "bo", "W1", "b1", "W2", "b2", "bn1_g", "bn1_b", "bn2_g", "bn2_b"]
_FFN = ["router_w1", "router_b1", "router_w2", "router_b2", "expert_w1", "expert_b1", "expert_w2", "expert_b2",
        "expert_w3", "expert_b3"]
_INS = {"x": "x", "src": "src", "dst": "dst"} | {f"L0_gnn_{n}": n for n in _GNN} | {f"L0_ffn_{n}": n for n in _FFN}


def kernel(**inputs):
    import numpy as _np
    import concourse.bacc as _bacc
    from concourse import mybir as _mybir
    from concourse.bass_utils import run_bass_kernel_spmd as _run

    nc = _bacc.Bacc("TRN2", target_bir_lowering=False, num_devices=1)
    arrays, io = {}, {}
    for name, short in _INS.items():
        a = _np.ascontiguousarray(inputs[name])
        arrays[f"in_{name}_dram"] = a
        io[short] = nc.dram_tensor(f"in_{name}_dram", a.shape, _mybir.dt.from_np(a.dtype), kind="ExternalInput").ap()
    io["out"] = nc.dram_tensor("out_0_dram", (N, D), _mybir.dt.float32, kind="ExternalOutput").ap()
    build(nc, io)
    r = _run(nc, [arrays], core_ids=[0])
    return r.results[0]["out_0_dram"]
```
